# Optimizing a Trainium2 kernel written in Bass

```python
import numpy as np
import jax
import jax.numpy as jnp

def _softmax(x, axis=-1):
    return jax.nn.softmax(x, axis=axis)

def _gelu(x):
    return jax.nn.gelu(x, approximate=True)

def _silu(x):
    return jax.nn.silu(x)

def _sigmoid(x):
    return jax.nn.sigmoid(x)

def _layernorm(x, axis=-1, eps=1e-05):
    m = jnp.mean(x, axis=axis, keepdims=True)
    v = jnp.var(x, axis=axis, keepdims=True)
    return (x - m) / jnp.sqrt(v + eps)

def _scatter_add(tgt, idx, src, axis=0):
    return tgt.at[idx].add(src)

def _segment_sum(src, seg, n):
    return jax.ops.segment_sum(src, seg, n)
kernel_name = 'mk_perceiver_d1_seqx_r8_899481'

def setup_inputs(seed: int=0):
    np.random.seed(seed)
    _w = jnp.asarray

    def _rec_inputs():
        import jax
        import jax.numpy as jnp
        _rk = jax.random.key(seed)
        x = -0.0002928 + 1 * jax.random.normal(jax.random.fold_in(_rk, 1), (128, 32, 256), jnp.float32)
        _lenS = 32 - jax.random.randint(jax.random.fold_in(_rk, 7), (128,), 0, max(1, 32 // 4) + 1, jnp.int32)
        _lenS2 = 257 - jax.random.randint(jax.random.fold_in(_rk, 8), (128,), 0, max(1, 257 // 4) + 1, jnp.int32)
        _ctx_2048P = jax.random.normal(jax.random.fold_in(_rk, 11), (128, 16, 256), jnp.float32)
        _ctx_2048c = jax.random.dirichlet(jax.random.fold_in(_rk, 511), 0.3 * jnp.ones((16,), jnp.float32), (128, 257))
        _ctx_2048t = jnp.einsum('bsk,bkd->bsd', _ctx_2048c, _ctx_2048P)
        _ctx_2048t = _ctx_2048t * jax.lax.rsqrt(jnp.mean(jnp.square(_ctx_2048t)) + 1e-12) * 0.953939
        ctx_2048 = 4.13588e-05 + 0.999923 * (_ctx_2048t + 0.3 * jax.random.normal(jax.random.fold_in(_rk, 611), (128, 257, 256), jnp.float32))
        _validS = jnp.arange(32)[None, :] < _lenS[:, None]
        _validS2 = jnp.arange(257)[None, :] < _lenS2[:, None]
        _causal = jnp.tril(jnp.ones((32, 32), dtype=bool))
        mask_1xSxS2_ff0 = jnp.where(jnp.ones((1, 32, 257), dtype=bool), 0.0, -1000000000.0).astype(jnp.float32)
        return (x, ctx_2048, mask_1xSxS2_ff0)
    x, ctx_2048, mask_1xSxS2_ff0 = _rec_inputs()

    def _L0_xattn_setup():
        import jax, jax.numpy as jnp
        import numpy as np
        H = 256
        NH = 16
        NKV = 4
        HD = 128
        GROUPS = NH // NKV
        EPS = 1e-06
        B, S, SE = (1, 256, 512)

        def _rmsnorm(x, w, eps=EPS):
            xf = x.astype(jnp.float32)
            var = jnp.mean(xf * xf, axis=-1, keepdims=True)
            return (xf * jax.lax.rsqrt(var + eps)).astype(x.dtype) * w
        key = jax.random.key(seed)
        ks = jax.random.split(key, 12)
        sc = 0.02
        return {'hidden_states': jax.random.normal(ks[0], (B, S, H), jnp.float32), 'encoder_hidden_states': jax.random.normal(ks[1], (B, SE, H), jnp.float32), 'attention_mask': jnp.zeros((B, S, SE), jnp.float32), 'Wq': jax.random.normal(ks[2], (H, NH * HD), jnp.float32) * sc, 'bq': jax.random.normal(ks[3], (NH * HD,), jnp.float32) * sc, 'Wk': jax.random.normal(ks[4], (H, NKV * HD), jnp.float32) * sc, 'bk': jax.random.normal(ks[5], (NKV * HD,), jnp.float32) * sc, 'Wv': jax.random.normal(ks[6], (H, NKV * HD), jnp.float32) * sc, 'bv': jax.random.normal(ks[7], (NKV * HD,), jnp.float32) * sc, 'Wo': jax.random.normal(ks[8], (NH * HD, H), jnp.float32) * sc, 'qn_w': jnp.ones((HD,), jnp.float32), 'kn_w': jnp.ones((HD,), jnp.float32)}
    _L0_xattn_all = _L0_xattn_setup()
    _L0_xattn_in = {k: v for k, v in _L0_xattn_all.items() if k in ('Wq', 'bq', 'Wk', 'bk', 'Wv', 'bv', 'Wo', 'qn_w', 'kn_w')}
    del _L0_xattn_all

    def _L0_attn_setup():
        import jax, jax.numpy as jnp
        import numpy as np
        HIDDEN = 256
        NUM_HEADS = 32
        HEAD_DIM = 64
        NUM_KV = 8
        GROUP = NUM_HEADS // NUM_KV
        SCALE = HEAD_DIM ** (-0.5)
        ROPE_BASE = 10000.0

        def apply_rope(t):
            S, D = (t.shape[-2], t.shape[-1])
            inv_freq = 1.0 / ROPE_BASE ** (jnp.arange(0, D, 2, dtype=jnp.float32) / D)
            ang = jnp.arange(S, dtype=jnp.float32)[:, None] * inv_freq[None, :]
            cos, sin = (jnp.cos(ang), jnp.sin(ang))
            x1, x2 = (t[..., :D // 2], t[..., D // 2:])
            return jnp.concatenate([x1 * cos - x2 * sin, x2 * cos + x1 * sin], axis=-1)
        key = jax.random.key(seed)
        ks = jax.random.split(key, 10)
        B, S = (2, 256)
        s_in = HIDDEN ** (-0.5)
        s_o = (NUM_HEADS * HEAD_DIM) ** (-0.5)
        return {'x': jax.random.normal(ks[0], (B, S, HIDDEN), jnp.float32), 'Wq': jax.random.normal(ks[1], (NUM_HEADS * HEAD_DIM, HIDDEN), jnp.float32) * s_in, 'bq': jnp.zeros((NUM_HEADS * HEAD_DIM,), jnp.float32), 'Wk': jax.random.normal(ks[2], (NUM_KV * HEAD_DIM, HIDDEN), jnp.float32) * s_in, 'bk': jnp.zeros((NUM_KV * HEAD_DIM,), jnp.float32), 'Wv': jax.random.normal(ks[3], (NUM_KV * HEAD_DIM, HIDDEN), jnp.float32) * s_in, 'bv': jnp.zeros((NUM_KV * HEAD_DIM,), jnp.float32), 'Wo': jax.random.normal(ks[4], (HIDDEN, NUM_HEADS * HEAD_DIM), jnp.float32) * s_o, 'bo': jnp.zeros((HIDDEN,), jnp.float32), 'key_weights': jax.random.normal(ks[5], (NUM_HEADS,), jnp.float32)}
    _L0_attn_all = _L0_attn_setup()
    _L0_attn_in = {k: v for k, v in _L0_attn_all.items() if k in ('Wq', 'bq', 'Wk', 'bk', 'Wv', 'bv', 'Wo', 'bo', 'key_weights')}
    del _L0_attn_all

    def _L0_ffn_setup():
        import jax, jax.numpy as jnp
        import numpy as np
        B, S, D = (4, 256, 256)
        DFF = 704
        E, K, R = (8, 2, 16)
        SCALING = 32.0 / 16.0
        key = jax.random.key(seed)
        ks = jax.random.split(key, 12)
        s = lambda k, shape, scale: jax.random.normal(k, shape, dtype=jnp.float32) * scale
        return {'x': s(ks[0], (B, S, D), 1.0), 'Wg': s(ks[1], (DFF, D), 0.02), 'Wu': s(ks[2], (DFF, D), 0.02), 'Wd': s(ks[3], (D, DFF), 0.02), 'Wr': s(ks[4], (E, D), 0.02), 'Ag': s(ks[5], (E, R, D), 0.02), 'Bg': s(ks[6], (E, DFF, R), 0.02), 'Au': s(ks[7], (E, R, D), 0.02), 'Bu': s(ks[8], (E, DFF, R), 0.02), 'Ad': s(ks[9], (E, R, DFF), 0.02), 'Bd': s(ks[10], (E, D, R), 0.02)}
    _L0_ffn_all = _L0_ffn_setup()
    _L0_ffn_in = {k: v for k, v in _L0_ffn_all.items() if k in ('Wg', 'Wu', 'Wd', 'Wr', 'Ag', 'Bg', 'Au', 'Bu', 'Ad', 'Bd')}
    del _L0_ffn_all
    return {'x': x, 'ctx_2048': ctx_2048, 'mask_1xSxS2_ff0': mask_1xSxS2_ff0, 'L0_xattn_Wq': _L0_xattn_in['Wq'], 'L0_xattn_bq': _L0_xattn_in['bq'], 'L0_xattn_Wk': _L0_xattn_in['Wk'], 'L0_xattn_bk': _L0_xattn_in['bk'], 'L0_xattn_Wv': _L0_xattn_in['Wv'], 'L0_xattn_bv': _L0_xattn_in['bv'], 'L0_xattn_Wo': _L0_xattn_in['Wo'], 'L0_xattn_qn_w': _L0_xattn_in['qn_w'], 'L0_xattn_kn_w': _L0_xattn_in['kn_w'], 'L0_attn_Wq': _L0_attn_in['Wq'], 'L0_attn_bq': _L0_attn_in['bq'], 'L0_attn_Wk': _L0_attn_in['Wk'], 'L0_attn_bk': _L0_attn_in['bk'], 'L0_attn_Wv': _L0_attn_in['Wv'], 'L0_attn_bv': _L0_attn_in['bv'], 'L0_attn_Wo': _L0_attn_in['Wo'], 'L0_attn_bo': _L0_attn_in['bo'], 'L0_attn_key_weights': _L0_attn_in['key_weights'], 'L0_ffn_Wg': _L0_ffn_in['Wg'], 'L0_ffn_Wu': _L0_ffn_in['Wu'], 'L0_ffn_Wd': _L0_ffn_in['Wd'], 'L0_ffn_Wr': _L0_ffn_in['Wr'], 'L0_ffn_Ag': _L0_ffn_in['Ag'], 'L0_ffn_Bg': _L0_ffn_in['Bg'], 'L0_ffn_Au': _L0_ffn_in['Au'], 'L0_ffn_Bu': _L0_ffn_in['Bu'], 'L0_ffn_Ad': _L0_ffn_in['Ad'], 'L0_ffn_Bd': _L0_ffn_in['Bd']}

def reference(x, ctx_2048, mask_1xSxS2_ff0, L0_xattn_Wq, L0_xattn_bq, L0_xattn_Wk, L0_xattn_bk, L0_xattn_Wv, L0_xattn_bv, L0_xattn_Wo, L0_xattn_qn_w, L0_xattn_kn_w, L0_attn_Wq, L0_attn_bq, L0_attn_Wk, L0_attn_bk, L0_attn_Wv, L0_attn_bv, L0_attn_Wo, L0_attn_bo, L0_attn_key_weights, L0_ffn_Wg, L0_ffn_Wu, L0_ffn_Wd, L0_ffn_Wr, L0_ffn_Ag, L0_ffn_Bg, L0_ffn_Au, L0_ffn_Bu, L0_ffn_Ad, L0_ffn_Bd):
    import jax
    import jax.numpy as jnp

    def _L0_xattn_ref(hidden_states, encoder_hidden_states, attention_mask, Wq, bq, Wk, bk, Wv, bv, Wo, qn_w, kn_w):
        import jax, jax.numpy as jnp
        import numpy as np
        H = 256
        NH = 16
        NKV = 4
        HD = 128
        GROUPS = NH // NKV
        EPS = 1e-06
        B, S, SE = (1, 256, 512)

        def _rmsnorm(x, w, eps=EPS):
            xf = x.astype(jnp.float32)
            var = jnp.mean(xf * xf, axis=-1, keepdims=True)
            return (xf * jax.lax.rsqrt(var + eps)).astype(x.dtype) * w
        b, s, _ = hidden_states.shape
        se = encoder_hidden_states.shape[1]
        q = (hidden_states @ Wq + bq).reshape(b, s, NH, HD).transpose(0, 2, 1, 3)
        k = (encoder_hidden_states @ Wk + bk).reshape(b, se, NKV, HD).transpose(0, 2, 1, 3)
        v = (encoder_hidden_states @ Wv + bv).reshape(b, se, NKV, HD).transpose(0, 2, 1, 3)
        k = jnp.repeat(k, GROUPS, axis=1)
        v = jnp.repeat(v, GROUPS, axis=1)
        q = _rmsnorm(q, qn_w)
        k = _rmsnorm(k, kn_w)
        scale = 1.0 / np.sqrt(HD).astype(np.float32)
        scores = jnp.einsum('bhsd,bhed->bhse', q, k) * scale
        scores = scores + attention_mask[:, None, :, :]
        probs = jax.nn.softmax(scores.astype(jnp.float32), axis=-1).astype(q.dtype)
        out = jnp.einsum('bhse,bhed->bhsd', probs, v)
        out = out.transpose(0, 2, 1, 3).reshape(b, s, NH * HD)
        return out @ Wo

    def _L0_attn_ref(x, Wq, bq, Wk, bk, Wv, bv, Wo, bo, key_weights):
        import jax, jax.numpy as jnp
        import numpy as np
        HIDDEN = 256
        NUM_HEADS = 32
        HEAD_DIM = 64
        NUM_KV = 8
        GROUP = NUM_HEADS // NUM_KV
        SCALE = HEAD_DIM ** (-0.5)
        ROPE_BASE = 10000.0

        def apply_rope(t):
            S, D = (t.shape[-2], t.shape[-1])
            inv_freq = 1.0 / ROPE_BASE ** (jnp.arange(0, D, 2, dtype=jnp.float32) / D)
            ang = jnp.arange(S, dtype=jnp.float32)[:, None] * inv_freq[None, :]
            cos, sin = (jnp.cos(ang), jnp.sin(ang))
            x1, x2 = (t[..., :D // 2], t[..., D // 2:])
            return jnp.concatenate([x1 * cos - x2 * sin, x2 * cos + x1 * sin], axis=-1)
        B, S, _ = x.shape
        q = (x @ Wq.T + bq).reshape(B, S, NUM_HEADS, HEAD_DIM).transpose(0, 2, 1, 3)
        k = (x @ Wk.T + bk).reshape(B, S, NUM_KV, HEAD_DIM).transpose(0, 2, 1, 3)
        v = (x @ Wv.T + bv).reshape(B, S, NUM_KV, HEAD_DIM).transpose(0, 2, 1, 3)
        q = apply_rope(q)
        k = apply_rope(k)
        qg = q.reshape(B, NUM_KV, GROUP, S, HEAD_DIM)
        scores = jnp.einsum('bkgsd,bktd->bkgst', qg, k) * SCALE
        scores = scores * key_weights.reshape(1, NUM_KV, GROUP, 1, 1)
        causal = jnp.tril(jnp.ones((S, S), bool))
        scores = jnp.where(causal, scores, -jnp.inf)
        a = jax.nn.softmax(scores, axis=-1)
        o = jnp.einsum('bkgst,bktd->bkgsd', a, v)
        o = o.reshape(B, NUM_HEADS, S, HEAD_DIM).transpose(0, 2, 1, 3).reshape(B, S, NUM_HEADS * HEAD_DIM)
        return o @ Wo.T + bo

    def _L0_ffn_ref(x, Wg, Wu, Wd, Wr, Ag, Bg, Au, Bu, Ad, Bd):
        import jax, jax.numpy as jnp
        import numpy as np
        B, S, D = (4, 256, 256)
        DFF = 704
        E, K, R = (8, 2, 16)
        SCALING = 32.0 / 16.0
        b, s, d = x.shape
        xf = x.reshape(-1, d)
        gate_base = xf @ Wg.T
        up_base = xf @ Wu.T
        base_out = jax.nn.silu(gate_base) * up_base @ Wd.T
        router_logits = xf @ Wr.T
        probs = jax.nn.softmax(router_logits.astype(jnp.float32), axis=-1)
        topw, topi = jax.lax.top_k(probs, K)
        topw = topw.astype(x.dtype)
        expert_w = jnp.sum(jax.nn.one_hot(topi, E, dtype=x.dtype) * topw[..., None], axis=1)

        def expert_step(acc, params):
            Ag_e, Bg_e, Au_e, Bu_e, Ad_e, Bd_e, we = params
            g_lora = xf @ Ag_e.T @ Bg_e.T * SCALING
            u_lora = xf @ Au_e.T @ Bu_e.T * SCALING
            h = jax.nn.silu(gate_base + g_lora) * (up_base + u_lora)
            d_delta = h @ Ad_e.T @ Bd_e.T * SCALING
            return (acc + d_delta * we[:, None], None)
        acc0 = jnp.zeros_like(base_out)
        acc, _ = jax.lax.scan(expert_step, acc0, (Ag, Bg, Au, Bu, Ad, Bd, expert_w.T))
        return (base_out + acc).reshape(b, s, d)
    x = x + _L0_xattn_ref(_layernorm(x, axis=-1), ctx_2048, mask_1xSxS2_ff0, L0_xattn_Wq, L0_xattn_bq, L0_xattn_Wk, L0_xattn_bk, L0_xattn_Wv, L0_xattn_bv, L0_xattn_Wo, L0_xattn_qn_w, L0_xattn_kn_w)
    x = x + _L0_attn_ref(_layernorm(x, axis=-1), L0_attn_Wq, L0_attn_bq, L0_attn_Wk, L0_attn_bk, L0_attn_Wv, L0_attn_bv, L0_attn_Wo, L0_attn_bo, L0_attn_key_weights)
    x = x + _L0_ffn_ref(_layernorm(x, axis=-1), L0_ffn_Wg, L0_ffn_Wu, L0_ffn_Wd, L0_ffn_Wr, L0_ffn_Ag, L0_ffn_Bg, L0_ffn_Au, L0_ffn_Bu, L0_ffn_Ad, L0_ffn_Bd)
    return x

_drawn_inputs = setup_inputs


def setup_inputs(seed=0):
    import zlib

    import numpy as np

    out = dict(_drawn_inputs(seed))
    spreads = {'L0_xattn_qn_w': (1.0, 0.6),
     'L0_xattn_kn_w': (1.0, 0.6),
     'L0_attn_bq': (0.0, 0.29),
     'L0_attn_bk': (0.0, 0.649),
     'L0_attn_bv': (0.0, 0.1),
     'L0_attn_bo': (0.0, 0.1)}
    factors = {'L0_xattn_bq': 8.0,
     'L0_xattn_bk': 8.0,
     'L0_ffn_Wr': 8.0,
     'L0_ffn_Ag': 8.0,
     'L0_ffn_Bg': 8.0,
     'L0_ffn_Au': 8.0,
     'L0_ffn_Bu': 8.0,
     'L0_ffn_Ad': 8.0,
     'L0_ffn_Bd': 8.0,
     'L0_ffn_Wd': 51.775}
    for name, (base, spread) in spreads.items():
        noise = np.random.default_rng([zlib.crc32(name.encode()), seed]).standard_normal(out[name].shape)
        drawn = base * np.exp(spread * noise) if base else spread * noise
        out[name] = jnp.asarray(drawn.astype(out[name].dtype))
    for name, factor in factors.items():
        out[name] = (out[name] * factor).astype(out[name].dtype)
    return out
```

```python
from contextlib import ExitStack

import concourse.bass as bass
from concourse import mybir

F32 = mybir.dt.float32
F16 = mybir.dt.float16
ALU = mybir.AluOpType
ACT = mybir.ActivationFunctionType
AX = mybir.AxisListType

P = 128
HID = 256
DK = HID // P
S = 32
BT = P // S
WS = 64.0
PS = 4096.0

XH, XKV, XD = 16, 4, 128
XG = XH // XKV
SE = 257
KT = 2
LAST = SE - 1
XR = 3


def split_terms(a, b):
    return [(a[0], b[0]), (a[1], b[0]), (a[0], b[1])]


class Ring:

    def __init__(self, order, tiles, steps, banks, first=1):
        self.first, self.last, self.found, slot, count, held = first, tiles - 1, {}, 0, 0, {}
        for t in range(-1, tiles + 1):
            for i in range(steps):
                for name in order(t, i):
                    if name is not None:
                        count += 1
                        self.found[t, i, name] = (slot % banks, count, held.get(slot % banks, 0))
                        held[slot % banks] = count
                    slot += 1
        for t, i, name in self.found:
            if first <= t < self.last:
                assert self.use(t, i, name) == self.linear(t, i, name), (t, i, name)

    def linear(self, t, i, name):
        (bank, n, before), (_, n2, _) = self.found[self.first, i, name], self.found[self.first + 1, i, name]
        return bank, n + (n2 - n) * (t - self.first), before + (n2 - n) * (t - self.first)

    def use(self, t, i, name):
        return self.found[t, i, name] if isinstance(t, int) else self.linear(t, i, name)


def wait(eng, sem, value):
    if not isinstance(value, int) or value > 0:
        eng.wait_ge(sem, value)


def wait_apart(eng, sem, value, passed):
    wait(eng, sem, value)
    if not isinstance(value, int):
        eng.sem_inc(passed, 1)


def spread(ap, n=P):
    return ap.partition_broadcast(n)


def prepare_cross(nc, io, sb_x, w, tiles):
    with ExitStack() as ctx:
        sb = lambda name, shape, dt=F32: ctx.enter_context(nc.sbuf_tensor(name, shape, dt))
        sem = lambda name: ctx.enter_context(nc.semaphore(name))
        pst = ctx.enter_context(nc.psum_tensor("p0_t", [P, 1024], F16))
        psk = ctx.enter_context(nc.psum_tensor("p0_k", [P, 2, 512], F32))
        psc = ctx.enter_context(nc.psum_tensor("p0_c", [P, HID], F32))
        raw_q = sb("raw_q", [P, DK, XH * XD])
        raw_kv = sb("raw_kv", [P, DK, 2, XKV * XD])
        raw_o = sb("raw_o", [P, XH, HID])
        bvt = sb("bvt", [P, XKV])
        kn = sb("kn", [P, XD])
        ct_in = sb("ct_in", [P, HID])
        ct_hl = sb("ct_hl", [P, 2, HID], F16)
        ctT = sb("ctT", [P, 2, DK, P], F16)
        kb = sb("kb0", [P, XKV * XD])
        ksq = sb("ksq0", [P, XKV * XD])
        ssq = sb("ssq0", [P, XKV])
        rk = sb("rk0", [P, XKV])
        mean = sb("mean0", [P, XKV])
        kh = sb("kh0", [P, 2, XKV * XD], F16)
        vpad = sb("vpad", [P, XKV, XR, XKV * XD], F16)

        w_in, x_in, small_in, mask_in, scratch_out = (sem(n) for n in ("w_in", "x_in", "small_in", "mask_in", "scratch_out"))
        hi_done, lo_done, pool_done, pe_done = (sem(n) for n in ("hi_done", "lo_done", "pool_done", "pe_done"))
        hold = sem("hold")
        block = ctx.enter_context(nc.Block())

        @block.sync
        def _(sp):
            sp.dma_start(raw_q[:], io["Wq"].rearrange("(c p) n -> p c n", p=P)).then_inc(w_in, 16)
            sp.dma_start(raw_kv[:, :, 0, :], io["Wk"].rearrange("(c p) n -> p c n", p=P)).then_inc(w_in, 16)
            sp.dma_start(raw_kv[:, :, 1, :], io["Wv"].rearrange("(c p) n -> p c n", p=P)).then_inc(w_in, 16)
            sp.dma_start(raw_o[:], io["Wo"].rearrange("(h p) n -> p h n", p=P)).then_inc(w_in, 16)
            sp.dma_start(ct_in[:], io["ctx"][:, LAST, :]).then_inc(small_in, 16)
            sp.dma_start(w["bq"][:], spread(io["bq"])).then_inc(small_in, 16)
            sp.dma_start(w["bk"][:], spread(io["bk"])).then_inc(small_in, 16)
            sp.dma_start(w["wqk"][:], spread(io["qn"])).then_inc(small_in, 16)
            sp.dma_start(kn[:], spread(io["kn"])).then_inc(small_in, 16)
            with nc.allow_non_contiguous_dma(reason="512 elements, once"):
                sp.dma_start(bvt[:], io["bv"].rearrange("(k p) -> p k", p=P)).then_inc(small_in, 16)
            for g in range(XG):
                sp.dma_start(w["mask"][g * S:(g + 1) * S, :], io["mask"][0]).then_inc(mask_in, 16)
            sp.dma_start(sb_x[:, 0:tiles, :], io["x"].rearrange("(t p) n -> p t n", p=P)[:, 0:tiles, :]).then_inc(x_in, 16)
            sp.wait_ge(lo_done, 14)
            sp.wait_ge(pool_done, 2)
            for k in range(XKV):
                sp.dma_start(w["v_last"][XR * k:XR * (k + 1)].rearrange("r b n -> b r n"), vpad[:, k, :, :]).then_inc(scratch_out, 16)
            sp.wait_ge(scratch_out, 16 * XKV)
            sp.wait_ge(x_in, 16)

        @block.gpsimd
        def _(pool):
            pool.memset(w["ident"][:], 0.0).then_inc(pool_done, 1)
            pool.wait_ge(pool_done, 1)
            pool.affine_select(out=w["ident"][:], in_=w["ident"][:], compare_op=ALU.not_equal, fill=1.0, base=0,
                               pattern=[[-1, P]], channel_multiplier=1).then_inc(pool_done, 1)
            pool.memset(w["minus_half"][:], -0.5).then_inc(pool_done, 1)
            pool.wait_ge(pool_done, 3)
            pool.wait_ge(lo_done, 9)
            pool.tensor_tensor(rk[:], mean[:], w["minus_half"][:, 0:XKV], ALU.pow).then_inc(pool_done, 1)

        @block.scalar
        def _(act):
            act.wait_ge(w_in, 64)
            act.wait_ge(small_in, 96)
            act.activation(w["Wq"][:, 0], raw_q[:], ACT.Copy, scale=WS).then_inc(hi_done, 1)
            act.activation(w["Wkv"][:, 0], raw_kv[:], ACT.Copy, scale=WS).then_inc(hi_done, 1)
            act.activation(w["Wo"][:, 0], raw_o[:], ACT.Copy, scale=WS).then_inc(hi_done, 1)
            act.activation(ct_hl[:, 0], ct_in[:], ACT.Copy).then_inc(hi_done, 1)
            act.wait_ge(pe_done, 3)
            act.wait_ge(lo_done, 6)
            for k in range(XKV):
                act.activation(vpad[:, k, 0, k * XD:(k + 1) * XD], psk[:, 1, k * XD:(k + 1) * XD], ACT.Copy, scale=1 / WS).then_inc(hi_done, 1)
                act.activation(vpad[:, k, 1, k * XD:(k + 1) * XD], psk[:, 1, k * XD:(k + 1) * XD], ACT.Copy, scale=1 / WS).then_inc(hi_done, 1)

        @block.vector
        def _(dve):
            dve.memset(vpad[:], 0.0)
            dve.wait_ge(small_in, 96)
            dve.wait_ge(mask_in, 16 * XG)
            dve.tensor_scalar(w["mask"][:], w["mask"][:], float(XD) ** 0.5, None, ALU.mult)
            dve.tensor_tensor(w["wqk"][:], w["wqk"][:], kn[:], ALU.mult)
            for n, (name, raw) in enumerate((("Wq", raw_q), ("Wkv", raw_kv), ("Wo", raw_o))):
                dve.wait_ge(hi_done, n + 1)
                if name == "Wkv":
                    dst, src = (w[name][:, h].rearrange("p c v n -> p (c v n)") for h in (1, 0)), raw[:].rearrange("p c v n -> p (c v n)")
                    lo, hi = dst
                else:
                    lo, hi = (w[name][:, h].rearrange("p c n -> p (c n)") for h in (1, 0))
                    src = raw[:].rearrange("p c n -> p (c n)")
                dve.scalar_tensor_tensor(out=lo, in0=src, scalar=WS, in1=hi, op0=ALU.mult, op1=ALU.subtract).then_inc(lo_done, 1)
            dve.wait_ge(hi_done, 4)
            dve.tensor_tensor(ct_hl[:, 1], ct_in[:], ct_hl[:, 0], ALU.subtract).then_inc(lo_done, 1)
            dve.wait_ge(pe_done, 1)
            dve.tensor_copy(ctT[:].rearrange("p l c n -> p (l c n)"), pst[:, 0:2 * DK * P]).then_inc(lo_done, 1)
            dve.wait_ge(pe_done, 2)
            dve.tensor_scalar(w["cvec"][:], psc[:], 1.0, None, ALU.mult).then_inc(lo_done, 1)
            dve.wait_ge(pe_done, 3)
            dve.scalar_tensor_tensor(out=kb[:], in0=psk[:, 0], scalar=1 / WS, in1=w["bk"][:], op0=ALU.mult, op1=ALU.add).then_inc(lo_done, 1)
            dve.wait_ge(lo_done, 7)
            dve.tensor_tensor(ksq[:], kb[:], kb[:], ALU.mult).then_inc(lo_done, 1)
            dve.wait_ge(lo_done, 8)
            dve.tensor_reduce(ssq[:], ksq[:].rearrange("p (k d) -> p k d", k=XKV), AX.X, ALU.add).then_inc(hold, 1)
            dve.wait_ge(hold, 1)
            dve.tensor_scalar(mean[:], ssq[:], 1.0 / XD, 1e-6, ALU.mult, ALU.add).then_inc(lo_done, 1)
            dve.wait_ge(pool_done, 4)
            for k in range(XKV):
                dve.tensor_scalar(kh[:, 0, k * XD:(k + 1) * XD], kb[:, k * XD:(k + 1) * XD], rk[:, k:k + 1], None, ALU.mult).then_inc(hold, 1)
            dve.wait_ge(hold, 1 + XKV)
            for k in range(XKV):
                ins = dve.scalar_tensor_tensor(out=kh[:, 1, k * XD:(k + 1) * XD], in0=kb[:, k * XD:(k + 1) * XD], scalar=rk[:, k:k + 1],
                                               in1=kh[:, 0, k * XD:(k + 1) * XD], op0=ALU.mult, op1=ALU.subtract)
            ins.then_inc(lo_done, 1)
            dve.wait_ge(hi_done, 4 + 2 * XKV)
            for k in range(XKV):
                dve.scalar_tensor_tensor(out=vpad[:, k, 2, k * XD:(k + 1) * XD], in0=psk[:, 1, k * XD:(k + 1) * XD], scalar=1 / WS,
                                         in1=vpad[:, k, 0, k * XD:(k + 1) * XD], op0=ALU.mult, op1=ALU.subtract).then_inc(lo_done, 1)
            dve.wait_ge(pe_done, 4)
            dve.tensor_copy(w["kT_last"][:].rearrange("p l k b -> p (l k b)"), pst[:]).then_inc(lo_done, 1)

        @block.tensor
        def _(pe):
            pe.wait_ge(pool_done, 2)
            pe.wait_ge(lo_done, 4)
            for l in range(2):
                for c in range(DK):
                    ins = pe.transpose(pst[:, (l * DK + c) * P:(l * DK + c + 1) * P], ct_hl[:, l, c * P:(c + 1) * P], w["ident"][:])
            ins.then_inc(pe_done, 1)
            for h in range(XH):
                ins = pe.matmul(psc[:], bvt[:, h // XG:h // XG + 1].broadcast_to([P, P]), raw_o[:, h, :], start=(h == 0), stop=(h == XH - 1))
            ins.then_inc(pe_done, 1)
            pe.wait_ge(lo_done, 5)
            for v in range(2):
                n = 0
                for c in range(DK):
                    for a, b in ((0, 0), (1, 0), (0, 1)):
                        ins = pe.matmul(psk[:, v], ctT[:, a, c, :], w["Wkv"][:, b, c, v, :], start=(n == 0), stop=(n == 3 * DK - 1))
                        n += 1
            ins.then_inc(pe_done, 1)
            pe.wait_ge(lo_done, 10)
            for l in range(2):
                for k in range(XKV):
                    ins = pe.transpose(pst[:, (l * XKV + k) * P:(l * XKV + k + 1) * P], kh[:, l, k * XD:(k + 1) * XD], w["ident"][:])
            ins.then_inc(pe_done, 1)


def cross_attention(nc, io, sb_x, w, tiles):
    rows = tiles * BT
    with ExitStack() as ctx:
        sb = lambda name, shape, dt=F32: ctx.enter_context(nc.sbuf_tensor(name, shape, dt))
        sem = lambda name: ctx.enter_context(nc.semaphore(name))
        bank_t = [ctx.enter_context(nc.psum_tensor(f"turn{n}", [P, 1024], F16)) for n in range(3)]
        bank_m = [ctx.enter_context(nc.psum_tensor(f"proj{n}", [P, 512], F32)) for n in range(2)]
        bank_s = [ctx.enter_context(nc.psum_tensor(f"score{n}", [P, SE], F32)) for n in range(2)]
        bank_o = ctx.enter_context(nc.psum_tensor("sum", [P, XKV, XG * S], F32))

        c_in = [sb(f"c_in{n}", [P, KT, HID]) for n in range(2)]
        c_hl = [sb(f"c_hl{n}", [P, 2, KT, HID], F16) for n in range(2)]
        cT = [sb(f"cT{n}", [P, 2, DK, KT, P], F16) for n in range(2)]
        k_b = sb("k_b", [P, KT, XKV * XD])
        k_sq = sb("k_sq", [P, KT, XKV * XD])
        k_ss = sb("k_ss", [P, KT * XKV])
        k_ms = sb("k_ms", [P, KT * XKV])
        k_r = sb("k_r", [P, KT * XKV])
        k_n = sb("k_n", [P, KT, XKV * XD])
        k_hl = sb("k_hl", [P, 2, KT, XKV * XD], F16)
        kT = [sb(f"kT{n}", [P, 2, XKV, SE], F16) for n in range(2)]
        v_hl = [sb(f"v_hl{n}", [P, 2, KT, XKV * XD], F16) for n in range(BT)]
        v_end = [sb(f"v_end{n}", [XKV * XR, XKV * XD], F16) for n in range(BT)]
        s_n = sb("s_n", [P, XKV, SE])
        s_min = sb("s_min", [P, XKV])
        p_f = sb("p_f", [P, XKV, SE])
        p_sum = sb("p_sum", [P, XKV])
        p_inv = sb("p_inv", [P, XKV])
        p_scl = sb("p_scl", [P, XKV])
        p_hl = sb("p_hl", [P, 2, XKV, SE], F16)
        p_end = sb("p_end", [P, XKV, XR], F16)
        pT = sb("pT", [P, XKV, 2, KT, P], F16)
        pT_end = sb("pT_end", [XKV * XR, P], F16)
        oT = sb("oT", [P, 2, XH, P], F16)
        n_st = sb("n_st", [P, 6])
        n_ag = sb("n_ag", [P, 2])
        n_r = sb("n_r", [P, 2])
        n_x = sb("n_x", [P, HID])
        n_hl = sb("n_hl", [P, 2, HID], F16)
        nT = sb("nT", [P, 2, DK, P], F16)
        q_b = sb("q_b", [P, XH * XD])
        q_w = sb("q_w", [P, XH * XD])
        q_ms = sb("q_ms", [P, XH])
        q_ss = sb("q_ss", [P, XH])
        q_r = sb("q_r", [P, XH])
        q_hl = sb("q_hl", [P, 2, XH * XD], F16)
        q_sq = q_hl[:].rearrange("p l n -> p (l n)").bitcast(F32)
        qT = sb("qT", [P, 2, XKV, BT, XG, S], F16)

        ctx_loaded = [sem(f"ctx_loaded{n}") for n in range(2)]
        end_loaded = [sem(f"end_loaded{n}") for n in range(BT)]
        t_fill, t_read, m_fill, m_read, s_fill, s_read, o_fill, o_read = (
            sem(n) for n in ("t_fill", "t_read", "m_fill", "m_read", "s_fill", "s_read", "o_fill", "o_read"))
        c_hi, v_hi, k_sqd, k_hi, exp_done, o_hi, n_hi, q_sqd, q_hi = (
            sem(n) for n in ("c_hi", "v_hi", "k_sqd", "k_hi", "exp_done", "o_hi", "n_hi", "q_sqd", "q_hi"))
        c_lo, k_rs, k_lo, k_end, p_hi, p_ends, n_rs, n_lo, q_rs, q_wd, q_lo = (
            sem(n) for n in ("c_lo", "k_rs", "k_lo", "k_end", "p_hi", "p_ends", "n_rs", "n_lo", "q_rs", "q_wd", "q_lo"))
        k_msd, k_nd, p_scd, p_lo, n_msd, n_xd, q_msd, q_nd, link, x_out = (
            sem(n) for n in ("k_msd", "k_nd", "p_scd", "p_lo", "n_msd", "n_xd", "q_msd", "q_nd", "link", "x_out"))

        row = lambda t, i: BT * t + i
        has = lambda j: not isinstance(j, int) or 0 <= j < rows
        has_tile = lambda t: not isinstance(t, int) or 0 <= t < tiles

        def order_t(t, i):
            j = row(t, i)
            out = (["K0", "K1"] if has(j - 1) else []) + (["P0", "P1", "Pe"] if has(j - 2) else [])
            out += ["Q0", "Q1", "Q2", "Q3"] if i == 0 and has_tile(t) else []
            out += ["C"] if has(j + 1) else []
            out += ["X"] if i == 0 and has_tile(t + 1) else []
            return out + ([None] if i == 3 else [])

        def order_m(t, i):
            out = ["W"] + [None] if i == 2 and has_tile(t - 1) else []
            out += ["K0", "V0", "K1", "V1"] if has(row(t, i)) else []
            return out + (["Q0", "Q1", "Q2", "Q3"] if i == 1 and has_tile(t + 1) else [])

        passed_dve, passed_pool = sem("passed_dve"), sem("passed_pool")
        turns, projs = Ring(order_t, tiles, BT, 3), Ring(order_m, tiles, BT, 2)
        block = ctx.enter_context(nc.Block())

        def over_tiles(eng, tile):
            tile(-1)
            tile(0)
            with eng.Fori(1, tiles - 1) as t:
                tile(t)
            tile(tiles - 1)
            tile(tiles)

        @block.sync
        def _(sp):
            def tile(t):
                for i in range(BT):
                    j = row(t, i)
                    if has(j + 2):
                        wait(sp, c_lo, j + 1)
                        sp.dma_start(c_in[i % 2][:], io["ctx"][bass.ds(j + 2, 1), 0:LAST, :].rearrange("o (c p) n -> p (o c) n", p=P)
                                     ).then_inc(ctx_loaded[i % 2], 16)
                    if has(j):
                        wait(sp, o_fill, j - 3)
                        sp.dma_start(v_end[i][:], w["v_last"][:, bass.ds(j, 1), :].rearrange("r o n -> r (o n)")).then_inc(end_loaded[i], 16)
            over_tiles(sp, tile)

        @block.gpsimd
        def _(pool):
            def tile(t):
                for i in range(BT):
                    j = row(t, i)
                    if has(j - 1):
                        wait_apart(pool, s_fill, XKV * (j - 2), passed_pool)
                        pool.tensor_copy(kT[(i - 1) % 2][:, :, :, LAST:SE],
                                         w["kT_last"][:, :, :, bass.ds(j - 1, 1)]).then_inc(k_end, 1)
                    if has_tile(t + 1) and i == 0:
                        pool.wait_ge(n_msd, t + 2)
                        wait(pool, n_xd, t + 1)
                        pool.tensor_tensor(n_r[:, 0:1], n_r[:, 1:2], w["minus_half"][:, 0:1], ALU.pow).then_inc(n_rs, 1)
                        pool.wait_ge(n_hi, t + 2)
                        pool.tensor_tensor(n_hl[:, 1], n_x[:], n_hl[:, 0], ALU.subtract).then_inc(n_lo, 1)
                    if has(j + 2):
                        pool.wait_ge(c_hi, j + 3)
                        pool.tensor_tensor(c_hl[i % 2][:, 1], c_in[i % 2][:], c_hl[i % 2][:, 0], ALU.subtract).then_inc(c_lo, 1)
                    if i == 2 and has_tile(t + 1):
                        pool.wait_ge(m_read, projs.use(t, 1, "Q3")[1])
                        wait(pool, q_nd, t + 1)
                        pool.tensor_tensor(q_w[:].rearrange("p (h d) -> p h d", h=XH), q_b[:].rearrange("p (h d) -> p h d", h=XH),
                                           w["wqk"][:].unsqueeze(1).broadcast_to([P, XH, XD]), ALU.mult).then_inc(q_wd, 1)
                        pool.wait_ge(q_msd, t + 2)
                        pool.tensor_tensor(q_r[:], q_ms[:], w["minus_half"][:, 0:XH], ALU.pow).then_inc(q_rs, 1)
                    if has(j - 1):
                        pool.wait_ge(p_scd, j)
                        wait_apart(pool, t_fill, turns.use(t, i, "Pe")[1] if has(j - 2) else 0, passed_pool)
                        for k in range(XKV):
                            ins = pool.tensor_scalar(p_hl[:, 0, k, :], p_f[:, k, :], p_scl[:, k:k + 1], None, ALU.mult)
                        ins.then_inc(p_hi, 1)
                        wait_apart(pool, p_lo, j, passed_pool)
                        for r, part in enumerate((0, 1, 0)):
                            ins = pool.tensor_copy(p_end[:, :, r], p_hl[:, part, :, LAST])
                        ins.then_inc(p_ends, 1)
                    if has(j):
                        pool.wait_ge(k_msd, j + 1)
                        wait(pool, k_nd, j)
                        pool.tensor_tensor(k_r[:], k_ms[:], w["minus_half"][:, 0:KT * XKV], ALU.pow).then_inc(k_rs, 1)
                        pool.wait_ge(k_hi, j + 1)
                        pool.tensor_tensor(k_hl[:, 1], k_n[:], k_hl[:, 0], ALU.subtract).then_inc(k_lo, 1)
                    if i == 3 and has_tile(t + 1):
                        pool.wait_ge(q_hi, t + 2)
                        pool.tensor_tensor(q_hl[:, 1], q_w[:], q_hl[:, 0], ALU.subtract).then_inc(q_lo, 1)
            over_tiles(pool, tile)

        @block.scalar
        def _(act):
            def tile(t):
                for i in range(BT):
                    j = row(t, i)
                    if has(j):
                        act.wait_ge(m_fill, projs.use(t, i, "V0")[1])
                        wait(act, o_fill, j - 3)
                        act.activation(v_hl[i][:, 0, 0, :], bank_m[projs.use(t, i, "V0")[0]][:], ACT.Copy, scale=1 / WS).then_inc(v_hi, 1)
                    if has(j - 1):
                        wait(act, p_lo, j - 1)
                        for k in range(XKV):
                            act.wait_ge(s_read, XKV * (j - 1) + k + 1)
                            ins = act.activation(p_f[:, k, :], s_n[:, k, :], ACT.Exp, bias=s_min[:, k:k + 1], scale=-1.0,
                                                 accum_out=p_sum[:, k:k + 1])
                        ins.then_inc(exp_done, 1)
                    if has(j):
                        act.wait_ge(m_fill, projs.use(t, i, "V1")[1])
                        act.activation(v_hl[i][:, 0, 1, :], bank_m[projs.use(t, i, "V1")[0]][:], ACT.Copy, scale=1 / WS).then_inc(v_hi, 1)
                        act.wait_ge(m_read, projs.use(t, i, "K1")[1])
                        act.activation(k_sq[:], k_b[:], ACT.Square).then_inc(k_sqd, 1)
                    if has(j - 2):
                        act.wait_ge(o_fill, j - 1)
                        tt = t if i >= 2 else t - 1
                        if has_tile(tt - 1):
                            act.wait_ge(m_fill, projs.use(tt, 2, "W")[1])
                        b = (i - 2) % BT
                        act.activation(oT[:, 0, :, b * S:(b + 1) * S], bank_o[:].rearrange("p k (g s) -> p (k g) s", g=XG), ACT.Copy,
                                       scale=1 / PS).then_inc(o_hi, 1)
                    if has(j + 2):
                        act.wait_ge(ctx_loaded[i % 2], 16 * (2 * t + i // 2 + 2))
                        wait(act, t_fill, turns.use(t, i - 1, "C")[1] if i else turns.use(t - 1, 3, "C")[1]) if has(j) else None
                        act.activation(c_hl[i % 2][:, 0], c_in[i % 2][:], ACT.Copy).then_inc(c_hi, 1)
                    if i == 0 and has_tile(t + 1):
                        act.wait_ge(n_xd, t + 2)
                        act.activation(n_hl[:, 0], n_x[:], ACT.Copy).then_inc(n_hi, 1)
                    if i == 2 and has_tile(t + 1):
                        act.wait_ge(m_read, projs.use(t, 1, "Q3")[1])
                        if has_tile(t):
                            act.wait_ge(t_fill, turns.use(t, 0, "Q3")[1])
                        act.activation(q_sq, q_b[:], ACT.Square).then_inc(q_sqd, 1)
                    if has(j):
                        act.wait_ge(k_nd, j + 1)
                        act.activation(k_hl[:, 0], k_n[:], ACT.Copy).then_inc(k_hi, 1)
                    if i == 3 and has_tile(t + 1):
                        act.wait_ge(q_nd, t + 2)
                        act.activation(q_hl[:, 0], q_w[:], ACT.Copy).then_inc(q_hi, 1)
            over_tiles(act, tile)

        @block.vector
        def _(dve):
            linked = [0]

            def read_turned(t, i, name, out, columns=1024, rows_=P):
                bank, n, _ = turns.use(t, i, name)
                dve.wait_ge(t_fill, n)
                dve.tensor_copy(out, bank_t[bank][0:rows_, 0:columns]).then_inc(t_read, 1)

            def tile(t):
                for i in range(BT):
                    j = row(t, i)
                    if i == 0 and has_tile(t + 1):
                        dve.bn_stats(n_st[:], sb_x[:, bass.ds(t + 1, 1), :].rearrange("p o n -> p (o n)")).then_inc(link_a, 1)
                        wait_apart(dve, link_a, 2 * (t + 1) + 1, passed_dve)
                        dve.bn_aggr(n_ag[:], n_st[:]).then_inc(link_a, 1)
                        dve.wait_ge(link_a, 2 * (t + 1) + 2)
                        wait(dve, n_rs, t + 1)
                        dve.tensor_scalar(n_r[:, 1:2], n_ag[:, 1:2], 1e-5, None, ALU.add).then_inc(n_msd, 1)
                    if has(j - 1):
                        wait(dve, s_fill, XKV * (j - 2))
                        for c in range(KT):
                            bank, n, _ = turns.use(t, i, f"K{c}")
                            dve.wait_ge(t_fill, n)
                            dve.tensor_copy(kT[(i - 1) % 2][:, :, :, c * P:(c + 1) * P],
                                            bank_t[bank][:].rearrange("p (l k n) -> p l k n", l=2, k=XKV)).then_inc(t_read, 1)
                    if has(j - 2):
                        wait(dve, o_fill, j - 2)
                        for half in range(2):
                            read_turned(t, i, f"P{half}", pT[:, 2 * half:2 * half + 2].rearrange("p k l c n -> p (k l c n)"))
                        read_turned(t, i, "Pe", pT_end[:], P, XKV * XR)
                    if i == 2 and has_tile(t - 1):
                        bank, n, _ = projs.use(t, i, "W")
                        dve.wait_ge(m_fill, n)
                        x_t = sb_x[:, bass.ds(t - 1, 1), :].rearrange("p o n -> p (o n)")
                        dve.scalar_tensor_tensor(out=x_t, in0=bank_m[bank][:, 0:HID], scalar=1 / WS, in1=x_t,
                                                 op0=ALU.mult, op1=ALU.add).then_inc(m_read, 1)
                        dve.wait_ge(m_read, n)
                        dve.tensor_tensor(x_t, x_t, w["cvec"][:], ALU.add).then_inc(x_out, 1)
                    if i == 0 and has_tile(t + 1):
                        dve.wait_ge(n_rs, t + 2)
                        wait(dve, n_lo, t + 1)
                        dve.tensor_scalar(n_x[:], sb_x[:, bass.ds(t + 1, 1), :].rearrange("p o n -> p (o n)"), n_ag[:, 0:1], n_r[:, 0:1],
                                          ALU.subtract, ALU.mult).then_inc(n_xd, 1)
                    for c in range(KT):
                        if has(j):
                            bank, n, _ = projs.use(t, i, f"K{c}")
                            dve.wait_ge(m_fill, n)
                            wait(dve, k_nd, j)
                            wait(dve, k_sqd, j)
                            dve.scalar_tensor_tensor(out=k_b[:, c, :], in0=bank_m[bank][:], scalar=1 / WS, in1=w["bk"][:],
                                                     op0=ALU.mult, op1=ALU.add).then_inc(m_read, 1)
                            bank, n, _ = projs.use(t, i, f"V{c}")
                            dve.wait_ge(v_hi, KT * j + c + 1)
                            dve.scalar_tensor_tensor(out=v_hl[i][:, 1, c, :], in0=bank_m[bank][:], scalar=1 / WS, in1=v_hl[i][:, 0, c, :],
                                                     op0=ALU.mult, op1=ALU.subtract).then_inc(m_read, 1)
                        if has(j - 1) and c == 0:
                            wait(dve, exp_done, j - 1)
                            for k in range(XKV):
                                wait_apart(dve, s_fill, XKV * (j - 1) + k + 1, passed_dve)
                                dve.tensor_tensor_reduce(out=s_n[:, k, :], in0=bank_s[k % 2][:], in1=w["mask"][:], scale=-(XD ** -0.5),
                                                         scalar=3e38, op0=ALU.add, op1=ALU.min,
                                                         accum_out=s_min[:, k:k + 1]).then_inc(s_read, 1)
                    if i == 0 and has_tile(t):
                        wait(dve, s_fill, XKV * BT * t)
                        for k in range(XKV):
                            bank, n, _ = turns.use(t, i, f"Q{k}")
                            dve.wait_ge(t_fill, n)
                            src = bank_t[bank][:].rearrange("p (l g b s) -> p l b g s", l=2, g=XG, b=BT)
                            dve.tensor_copy(qT[:, 0, k], src[:, 0])
                            dve.tensor_copy(qT[:, 1, k], src[:, 1]).then_inc(t_read, 1)
                    if has(j - 1):
                        dve.wait_ge(exp_done, j)
                        wait(dve, p_hi, j - 1)
                        wait(dve, p_lo, j - 1)
                        dve.reciprocal(p_inv[:], p_sum[:]).then_inc(link_p, 1)
                        dve.wait_ge(link_p, j)
                        dve.tensor_scalar(p_scl[:], p_inv[:], PS, None, ALU.mult).then_inc(p_scd, 1)
                    if has(j):
                        dve.wait_ge(k_sqd, j + 1)
                        dve.tensor_reduce(k_ss[:], k_sq[:].rearrange("p c (k d) -> p (c k) d", k=XKV), AX.X, ALU.add).then_inc(link_k, 1)
                        dve.wait_ge(link_k, j + 1)
                        wait(dve, k_rs, j)
                        dve.tensor_scalar(k_ms[:], k_ss[:], 1.0 / XD, 1e-6, ALU.mult, ALU.add).then_inc(k_msd, 1)
                    if has(j + 1):
                        read_turned(t, i, "C", cT[(i + 1) % 2][:].rearrange("p l d c n -> p (l d c n)"))
                    if i == 0 and has_tile(t + 1):
                        read_turned(t, i, "X", nT[:].rearrange("p l d n -> p (l d n)"), 2 * DK * P)
                    if has(j - 2):
                        dve.wait_ge(o_hi, j - 1)
                        b = (i - 2) % BT
                        dve.scalar_tensor_tensor(out=oT[:, 1, :, b * S:(b + 1) * S], in0=bank_o[:].rearrange("p k (g s) -> p (k g) s", g=XG),
                                                 scalar=1 / PS, in1=oT[:, 0, :, b * S:(b + 1) * S],
                                                 op0=ALU.mult, op1=ALU.subtract).then_inc(o_read, 1)
                    if i == 1 and has_tile(t + 1):
                        wait(dve, q_wd, t + 1)
                        wait(dve, q_sqd, t + 1)
                        for c in range(XKV):
                            bank, n, _ = projs.use(t, i, f"Q{c}")
                            dve.wait_ge(m_fill, n)
                            dve.scalar_tensor_tensor(out=q_b[:, 512 * c:512 * (c + 1)], in0=bank_m[bank][:], scalar=1 / WS,
                                                     in1=w["bq"][:, 512 * c:512 * (c + 1)], op0=ALU.mult, op1=ALU.add).then_inc(m_read, 1)
                    if i == 2 and has_tile(t + 1):
                        dve.wait_ge(q_sqd, t + 2)
                        dve.tensor_reduce(q_ss[:], q_sq.rearrange("p (h d) -> p h d", h=XH), AX.X, ALU.add).then_inc(link_q, 1)
                        dve.wait_ge(link_q, t + 2)
                        wait(dve, q_rs, t + 1)
                        dve.tensor_scalar(q_ms[:], q_ss[:], 1.0 / XD, 1e-6, ALU.mult, ALU.add).then_inc(q_msd, 1)
                    if has(j - 1):
                        dve.wait_ge(p_hi, j)
                        wait(dve, t_fill, turns.use(t, i, "P1")[1] if has(j - 2) else 0)
                        for k in range(XKV):
                            ins = dve.scalar_tensor_tensor(out=p_hl[:, 1, k, :], in0=p_f[:, k, :], scalar=p_scl[:, k:k + 1],
                                                           in1=p_hl[:, 0, k, :], op0=ALU.mult, op1=ALU.subtract)
                        ins.then_inc(p_lo, 1)
                    if has(j):
                        dve.wait_ge(k_rs, j + 1)
                        wait(dve, k_lo, j)
                        dve.tensor_tensor(k_n[:].rearrange("p c (k d) -> p (c k) d", k=XKV), k_b[:].rearrange("p c (k d) -> p (c k) d", k=XKV),
                                          k_r[:].unsqueeze(2).broadcast_to([P, KT * XKV, XD]), ALU.mult).then_inc(k_nd, 1)
                    if i == 3 and has_tile(t + 1):
                        dve.wait_ge(q_rs, t + 2)
                        dve.wait_ge(q_wd, t + 2)
                        dve.tensor_tensor(q_w[:].rearrange("p (h d) -> p h d", h=XH), q_w[:].rearrange("p (h d) -> p h d", h=XH),
                                          q_r[:].unsqueeze(2).broadcast_to([P, XH, XD]), ALU.mult).then_inc(q_nd, 1)
            link_a, link_p, link_k, link_q = (sem(n) for n in ("link_a", "link_p", "link_k", "link_q"))
            over_tiles(dve, tile)

        @block.tensor
        def _(pe):
            ident = w["ident"]

            def take(ring, t, i, name, read):
                bank, n, before = ring.use(t, i, name)
                wait(pe, read, before)
                return bank

            def project(t, i, name, terms):
                out = bank_m[take(projs, t, i, name, m_read)]
                for n, (a, b) in enumerate(terms):
                    ins = pe.matmul(out[:, 0:b.shape[-1]], a, b, start=(n == 0), stop=(n == len(terms) - 1))
                ins.then_inc(m_fill, 1)

            def tile(t):
                for i in range(BT):
                    j = row(t, i)
                    if has(j - 1):
                        pe.wait_ge(k_lo, j)
                        for c in range(KT):
                            out = bank_t[take(turns, t, i, f"K{c}", t_read)]
                            for l in range(2):
                                for k in range(XKV):
                                    ins = pe.transpose(out[:, (l * XKV + k) * P:(l * XKV + k + 1) * P], k_hl[:, l, c, k * XD:(k + 1) * XD], ident[:])
                            ins.then_inc(t_fill, 1)
                    if has(j - 2):
                        pe.wait_ge(p_lo, j - 1)
                        for half in range(2):
                            out = bank_t[take(turns, t, i, f"P{half}", t_read)]
                            n = 0
                            for k in (2 * half, 2 * half + 1):
                                for l in range(2):
                                    for c in range(KT):
                                        ins = pe.transpose(out[:, n * P:(n + 1) * P], p_hl[:, l, k, c * P:(c + 1) * P], ident[:])
                                        n += 1
                            ins.then_inc(t_fill, 1)
                        pe.wait_ge(p_ends, j - 1)
                        out = bank_t[take(turns, t, i, "Pe", t_read)]
                        pe.transpose(out[0:XKV * XR, 0:P], p_end[:].rearrange("p k r -> p (k r)"), ident[:]).then_inc(t_fill, 1)
                    if i == 2 and has_tile(t - 1):
                        pe.wait_ge(o_read, BT * t)
                        project(t, i, "W", [(oT[:, a, h, :], w["Wo"][:, b, h, :]) for h in range(XH) for a, b in ((0, 0), (1, 0), (0, 1))])
                    for c in range(KT):
                        if has(j):
                            if c == 0:
                                pe.wait_ge(t_read, turns.use(t, i - 1, "C")[1] if i else turns.use(t - 1, 3, "C")[1])
                            for v, name in enumerate("KV"):
                                project(t, i, f"{name}{c}", [(cT[i % 2][:, a, d, c, :], w["Wkv"][:, b, d, v, :])
                                                             for d in range(DK) for a, b in ((0, 0), (1, 0), (0, 1))])
                        if has(j - 1) and c == 0:
                            pe.wait_ge(t_read, turns.use(t, i, "K1")[1])
                            pe.wait_ge(k_end, j)
                            b = (i - 1) % BT
                            for k in range(XKV):
                                wait(pe, s_read, XKV * (j - 1) + k - 1)
                                for n, (x, y) in enumerate(((0, 0), (1, 0), (0, 1))):
                                    ins = pe.matmul(bank_s[k % 2][:], qT[:, x, k, b].rearrange("p g s -> p (g s)"), kT[(i - 1) % 2][:, y, k, :],
                                                    start=(n == 0), stop=(n == 2))
                                ins.then_inc(s_fill, 1)
                    if i == 0 and has_tile(t):
                        pe.wait_ge(q_lo, t + 1)
                        for k in range(XKV):
                            out = bank_t[take(turns, t, i, f"Q{k}", t_read)]
                            for l in range(2):
                                for g in range(XG):
                                    h = k * XG + g
                                    ins = pe.transpose(out[:, (l * XG + g) * P:(l * XG + g + 1) * P], q_hl[:, l, h * XD:(h + 1) * XD], ident[:])
                            ins.then_inc(t_fill, 1)
                    if has(j - 2):
                        pe.wait_ge(t_read, turns.use(t, i, "Pe")[1])
                        wait(pe, o_read, j - 2)
                        b = (i - 2) % BT
                        pe.wait_ge(end_loaded[b], 16 * (t + 1 if i >= 2 else t))
                        for k in range(XKV):
                            for c in range(KT):
                                for n, (x, y) in enumerate(((0, 0), (1, 0), (0, 1))):
                                    pe.matmul(bank_o[:, k, :], v_hl[b][:, x, c, k * XD:(k + 1) * XD], pT[:, k, y, c, :],
                                              start=(c == 0 and n == 0), stop=False)
                            ins = pe.matmul(bank_o[:, k, :], v_end[b][:, k * XD:(k + 1) * XD], pT_end[:], start=False, stop=True)
                        ins.then_inc(o_fill, 1)
                    if has(j + 1):
                        pe.wait_ge(c_lo, j + 2)
                        out = bank_t[take(turns, t, i, "C", t_read)]
                        n = 0
                        for l in range(2):
                            for d in range(DK):
                                for c in range(KT):
                                    ins = pe.transpose(out[:, n * P:(n + 1) * P], c_hl[(i + 1) % 2][:, l, c, d * P:(d + 1) * P], ident[:])
                                    n += 1
                        ins.then_inc(t_fill, 1)
                    if i == 0 and has_tile(t + 1):
                        pe.wait_ge(n_lo, t + 2)
                        out = bank_t[take(turns, t, i, "X", t_read)]
                        n = 0
                        for l in range(2):
                            for d in range(DK):
                                ins = pe.transpose(out[:, n * P:(n + 1) * P], n_hl[:, l, d * P:(d + 1) * P], ident[:])
                                n += 1
                        ins.then_inc(t_fill, 1)
                    if i == 1 and has_tile(t + 1):
                        pe.wait_ge(t_read, turns.use(t, 0, "X")[1])
                        for c in range(XKV):
                            project(t, i, f"Q{c}", [(nT[:, a, d, :], w["Wq"][:, b, d, 512 * c:512 * (c + 1)])
                                                    for d in range(DK) for a, b in ((0, 0), (1, 0), (0, 1))])
            over_tiles(pe, tile)


def cross_weights(nc, ctx):
    sb = lambda name, shape, dt=F32: ctx.enter_context(nc.sbuf_tensor(name, shape, dt))
    return {
        "Wq": sb("wq_hl", [P, 2, DK, XH * XD], F16), "Wkv": sb("wkv_hl", [P, 2, DK, 2, XKV * XD], F16),
        "Wo": sb("wo_hl", [P, 2, XH, HID], F16), "bq": sb("bq_all", [P, XH * XD]), "bk": sb("bk_all", [P, XKV * XD]),
        "wqk": sb("wqk", [P, XD]), "mask": sb("mask_all", [P, SE]), "cvec": sb("cvec", [P, HID]),
        "kT_last": sb("kT_last", [P, 2, XKV, P], F16),
        "v_last": nc.dram_tensor("v_last", [XKV * XR, P, XKV * XD], F16, kind="Internal").ap(),
    }


AH, AKV, AD = 32, 8, 64
AG = AH // AKV
AQ, AK = AH * AD, AKV * AD
AQKV = AQ + 2 * AK
AP2 = AKV // 2
ROT = AD // 2
PARTS = 4


def prepare_self(nc, io, w):
    with ExitStack() as ctx:
        sb = lambda name, shape, dt=F32: ctx.enter_context(nc.sbuf_tensor(name, shape, dt))
        sem = lambda name: ctx.enter_context(nc.semaphore(name))
        pst = [ctx.enter_context(nc.psum_tensor(f"p1_t{n}", [P, 2 * DK * P], F16)) for n in range(2)]
        NQ, NKV = AQ // P, AK // P
        NR = NQ + 2 * NKV
        raw = sb("raw_qkv", [P, NR, HID])
        hl = sb("hl_qkv", [P, 2, NR, HID], F16)
        raw_o = sb("raw_wo", [P, DK, AQ])
        kw = sb("kw", [P, AH])
        w_in, small_in, hi_done, lo_done, pe_done, read = (sem(n) for n in ("a_w_in", "a_small_in", "a_hi", "a_lo", "a_pe", "a_read"))
        o_in = sem("a_o_in")
        link = sem("a_link")
        block = ctx.enter_context(nc.Block())
        NO = AP2 * AG

        @block.sync
        def _(sp):
            for name, at, n in (("Wq", 0, NQ), ("Wk", NQ, NKV), ("Wv", NQ + NKV, NKV)):
                sp.dma_start(raw[:, at:at + n, :], io["a_" + name].rearrange("(c p) n -> p c n", p=P)).then_inc(w_in, 16)
            for name, at, n in (("bq", 0, AQ), ("bk", AQ, AK), ("bv", AQ + AK, AK)):
                sp.dma_start(w["b"][:, at:at + n], spread(io["a_" + name])).then_inc(small_in, 16)
            sp.dma_start(w["bo"][:], spread(io["a_bo"])).then_inc(small_in, 16)
            sp.dma_start(kw[:], spread(io["a_kw"])).then_inc(small_in, 16)
            for b in range(BT):
                for n in range(2):
                    for half in range(2):
                        sp.dma_start(w["rot"][b * S:(b + 1) * S, n, half, :], io["rope"][n]).then_inc(small_in, 16)
            wo = io["a_Wo"].rearrange("(c p) (k e g d) -> c k p e g d", p=P, k=AP2, e=2, g=AG)
            for c in range(DK):
                for k in range(AP2):
                    for e in range(2):
                        dst = raw_o[:, c, k * 2 * AG * AD:(k + 1) * 2 * AG * AD].rearrange("p (g e d) -> p e g d", g=AG, e=2)
                        sp.dma_start(dst[:, e], wo[c, k, :, e]).then_inc(o_in, 16)

        @block.scalar
        def _(act):
            act.wait_ge(w_in, 48)
            act.activation(hl[:, 0], raw[:], ACT.Copy, scale=WS).then_inc(hi_done, 1)
            act.wait_ge(o_in, 16 * DK * AP2 * 2)
            act.wait_ge(pe_done, NR)
            act.activation(hl[:, 0, 0:NQ, :].rearrange("p c n -> p (c n)"), raw_o[:].rearrange("p c n -> p (c n)"), ACT.Copy, scale=WS).then_inc(hi_done, 1)

        @block.gpsimd
        def _(pool):
            pool.memset(w["causal"][:], 0.0).then_inc(link, 1)
            for n in range(BT * AG // AG):
                pool.wait_ge(link, n + 1)
                part = w["causal"][n * S:(n + 1) * S, :]
                pool.affine_select(out=part, in_=part, compare_op=ALU.is_ge, fill=-1e30, base=0, pattern=[[-1, S]],
                                   channel_multiplier=1).then_inc(link, 1)

        @block.vector
        def _(dve):
            dve.wait_ge(hi_done, 1)
            dve.scalar_tensor_tensor(out=hl[:, 1], in0=raw[:], scalar=WS, in1=hl[:, 0], op0=ALU.mult, op1=ALU.subtract).then_inc(lo_done, 1)
            dve.wait_ge(small_in, 16 * (5 + BT * 4))
            dve.tensor_scalar(w["rot"][:, 1, 0, :], w["rot"][:, 1, 0, :], -1.0, None, ALU.mult).then_inc(lo_done, 1)
            dve.wait_ge(lo_done, 2)
            for n in range(2):
                dve.tensor_tensor(w["rot_q"][:, n], w["rot"][:, n].rearrange("p a f -> p (a f)").unsqueeze(1).broadcast_to([P, AH, AD]),
                                  kw[:].unsqueeze(2).broadcast_to([P, AH, AD]), ALU.mult)
            for r in range(NR):
                dve.wait_ge(pe_done, r + 1)
                dve.tensor_copy(w["Wqkv"][:, :, :, r * P:(r + 1) * P], pst[r % 2][:].rearrange("p (l c n) -> p l c n", l=2, c=DK)).then_inc(read, 1)
            dve.wait_ge(hi_done, 2)
            dve.scalar_tensor_tensor(out=hl[:, 1, 0:NQ, :].rearrange("p c n -> p (c n)"), in0=raw_o[:].rearrange("p c n -> p (c n)"), scalar=WS,
                                     in1=hl[:, 0, 0:NQ, :].rearrange("p c n -> p (c n)"), op0=ALU.mult, op1=ALU.subtract).then_inc(lo_done, 1)
            for r in range(NO):
                dve.wait_ge(pe_done, NR + r + 1)
                dve.tensor_copy(w["Wo"][:, :, r, :].rearrange("p l (c n) -> p l c n", c=DK),
                                pst[(NR + r) % 2][:].rearrange("p (l c n) -> p l c n", l=2, c=DK)).then_inc(read, 1)

        @block.tensor
        def _(pe):
            pe.wait_ge(lo_done, 1)
            for r in range(NR):
                wait(pe, read, r - 1)
                for l in range(2):
                    for c in range(DK):
                        ins = pe.transpose(pst[r % 2][:, (l * DK + c) * P:(l * DK + c + 1) * P], hl[:, l, r, c * P:(c + 1) * P], w["ident"][:])
                ins.then_inc(pe_done, 1)
            pe.wait_ge(lo_done, 3)
            wo = hl[:, :, 0:NQ, :].rearrange("p l c n -> p l (c n)").rearrange("p l (c r m) -> p l c r m", c=DK, r=NO)
            for r in range(NO):
                wait(pe, read, NR + r - 1)
                for l in range(2):
                    for c in range(DK):
                        ins = pe.transpose(pst[(NR + r) % 2][:, (l * DK + c) * P:(l * DK + c + 1) * P], wo[:, l, c, r, :], w["ident"][:])
                ins.then_inc(pe_done, 1)


def self_weights(nc, ctx):
    sb = lambda name, shape, dt=F32: ctx.enter_context(nc.sbuf_tensor(name, shape, dt))
    return {
        "Wqkv": sb("a_wqkv", [P, 2, DK, AQKV], F16), "Wo": sb("a_wo", [P, 2, AP2 * AG, HID], F16), "b": sb("a_b", [P, AQKV]),
        "bo": sb("a_bo", [P, HID]), "rot": sb("a_rot", [P, 2, 2, ROT]), "rot_q": sb("a_rot_q", [P, 2, AH, AD]),
        "causal": sb("a_causal", [P, S]), 
        "v_rows": [nc.dram_tensor(f"v_rows{n}", [2, BT, S, AK], F16, kind="Internal").ap() for n in range(1)],
    }


def self_attention(nc, io, sb_x, w, tiles):
    with ExitStack() as ctx:
        sb = lambda name, shape, dt=F32: ctx.enter_context(nc.sbuf_tensor(name, shape, dt))
        sem = lambda name: ctx.enter_context(nc.semaphore(name))
        bank_t = [ctx.enter_context(nc.psum_tensor(f"a_turn{n}", [P, 1024], F16)) for n in range(2)]
        bank_m = [ctx.enter_context(nc.psum_tensor(f"a_proj{n}", [P, 512], F32)) for n in range(2)]
        bank_s = ctx.enter_context(nc.psum_tensor("a_score", [P, AKV, BT, S], F32))
        bank_o = [ctx.enter_context(nc.psum_tensor(f"a_sum{n}", [P, BT, AG * S], F32)) for n in range(2)]
        n_st, n_ag, n_r = sb("a_st", [P, 6]), sb("a_ag", [P, 2]), sb("a_r", [P, 2])
        n_x, n_hl = sb("a_n", [P, HID]), sb("a_nhl", [P, 2, HID], F16)
        nT = sb("a_nT", [P, 2, DK, P], F16)
        qk = sb("a_qk", [P, AH + AKV, 2, ROT])
        qk_c = sb("a_qkc", [P, AH + AKV, 2, ROT])
        qk_s = sb("a_qks", [P, AH + AKV, 2, ROT])
        q_hl = sb("a_qhl", [P, AH, 2, AD], F16)
        k_hl = sb("a_khl", [P, AKV, 2, 2, AD], F16)
        v_f = sb("a_vf", [P, AK])
        v_hl = sb("a_vhl", [P, 2, AK], F16)
        v4 = [sb(f"a_v4{n}", [P, BT, AK], F16) for n in range(1)]
        qT = sb("a_qT", [P, AKV, BT, AG, S], F16)
        kT = sb("a_kT", [P, 2, AKV, P], F16)
        s_f = sb("a_s", [P, AKV * BT, S])
        s_max, p_sum, p_inv, p_scl = (sb(n, [P, AKV * BT]) for n in ("a_smax", "a_psum", "a_pinv", "a_pscl"))
        p4 = sb("a_p4", [P, AKV * BT, PARTS, S], F16)
        pT = sb("a_pT", [P, AKV, BT, AG * S], F16)
        oT = sb("a_oT", [P, 2, AP2, AG, BT, S], F16)

        t_fill, t_read, m_fill, m_read, s_fill, s_read, o_fill, o_read = (
            sem("a_" + n) for n in ("t_fill", "t_read", "m_fill", "m_read", "s_fill", "s_read", "o_fill", "o_read"))
        v_saved, v_here = sem("a_v_saved"), sem("a_v_here")
        n_hi, q_hi, v_hi, exp_done, p_hi, o_hi = (sem("a_" + n) for n in ("n_hi", "q_hi", "v_hi", "exp_done", "p_hi", "o_hi"))
        n_rs, n_lo, q_lo, c_done, p_nd, p_lo = (sem("a_" + n) for n in ("n_rs", "n_lo", "q_lo", "c_done", "p_nd", "p_lo"))
        n_msd, n_xd, v_lo, rot_done, s_maxd, s_sub, p_invd, x_out = (
            sem("a_" + n) for n in ("n_msd", "n_xd", "v_lo", "rot_done", "s_maxd", "s_sub", "p_invd", "x_out"))
        link_n, link_r, link_p, link_i = (sem("a_" + n) for n in ("link_n", "link_r", "link_p", "link_i"))
        has = lambda t: not isinstance(t, int) or 0 <= t < tiles

        def order_t(t, i):
            out = ["X"] if has(t + 1) else [None]
            out += [f"Q{n}" for n in range(4)] + ["K0", "K1"] if has(t) else [None] * 6
            out += [f"P{n}" for n in range(4)] if has(t - 1) else [None] * 4
            return out + [None]

        def order_m(t, i):
            return ([f"M{n}" for n in range(6)] if has(t + 1) else [None] * 6) + (["W"] if has(t - 1) else [None]) + [None]

        passed_dve, passed_pool, passed_sp = (sem(n) for n in ("a_passed_dve", "a_passed_pool", "a_passed_sp"))
        turns, projs = Ring(order_t, tiles, 1, 2, 2), Ring(order_m, tiles, 1, 2, 2)
        block = ctx.enter_context(nc.Block())

        def over_tiles(eng, tile):
            for t in (-2, -1, 0, 1):
                tile(t)
            with eng.Fori(2, tiles - 2) as t:
                tile(t)
            for t in (tiles - 2, tiles - 1, tiles):
                tile(t)

        @block.sync
        def _(sp):
            def tile(t):
                if has(t + 1):
                    sp.wait_ge(v_lo, t + 2)
                    wait(sp, v_here, 16 * PARTS * (t + 1))
                    sp.dma_start(w["v_rows"][0].rearrange("l b s n -> (b s) l n"), v_hl[:]).then_inc(v_saved, 16)
                    wait_apart(sp, v_saved, 16 * (t + 2), passed_sp)
                    wait(sp, o_fill, AP2 * (t + 1))
                    for r, part in enumerate((0, 0, 1, 1)):
                        sp.dma_start(v4[0][r * S:(r + 1) * S], w["v_rows"][0][part].rearrange("b s n -> s b n")).then_inc(v_here, 16)
            over_tiles(sp, tile)

        @block.gpsimd
        def _(pool):
            def tile(t):
                if has(t + 2):
                    pool.wait_ge(n_msd, t + 3)
                    wait(pool, n_xd, t + 2)
                    pool.tensor_tensor(n_r[:, 0:1], n_r[:, 1:2], w["minus_half"][:, 0:1], ALU.pow).then_inc(n_rs, 1)
                    pool.wait_ge(n_hi, t + 3)
                    wait(pool, t_fill, turns.use(t, 0, "X")[1] if has(t + 1) else 0)
                    pool.tensor_tensor(n_hl[:, 1], n_x[:], n_hl[:, 0], ALU.subtract).then_inc(n_lo, 1)
                if has(t):
                    pool.wait_ge(p_invd, t + 1)
                    pool.tensor_tensor(s_f[:], s_f[:], p_scl[:].unsqueeze(2).broadcast_to([P, AKV * BT, S]), ALU.mult).then_inc(p_nd, 1)
                    pool.wait_ge(p_hi, 2 * t + 2)
                    pool.tensor_tensor(p4[:, :, 1, :], s_f[:], p4[:, :, 0, :], ALU.subtract).then_inc(p_lo, 1)
                    wait_apart(pool, p_lo, 2 * t + 1, passed_pool)
                    pool.tensor_copy(p4[:, :, 3, :], p4[:, :, 1, :]).then_inc(p_lo, 1)
                if has(t + 1):
                    pool.wait_ge(m_read, projs.use(t, 0, "M3")[1])
                    wait(pool, q_lo, t + 1)
                    pool.tensor_tensor(qk_c[:, 0:AH].rearrange("p h a f -> p h (a f)"), qk[:, 0:AH].rearrange("p h a f -> p h (a f)"),
                                       w["rot_q"][:, 0], ALU.mult).then_inc(c_done, 1)
            over_tiles(pool, tile)

        @block.scalar
        def _(act):
            def tile(t):
                if has(t + 2):
                    act.wait_ge(n_xd, t + 3)
                    wait(act, t_fill, turns.use(t, 0, "X")[1] if has(t + 1) else 0)
                    act.activation(n_hl[:, 0], n_x[:], ACT.Copy).then_inc(n_hi, 1)
                if has(t):
                    act.wait_ge(s_sub, t + 1)
                    act.activation(s_f[:], s_f[:], ACT.Exp).then_inc(exp_done, 1)
                if has(t + 1):
                    act.wait_ge(m_read, projs.use(t, 0, "M5")[1])
                    wait(act, v_saved, 16 * (t + 1))
                    act.activation(v_hl[:, 0], v_f[:], ACT.Copy).then_inc(v_hi, 1)
                if has(t):
                    act.wait_ge(p_nd, t + 1)
                    wait(act, t_fill, turns.use(t, 0, "P3")[1] if has(t - 1) else 0)
                    for part in (0, 2):
                        act.activation(p4[:, :, part, :], s_f[:], ACT.Copy).then_inc(p_hi, 1)
                if has(t - 1):
                    for n in range(AP2):
                        act.wait_ge(o_fill, AP2 * (t - 1) + n + 1)
                        if has(t - 2):
                            act.wait_ge(m_fill, projs.use(t - 1, 0, "W")[1])
                        act.activation(oT[:, 0, n], bank_o[n % 2][:].rearrange("p b (g s) -> p g b s", g=AG), ACT.Copy, scale=1 / PS
                                       ).then_inc(o_hi, 1)
                if has(t + 1):
                    act.wait_ge(rot_done, t + 2)
                    act.activation(q_hl[:, :, 0, :], qk_c[:, 0:AH].rearrange("p h a f -> p h (a f)"), ACT.Copy).then_inc(q_hi, 1)
                    for n in range(2):
                        act.activation(k_hl[:, :, 0, n, :], qk_c[:, AH:].rearrange("p h a f -> p h (a f)"), ACT.Copy).then_inc(q_hi, 1)
            over_tiles(act, tile)

        @block.vector
        def _(dve):
            def read_turned(t, name, out):
                bank, n, _ = turns.use(t, 0, name)
                dve.wait_ge(t_fill, n)
                dve.tensor_copy(out, bank_t[bank][:, 0:out.shape[1]]).then_inc(t_read, 1)

            def tile(t):
                if has(t + 2):
                    x_t = sb_x[:, bass.ds(t + 2, 1), :].rearrange("p o n -> p (o n)")
                    dve.bn_stats(n_st[:], x_t).then_inc(link_n, 1)
                    wait_apart(dve, link_n, 2 * (t + 2) + 1, passed_dve)
                    dve.bn_aggr(n_ag[:], n_st[:]).then_inc(link_n, 1)
                    dve.wait_ge(link_n, 2 * (t + 2) + 2)
                    wait(dve, n_rs, t + 2)
                    dve.tensor_scalar(n_r[:, 1:2], n_ag[:, 1:2], 1e-5, None, ALU.add).then_inc(n_msd, 1)
                if has(t + 1):
                    read_turned(t, "X", nT[:].rearrange("p l d n -> p (l d n)"))
                if has(t):
                    for k in range(4):
                        bank, n, _ = turns.use(t, 0, f"Q{k}")
                        dve.wait_ge(t_fill, n)
                        src = bank_t[bank][:].rearrange("p (k g b s) -> p k b g s", k=2, g=AG, b=BT)
                        dve.tensor_copy(qT[:, 2 * k], src[:, 0])
                        dve.tensor_copy(qT[:, 2 * k + 1], src[:, 1]).then_inc(t_read, 1)
                    for n in range(2):
                        read_turned(t, f"K{n}", kT[:, n].rearrange("p k n -> p (k n)"))
                if has(t + 2):
                    dve.wait_ge(n_rs, t + 3)
                    wait(dve, n_lo, t + 2)
                    dve.tensor_scalar(n_x[:], x_t, n_ag[:, 0:1], n_r[:, 0:1], ALU.subtract, ALU.mult).then_inc(n_xd, 1)
                if has(t):
                    wait(dve, p_lo, 2 * t)
                    dve.wait_ge(s_fill, t + 1)
                    dve.scalar_tensor_tensor(out=s_f[:], in0=bank_s[:].rearrange("p k b s -> p (k b) s"), scalar=AD ** -0.5,
                                             in1=w["causal"][:].unsqueeze(1).broadcast_to([P, AKV * BT, S]),
                                             op0=ALU.mult, op1=ALU.add).then_inc(s_read, 1)
                    dve.wait_ge(s_read, t + 1)
                    dve.tensor_reduce(s_max[:], s_f[:], AX.X, ALU.max).then_inc(s_maxd, 1)
                    dve.wait_ge(s_maxd, t + 1)
                    dve.tensor_tensor(s_f[:], s_f[:], s_max[:].unsqueeze(2).broadcast_to([P, AKV * BT, S]), ALU.subtract).then_inc(s_sub, 1)
                if has(t - 1):
                    for n in range(4):
                        read_turned(t, f"P{n}", pT[:, 2 * n:2 * n + 2].rearrange("p k b n -> p (k b n)"))
                if has(t):
                    dve.wait_ge(exp_done, t + 1)
                    dve.tensor_reduce(p_sum[:], s_f[:], AX.X, ALU.add).then_inc(link_p, 1)
                    dve.wait_ge(link_p, t + 1)
                    dve.reciprocal(p_inv[:], p_sum[:]).then_inc(link_r, 1)
                    dve.wait_ge(link_r, t + 1)
                    wait(dve, p_nd, t)
                    dve.tensor_scalar(p_scl[:], p_inv[:], PS, None, ALU.mult).then_inc(p_invd, 1)
                if has(t + 1):
                    wait(dve, rot_done, t + 1)
                    wait(dve, c_done, t + 1)
                    for c in range(6):
                        bank, n, _ = projs.use(t, 0, f"M{c}")
                        dve.wait_ge(m_fill, n)
                        if c == 5:
                            wait(dve, v_lo, t + 1)
                            wait(dve, v_hi, t + 1)
                        out = qk[:].rearrange("p h a f -> p (h a f)")[:, 512 * c:512 * (c + 1)] if c < 5 else v_f[:]
                        dve.scalar_tensor_tensor(out=out, in0=bank_m[bank][:], scalar=1 / WS, in1=w["b"][:, 512 * c:512 * (c + 1)],
                                                 op0=ALU.mult, op1=ALU.add).then_inc(m_read, 1)
                    dve.wait_ge(v_hi, t + 2)
                    wait(dve, v_saved, 16 * (t + 1))
                    dve.tensor_tensor(v_hl[:, 1], v_f[:], v_hl[:, 0], ALU.subtract).then_inc(v_lo, 1)
                    dve.wait_ge(m_read, projs.use(t, 0, "M4")[1])
                    for half in range(2):
                        dve.tensor_tensor(qk_s[:, 0:AH, half, :], qk[:, 0:AH, 1 - half, :], w["rot_q"][:, 1, :, half * ROT:(half + 1) * ROT], ALU.mult)
                        dve.tensor_tensor(qk_s[:, AH:, half, :], qk[:, AH:, 1 - half, :],
                                          w["rot"][:, 1, half, :].unsqueeze(1).broadcast_to([P, AKV, ROT]), ALU.mult)
                    wait(dve, q_lo, t + 1)
                    dve.tensor_tensor(qk_c[:, AH:].rearrange("p h a f -> p h (a f)"), qk[:, AH:].rearrange("p h a f -> p h (a f)"),
                                      w["rot"][:, 0].rearrange("p a f -> p (a f)").unsqueeze(1).broadcast_to([P, AKV, AD]), ALU.mult).then_inc(link_i, 1)
                    dve.wait_ge(link_i, t + 2)
                    dve.wait_ge(c_done, t + 2)
                    dve.tensor_tensor(qk_c[:].rearrange("p h a f -> p (h a f)"), qk_c[:].rearrange("p h a f -> p (h a f)"),
                                      qk_s[:].rearrange("p h a f -> p (h a f)"), ALU.add).then_inc(rot_done, 1)
                if has(t - 1):
                    for n in range(AP2):
                        dve.wait_ge(o_hi, AP2 * (t - 1) + n + 1)
                        for g in range(AG):
                            ins = dve.scalar_tensor_tensor(out=oT[:, 1, n, g], in0=bank_o[n % 2][:, :, g * S:(g + 1) * S], scalar=1 / PS,
                                                           in1=oT[:, 0, n, g], op0=ALU.mult, op1=ALU.subtract)
                        ins.then_inc(o_read, 1)
                if has(t + 1):
                    dve.wait_ge(q_hi, 3 * (t + 2))
                    q_r = qk_c[:].rearrange("p h a f -> p h (a f)")
                    dve.tensor_tensor(q_hl[:, :, 1, :], q_r[:, 0:AH], q_hl[:, :, 0, :], ALU.subtract)
                    dve.tensor_tensor(k_hl[:, :, 1, 0, :], q_r[:, AH:], k_hl[:, :, 0, 0, :], ALU.subtract)
                    dve.tensor_tensor(k_hl[:, :, 1, 1, :], q_r[:, AH:], k_hl[:, :, 0, 0, :], ALU.subtract).then_inc(q_lo, 1)
                if has(t - 1):
                    bank, n, _ = projs.use(t, 0, "W")
                    dve.wait_ge(m_fill, n)
                    x_t = sb_x[:, bass.ds(t - 1, 1), :].rearrange("p o n -> p (o n)")
                    dve.scalar_tensor_tensor(out=x_t, in0=bank_m[bank][:, 0:HID], scalar=1 / WS, in1=x_t,
                                             op0=ALU.mult, op1=ALU.add).then_inc(m_read, 1)
                    dve.wait_ge(m_read, n)
                    dve.tensor_tensor(x_t, x_t, w["bo"][:], ALU.add).then_inc(x_out, 1)
            over_tiles(dve, tile)

        @block.tensor
        def _(pe):
            ident = w["ident"]

            def take(ring, t, name, read):
                bank, n, before = ring.use(t, 0, name)
                wait(pe, read, before)
                return bank

            def turn(t, name, parts):
                out = bank_t[take(turns, t, name, t_read)]
                for n, part in enumerate(parts):
                    ins = pe.transpose(out[:, n * P:(n + 1) * P], part, ident[:])
                ins.then_inc(t_fill, 1)

            def project(t, name, terms):
                out = bank_m[take(projs, t, name, m_read)]
                for n, (a, b) in enumerate(terms):
                    ins = pe.matmul(out[:, 0:b.shape[-1]], a, b, start=(n == 0), stop=(n == len(terms) - 1))
                ins.then_inc(m_fill, 1)

            def tile(t):
                if has(t + 1):
                    pe.wait_ge(n_lo, t + 2)
                    turn(t, "X", [n_hl[:, l, d * P:(d + 1) * P] for l in range(2) for d in range(DK)])
                if has(t):
                    pe.wait_ge(q_lo, t + 1)
                    for n in range(4):
                        turn(t, f"Q{n}", [q_hl[:, h].rearrange("p l d -> p (l d)") for h in range(8 * n, 8 * n + 8)])
                    for n in range(2):
                        turn(t, f"K{n}", [k_hl[:, k, n].rearrange("p l d -> p (l d)") for k in range(AKV)])
                    pe.wait_ge(t_read, turns.use(t, 0, "K1")[1])
                    wait(pe, s_read, t)
                    for k in range(AKV):
                        for b in range(BT):
                            for n in range(2):
                                ins = pe.matmul(bank_s[:, k, b, :], qT[:, k, b].rearrange("p g s -> p (g s)"), kT[:, n, k, b * S:(b + 1) * S],
                                                start=(n == 0), stop=(n == 1))
                    ins.then_inc(s_fill, 1)
                if has(t - 1):
                    pe.wait_ge(p_lo, 2 * t)
                    for n in range(4):
                        turn(t, f"P{n}", [p4[:, k * BT + b].rearrange("p r s -> p (r s)") for k in (2 * n, 2 * n + 1) for b in range(BT)])
                if has(t + 1):
                    pe.wait_ge(t_read, turns.use(t, 0, "X")[1])
                    for c in range(6):
                        project(t, f"M{c}", [(nT[:, a, d, :], w["Wqkv"][:, b, d, 512 * c:512 * (c + 1)])
                                             for d in range(DK) for a, b in ((0, 0), (1, 0), (0, 1))])
                if has(t - 1):
                    pe.wait_ge(v_here, 16 * PARTS * t)
                    pe.wait_ge(t_read, turns.use(t, 0, "P3")[1])
                    for n in range(AP2):
                        wait(pe, o_read, AP2 * (t - 1) + n - 1)
                        for e in range(2):
                            k = 2 * n + e
                            for b in range(BT):
                                ins = pe.matmul(bank_o[n % 2][e * AD:(e + 1) * AD, b, :], v4[0][:, b, k * AD:(k + 1) * AD], pT[:, k, b, :],
                                                start=True, stop=True)
                        ins.then_inc(o_fill, 1)
                    pe.wait_ge(o_read, AP2 * t)
                    project(t, "W", [(oT[:, a, n, g].rearrange("p b s -> p (b s)"), w["Wo"][:, b, n * AG + g, :])
                                     for n in range(AP2) for g in range(AG) for a, b in ((0, 0), (1, 0), (0, 1))])
            over_tiles(pe, tile)


FF, NE, ER = 704, 8, 16
FC = -(-FF // P)
ERS = NE * ER
SCALING = 2.0
TOP = 2
EPB = 4
LR = 32
STACK = 3 * 2 * ER
TB = 4
NB = TB * P


def rows_of(f):
    return min(P, FF - f * P)


def ffn_weights(nc, ctx, tiles):
    sb = lambda name, shape, dt=F32: ctx.enter_context(nc.sbuf_tensor(name, shape, dt))
    dram = lambda name, shape, dt: nc.dram_tensor(name, shape, dt, kind="Internal").ap()
    return {
        "Wgu": sb("f_wgu", [P, 2, DK, 2, FF], F16), "B": sb("f_B", [STACK, 2, NE, FF], F16), "WdT": sb("f_WdT", [P, FC, HID]),
        "AdT": sb("f_AdT", [P, FC, NE, LR]), "BdT": sb("f_BdT", [P, 2, 2, HID], F16),
        "nT": sb("f_nT", [P, 2, DK, tiles * P], F16), "weT": sb("f_weT", [P, 2, tiles * P]),
        "b_rows": dram("b_rows", [2, 2, 2, ER + ERS, FF], F16), "a_rows": dram("a_rows", [2, 2, ER + ERS, tiles * P], F16),
    }


def prepare_ffn(nc, io, w, tiles):
    with ExitStack() as ctx:
        sb = lambda name, shape, dt=F32: ctx.enter_context(nc.sbuf_tensor(name, shape, dt))
        sem = lambda name: ctx.enter_context(nc.semaphore(name))
        bank = [ctx.enter_context(nc.psum_tensor(f"p2_t{n}", [P, 1024], F16)) for n in range(2)]
        bank_f = [ctx.enter_context(nc.psum_tensor(f"p2_f{n}", [P, 512], F32)) for n in range(2)]
        raw = sb("raw_gu", [P, 2, FC, HID])
        hl = sb("hl_gu", [P, 2, 2, FC, HID], F16)
        raw_b = sb("raw_b", [P, 2, FC, NE, ER])
        hl_b = sb("hl_b", [P, 2, 2, FC, ERS], F16)
        bT = sb("bT", [P, 2, 2, 2, FF], F16)
        raw_bd = sb("raw_bd", [P, DK, NE, LR])
        hl_bd = sb("hl_bd", [P, 2, DK, NE * LR], F16)
        raw_d = sb("raw_d", [P, DK, FF])
        raw_ad = sb("raw_ad", [ERS, FF])
        ident32 = sb("ident32", [P, P])
        zero = w["nT"][0:ER, 0, 0, :]
        loads, hi, lo, fill, read, fill_f, read_f, saved, stacked, setup = (
            sem("f0_" + n) for n in ("loads", "hi", "lo", "fill", "read", "fill_f", "read_f", "saved", "stacked", "setup"))
        block = ctx.enter_context(nc.Block())

        @block.sync
        def _(sp):
            sp.wait_ge(setup, 2)

            def load(dst, src):
                sp.dma_start(dst, src).then_inc(loads, 16)

            full = FF // P
            for v, name in enumerate(("f_Wg", "f_Wu")):
                load(raw[:, v, 0:full, :], io[name][0:full * P].rearrange("(c p) n -> p c n", p=P))
                load(raw[0:FF - full * P, v, full, :], io[name][full * P:FF])
            for v, name in enumerate(("f_Bg", "f_Bu")):
                for e in range(NE):
                    load(raw_b[:, v, 0:full, e, :], io[name][e, 0:full * P].rearrange("(c p) r -> p c r", p=P))
                    load(raw_b[0:FF - full * P, v, full, e, :], io[name][e, full * P:FF])
            for e in range(NE):
                load(raw_bd[:, :, e, 0:ER], io["f_Bd"][e].rearrange("(c p) r -> p c r", p=P))
            load(raw_d[:], io["f_Wd"].rearrange("(c p) n -> p c n", p=P))
            load(raw_ad[:], io["f_Ad"].rearrange("e r n -> (e r) n"))
            for v in range(2):
                for a in range(2):
                    sp.dma_start(w["a_rows"][v, a, 0:ER, :], zero[:, 0:tiles * P]).then_inc(saved, 16)
                    for b in range(2):
                        sp.dma_start(w["b_rows"][v, a, b, 0:ER, :], zero[:, 0:FF]).then_inc(saved, 16)
            sp.wait_ge(read, 4 * FC)
            for v in range(2):
                for a in range(2):
                    sp.dma_start(w["b_rows"][v, a, :, ER:].rearrange("l r n -> r l n"), bT[:, v, a]).then_inc(saved, 16)
            sp.wait_ge(saved, 16 * 16)
            for v in range(2):
                for r, part in enumerate((0, 0, 1)):
                    for a, first in ((1, 0), (0, ER)):
                        at = r * 2 * ER + (0 if a else ER)
                        sp.dma_start(w["B"][at:at + ER, v], w["b_rows"][v, a, part, first:first + ERS].rearrange("(e r) n -> r e n", r=ER)
                                     ).then_inc(stacked, 16)
            sp.wait_ge(stacked, 16 * 12)

        total = 16 * (4 + 4 * NE + NE + 2)

        @block.gpsimd
        def _(pool):
            pool.memset(raw_bd[:], 0.0).then_inc(setup, 1)
            pool.memset(zero, 0.0).then_inc(setup, 1)
            pool.memset(ident32[:], 0.0).then_inc(setup, 1)
            pool.wait_ge(setup, 3)
            pool.affine_select(out=ident32[:], in_=ident32[:], compare_op=ALU.not_equal, fill=1.0, base=0,
                               pattern=[[-1, P]], channel_multiplier=1).then_inc(setup, 1)
            pool.memset(w["AdT"][:], 0.0).then_inc(setup, 1)

        full, rest = FF // P, FF - FF // P * P

        @block.scalar
        def _(act):
            act.wait_ge(loads, total)
            act.activation(hl[:, 0, :, 0:full], raw[:, :, 0:full], ACT.Copy, scale=WS)
            act.activation(hl[0:rest, 0, :, full], raw[0:rest, :, full], ACT.Copy, scale=WS).then_inc(hi, 1)
            act.activation(hl_b[:, 0, :, 0:full], raw_b[:, :, 0:full].rearrange("p v c e r -> p v c (e r)"), ACT.Copy, scale=WS * SCALING)
            act.activation(hl_b[0:rest, 0, :, full], raw_b[0:rest, :, full].rearrange("p v e r -> p v (e r)"), ACT.Copy, scale=WS * SCALING).then_inc(hi, 1)
            act.activation(hl_bd[:, 0].rearrange("p c n -> p (c n)"), raw_bd[:].rearrange("p c e r -> p (c e r)"), ACT.Copy, scale=SCALING).then_inc(hi, 1)

        @block.vector
        def _(dve):
            dve.wait_ge(hi, 3)
            for v in range(2):
                for p, a, b in ((P, 0, full), (rest, full, FC)):
                    dve.scalar_tensor_tensor(out=hl[0:p, 1, v, a:b], in0=raw[0:p, v, a:b], scalar=WS, in1=hl[0:p, 0, v, a:b],
                                             op0=ALU.mult, op1=ALU.subtract)
                    dve.scalar_tensor_tensor(out=hl_b[0:p, 1, v, a:b], in0=raw_b[0:p, v, a:b].rearrange("p c e r -> p c (e r)"),
                                             scalar=WS * SCALING, in1=hl_b[0:p, 0, v, a:b], op0=ALU.mult, op1=ALU.subtract)
            dve.scalar_tensor_tensor(out=hl_bd[:, 1].rearrange("p c n -> p (c n)"), in0=raw_bd[:].rearrange("p c e r -> p (c e r)"),
                                     scalar=SCALING, in1=hl_bd[:, 0].rearrange("p c n -> p (c n)"), op0=ALU.mult, op1=ALU.subtract).then_inc(lo, 1)
            n = 0
            for v in range(2):
                for f in range(FC):
                    m = rows_of(f)
                    dve.wait_ge(fill, n + 1)
                    src = bank[n % 2][:, 0:2 * DK * m].rearrange("p (l c n) -> p l c n", l=2, c=DK)
                    dve.tensor_copy(w["Wgu"][:, :, :, v, f * P:f * P + m], src).then_inc(read, 1)
                    n += 1
            for v in range(2):
                for f in range(FC):
                    m = rows_of(f)
                    dve.wait_ge(fill, n + 1)
                    src = bank[n % 2][:, 0:2 * m].rearrange("p (l n) -> p l n", l=2)
                    dve.tensor_copy(bT[:, v, 0, :, f * P:f * P + m], src)
                    ins = dve.tensor_scalar(bT[:, v, 1, :, f * P:f * P + m], src, -1.0, None, ALU.mult)
                    ins.then_inc(read, 1)
                    n += 1
            dve.wait_ge(fill, n + 1)
            dve.tensor_copy(w["BdT"][:].rearrange("p l b n -> p (l b n)"), bank[n % 2][:]).then_inc(read, 1)
            dve.wait_ge(setup, 5)
            for f in range(FC):
                m = rows_of(f)
                dve.wait_ge(fill_f, f + 1)
                b = bank_f[f % 2]
                dve.tensor_scalar(w["WdT"][0:m, f, :], b[0:m, 0:HID], WS, None, ALU.mult)
                dve.tensor_scalar(w["AdT"][0:m, f, :, 0:ER], b[0:m, HID:HID + ERS].rearrange("p (e r) -> p e r", e=NE), WS, None,
                                  ALU.mult).then_inc(read_f, 1)
        @block.tensor
        def _(pe):
            ident = w["ident"]
            pe.wait_ge(lo, 1)
            pe.wait_ge(setup, 4)
            n = 0
            for v in range(2):
                for f in range(FC):
                    m = rows_of(f)
                    wait(pe, read, n - 1)
                    for l in range(2):
                        for c in range(DK):
                            ins = pe.transpose(bank[n % 2][:, (l * DK + c) * m:(l * DK + c + 1) * m], hl[0:m, l, v, f, c * P:(c + 1) * P], ident[0:m, 0:m])
                    ins.then_inc(fill, 1)
                    n += 1
            for v in range(2):
                for f in range(FC):
                    m = rows_of(f)
                    wait(pe, read, n - 1)
                    for l in range(2):
                        ins = pe.transpose(bank[n % 2][:, l * m:(l + 1) * m], hl_b[0:m, l, v, f, :], ident[0:m, 0:m])
                    ins.then_inc(fill, 1)
                    n += 1
            wait(pe, read, n - 1)
            for l in range(2):
                for b in range(2):
                    for c in range(DK):
                        at = (l * 2 + b) * HID + c * P
                        ins = pe.transpose(bank[n % 2][:, at:at + P], hl_bd[:, l, c, b * P:(b + 1) * P], ident[:])
            ins.then_inc(fill, 1)
            for f in range(FC):
                m = rows_of(f)
                wait(pe, read_f, f - 1)
                b = bank_f[f % 2]
                for c in range(DK):
                    pe.transpose(b[0:m, c * P:(c + 1) * P], raw_d[:, c, f * P:f * P + m], ident32[:])
                pe.transpose(b[0:m, HID:HID + ERS], raw_ad[:, f * P:f * P + m], ident32[:]).then_inc(fill_f, 1)


def route(nc, io, sb_x, w, tiles):
    with ExitStack() as ctx:
        sb = lambda name, shape, dt=F32: ctx.enter_context(nc.sbuf_tensor(name, shape, dt))
        sem = lambda name: ctx.enter_context(nc.semaphore("r_" + name))
        bank_w = ctx.enter_context(nc.psum_tensor("r_w", [P, 1024], F16))
        bank_t = [ctx.enter_context(nc.psum_tensor(f"r_t{n}", [P, 2 * DK * P], F16)) for n in range(2)]
        bank_l = ctx.enter_context(nc.psum_tensor("r_l", [P, TB, NE], F32))
        bank_a = [ctx.enter_context(nc.psum_tensor(f"r_a{n}", [P, NB], F32)) for n in range(2)]
        bank_e = ctx.enter_context(nc.psum_tensor("r_e", [P, 2, P], F32))
        raw_a = sb("r_raw", [P, 2, HID])
        hl_a = sb("r_hl", [P, 2, 2, HID], F16)
        aT = sb("r_aT", [P, 2, 2, DK, P], F16)
        wr = sb("r_wr", [P, DK, NE])
        wr_hl = sb("r_wrhl", [P, 2, DK, NE], F16)
        st, ag, rs = sb("r_st", [P, TB, 6]), sb("r_ag", [P, TB, 2]), sb("r_rs", [P, 2, TB])
        n_x, n_hl = sb("r_nx", [P, TB, HID]), sb("r_nhl", [P, 2, TB, HID], F16)
        a_f = sb("r_af", [P, 2, NB])
        a_hl = sb("r_ahl", [P, 2, 2, NB], F16)
        logit = sb("r_logit", [P, tiles, NE])
        top = sb("r_top", [P, tiles])
        total = sb("r_total", [P, tiles])
        inv = sb("r_inv", [P, tiles])
        rank = sb("r_rank", [P, tiles, NE])
        earlier = sb("r_earlier", [P, NE, NE])
        more = sb("r_more", [P, tiles, NE, NE])
        same = sb("r_same", [P, tiles, NE, NE])
        wide = [sb(f"r_wide{n}", [P, NE, LR]) for n in range(2)]
        ident32 = sb("r_ident32", [P, P])
        loads, setup, w_hi, w_lo, w_fill, w_read = (sem(n) for n in ("loads", "setup", "w_hi", "w_lo", "w_fill", "w_read"))
        stats, agg, msd, rsd, xd, n_hi, n_lo, t_fill, t_read = (sem(n) for n in ("stats", "agg", "msd", "rsd", "xd", "n_hi", "n_lo", "t_fill", "t_read"))
        l_fill, l_read, a_fill, a_read, a_hi, a_lo, saved = (sem(n) for n in ("l_fill", "l_read", "a_fill", "a_read", "a_hi", "a_lo", "saved"))
        step, exp_d, e_fill, e_read, wide_d = (sem(n) for n in ("step", "exp_d", "e_fill", "e_read", "wide_d"))
        block = ctx.enter_context(nc.Block())
        blocks = tiles // TB
        passed_dve, passed_pe = sem("passed_dve"), sem("passed_pe")

        @block.sync
        def _(sp):
            for v, name in enumerate(("f_Ag", "f_Au")):
                sp.dma_start(raw_a[:, v, :], io[name].rearrange("e r n -> (e r) n")).then_inc(loads, 16)
            with nc.allow_non_contiguous_dma(reason="2048 elements, once"):
                for c in range(DK):
                    sp.dma_start(wr[:, c, :], io["f_Wr"][:, c * P:(c + 1) * P].rearrange("e p -> p e")).then_inc(loads, 16)

            with sp.Fori(0, blocks) as b:
                sp.wait_ge(a_lo, 2 * b + 2)
                for v in range(2):
                    sp.dma_start(w["a_rows"][v, :, ER:, bass.ds(b * NB, NB)].rearrange("l r n -> r l n"), a_hl[:, :, v, :]).then_inc(saved, 16)
            sp.wait_ge(saved, 32 * blocks)

        @block.gpsimd
        def _(pool):
            pool.memset(ident32[:], 0.0).then_inc(setup, 1)
            pool.memset(earlier[:], 1.0).then_inc(setup, 1)
            pool.wait_ge(setup, 2)
            pool.affine_select(out=ident32[:], in_=ident32[:], compare_op=ALU.not_equal, fill=1.0, base=0,
                               pattern=[[-1, P]], channel_multiplier=1).then_inc(setup, 1)
            pool.affine_select(out=earlier[:], in_=earlier[:], compare_op=ALU.is_gt, fill=0.0, base=0,
                               pattern=[[1, NE], [-1, NE]], channel_multiplier=0).then_inc(setup, 1)

            with pool.Fori(0, blocks) as b:
                pool.wait_ge(msd, b + 1)
                pool.tensor_tensor(rs[:, 0], rs[:, 1], w["minus_half"][:, 0:1].broadcast_to([P, TB]), ALU.pow).then_inc(rsd, 1)
                pool.wait_ge(n_hi, b + 1)
                pool.tensor_tensor(n_hl[:, 1], n_x[:], n_hl[:, 0], ALU.subtract).then_inc(n_lo, 1)

        @block.scalar
        def _(act):
            act.wait_ge(loads, 16 * (2 + DK))
            act.activation(hl_a[:, 0], raw_a[:], ACT.Copy, scale=WS).then_inc(w_hi, 1)
            act.activation(wr_hl[:, 0], wr[:], ACT.Copy, scale=WS).then_inc(w_hi, 1)
            with act.Fori(0, blocks) as b:
                act.wait_ge(xd, b + 1)
                act.wait_ge(t_fill, TB * b)
                act.activation(n_hl[:, 0], n_x[:], ACT.Copy).then_inc(n_hi, 1)
                act.wait_ge(saved, 32 * b)
                for v in range(2):
                    act.wait_ge(a_fill, 2 * b + v + 1)
                    act.activation(a_hl[:, 0, v, :], bank_a[v][:], ACT.Copy, scale=1 / WS).then_inc(a_hi, 1)
            act.wait_ge(step, 2)
            act.activation(logit[:], logit[:], ACT.Exp).then_inc(exp_d, 1)

        @block.vector
        def _(dve):
            dve.wait_ge(w_hi, 2)
            dve.scalar_tensor_tensor(out=hl_a[:, 1], in0=raw_a[:], scalar=WS, in1=hl_a[:, 0], op0=ALU.mult, op1=ALU.subtract)
            dve.scalar_tensor_tensor(out=wr_hl[:, 1], in0=wr[:], scalar=WS, in1=wr_hl[:, 0], op0=ALU.mult, op1=ALU.subtract).then_inc(w_lo, 1)
            dve.wait_ge(w_fill, 1)
            dve.tensor_copy(aT[:].rearrange("p l v c n -> p (l v c n)"), bank_w[:]).then_inc(w_read, 1)
            with dve.Fori(0, blocks) as b:
                x_b = sb_x[:, bass.ds(TB * b, TB), :]
                for n in range(TB):
                    dve.bn_stats(st[:, n, :], sb_x[:, bass.ds(TB * b + n, 1), :].rearrange("p o n -> p (o n)")).then_inc(stats, 1)
                for n in range(TB):
                    wait_apart(dve, stats, TB * b + n + 1, passed_dve)
                    dve.bn_aggr(ag[:, n, :], st[:, n, :]).then_inc(agg, 1)
                dve.wait_ge(agg, TB * b + TB)
                dve.wait_ge(rsd, b)
                dve.tensor_scalar(rs[:, 1], ag[:, :, 1], 1e-5, None, ALU.add).then_inc(msd, 1)
                dve.wait_ge(rsd, b + 1)
                dve.wait_ge(n_lo, b)
                for n in range(TB):
                    ins = dve.tensor_scalar(n_x[:, n, :], sb_x[:, bass.ds(TB * b + n, 1), :].rearrange("p o n -> p (o n)"), ag[:, n, 0:1],
                                            rs[:, 0, n:n + 1], ALU.subtract, ALU.mult)
                ins.then_inc(xd, 1)
                for n in range(TB):
                    dve.wait_ge(t_fill, TB * b + n + 1)
                    dve.tensor_copy(w["nT"][:, :, :, bass.ds(b * NB + n * P, P)], bank_t[n % 2][:].rearrange("p (l c n) -> p l c n", l=2, c=DK)
                                    ).then_inc(t_read, 1)
                dve.wait_ge(l_fill, b + 1)
                dve.tensor_scalar(logit[:, bass.ds(TB * b, TB), :], bank_l[:], 1 / WS, None, ALU.mult).then_inc(l_read, 1)
                for v in range(2):
                    dve.wait_ge(a_hi, 2 * b + v + 1)
                    dve.scalar_tensor_tensor(out=a_hl[:, 1, v, :], in0=bank_a[v][:], scalar=1 / WS, in1=a_hl[:, 0, v, :],
                                             op0=ALU.mult, op1=ALU.subtract).then_inc(a_lo, 1)
            dve.wait_ge(l_read, blocks)
            dve.tensor_reduce(top[:], logit[:], AX.X, ALU.max).then_inc(step, 1)
            dve.wait_ge(step, 1)
            dve.tensor_tensor(logit[:], logit[:], top[:].unsqueeze(2).broadcast_to([P, tiles, NE]), ALU.subtract).then_inc(step, 1)
            dve.wait_ge(exp_d, 1)
            dve.tensor_reduce(total[:], logit[:], AX.X, ALU.add).then_inc(step, 1)
            dve.wait_ge(step, 3)
            dve.reciprocal(inv[:], total[:]).then_inc(step, 1)
            dve.wait_ge(step, 4)
            dve.tensor_tensor(logit[:], logit[:], inv[:].unsqueeze(2).broadcast_to([P, tiles, NE]), ALU.mult).then_inc(step, 1)
            dve.wait_ge(step, 5)
            dve.wait_ge(setup, 4)
            own = logit[:].unsqueeze(3).broadcast_to([P, tiles, NE, NE])
            other = logit[:].unsqueeze(2).broadcast_to([P, tiles, NE, NE])
            dve.tensor_tensor(more[:], other, own, ALU.is_gt)
            dve.tensor_tensor(same[:], other, own, ALU.is_equal).then_inc(step, 1)
            dve.wait_ge(step, 6)
            flat = lambda a: a[:].rearrange("p t e j -> p t (e j)")
            dve.tensor_tensor(flat(same), flat(same), earlier[:].rearrange("p e j -> p (e j)").unsqueeze(1).broadcast_to([P, tiles, NE * NE]),
                              ALU.mult).then_inc(step, 1)
            dve.wait_ge(step, 7)
            dve.tensor_tensor(flat(more), flat(more), flat(same), ALU.add).then_inc(step, 1)
            dve.wait_ge(step, 8)
            dve.tensor_reduce(rank[:], more[:], AX.X, ALU.add).then_inc(step, 1)
            dve.wait_ge(step, 9)
            dve.scalar_tensor_tensor(out=rank[:], in0=rank[:], scalar=TOP - 0.5, in1=logit[:], op0=ALU.is_lt, op1=ALU.mult).then_inc(step, 1)
            dve.wait_ge(step, 10)
            with dve.Fori(0, tiles // 2) as t:
                for n in range(2):
                    dve.tensor_copy(wide[n][:], rank[:, bass.ds(2 * t + n, 1), :].rearrange("p o e -> p (o e)").unsqueeze(2)
                                    .broadcast_to([P, NE, LR])).then_inc(wide_d, 1)
                    dve.wait_ge(e_fill, 2 * t + n + 1)
                    dve.tensor_copy(w["weT"][:, :, bass.ds((2 * t + n) * P, P)], bank_e[:]).then_inc(e_read, 1)

        @block.tensor
        def _(pe):
            ident = w["ident"]
            pe.wait_ge(w_lo, 1)
            pe.wait_ge(setup, 3)
            for l in range(2):
                for v in range(2):
                    for c in range(DK):
                        at = ((l * 2 + v) * DK + c) * P
                        ins = pe.transpose(bank_w[:, at:at + P], hl_a[:, l, v, c * P:(c + 1) * P], ident[:])
            ins.then_inc(w_fill, 1)
            pe.wait_ge(w_read, 1)
            terms = [(d, a, b) for d in range(DK) for a, b in ((0, 0), (1, 0), (0, 1))]
            with pe.Fori(0, blocks) as b:
                pe.wait_ge(n_lo, b + 1)
                for n in range(TB):
                    if n >= 2:
                        pe.wait_ge(t_read, TB * b + n - 1)
                    for l in range(2):
                        for c in range(DK):
                            ins = pe.transpose(bank_t[n % 2][:, (l * DK + c) * P:(l * DK + c + 1) * P], n_hl[:, l, n, c * P:(c + 1) * P], ident[:])
                    ins.then_inc(t_fill, 1)
                pe.wait_ge(l_read, b)
                wait_apart(pe, t_read, TB * (b + 1), passed_pe)
                for n in range(TB):
                    for m, (d, x, y) in enumerate(terms):
                        ins = pe.matmul(bank_l[:, n, :], w["nT"][:, x, d, bass.ds(b * NB + n * P, P)], wr_hl[:, y, d, :], start=(m == 0), stop=(m == len(terms) - 1))
                ins.then_inc(l_fill, 1)
                pe.wait_ge(a_lo, 2 * b)
                for v in range(2):
                    for m, (d, x, y) in enumerate(terms):
                        ins = pe.matmul(bank_a[v][:], aT[:, y, v, d, :], w["nT"][:, x, d, bass.ds(b * NB, NB)], start=(m == 0), stop=(m == len(terms) - 1))
                    ins.then_inc(a_fill, 1)
            with pe.Fori(0, tiles // 2) as t:
                for n in range(2):
                    pe.wait_ge(wide_d, 2 * t + n + 1)
                    pe.wait_ge(e_read, 2 * t + n)
                    for m in range(2):
                        ins = pe.transpose(bank_e[:, m, :], wide[n][:, EPB * m:EPB * (m + 1), :].rearrange("p e r -> p (e r)"), ident32[:])
                    ins.then_inc(e_fill, 1)


def feed_forward(nc, io, sb_x, w, tiles):
    with ExitStack() as ctx:
        sb = lambda name, shape, dt=F32: ctx.enter_context(nc.sbuf_tensor(name, shape, dt))
        sem = lambda name: ctx.enter_context(nc.semaphore("m_" + name))
        ps = lambda name, n=2: [ctx.enter_context(nc.psum_tensor(f"{name}{i}", [P, NB], F32)) for i in range(n)]
        gate, up, down, y = ps("m_gate"), ps("m_up"), ps("m_down"), ps("m_y")
        RING = 6
        a6 = sb("m_a6", [STACK, 2, NE, NB], F16)
        sg = [sb(f"m_sg{n}", [P, NB]) for n in range(3)]
        h_base = [sb(f"m_hb{n}", [P, NB]) for n in range(2)]
        h_e = [[sb(f"m_he{f}_{n}", [P, NB]) for n in range(RING)] for f in range(2)]
        d_f, d_hl = sb("m_df", [P, 2, NB]), sb("m_dhl", [P, 2, 2, NB], F16)
        a_here, g_fill, g_read, u_fill, u_read, d_done, d_scaled, d_hi, d_lo, y_fill, y_read, stored = (
            sem(n) for n in ("a_here", "g_fill", "g_read", "u_fill", "u_read", "d_done", "d_scaled", "d_hi", "d_lo", "y_fill", "y_read", "stored"))
        block = ctx.enter_context(nc.Block())
        blocks = tiles // TB
        PAIRS = FC // 2
        UNITS = PAIRS * 2 * (NE + 1)
        GROUPS = NE // EPB
        DOWNS = PAIRS * 2 * (1 + GROUPS)
        ADMAS = 12

        def unit(b, p, k, fi):
            return UNITS * b + (p * (NE + 1) + k + 1) * 2 + fi + 1

        def downed(b, p, group, fi):
            return DOWNS * b + (p * (GROUPS + 1) + group + 1) * 2 + fi + 1

        def free_at(b, p, k, fi):
            m = NE * p + k - RING
            if m >= 0:
                return downed(b, m // NE, m % NE // EPB, fi)
            m += NE * PAIRS
            return downed(b - 1, m // NE, m % NE // EPB, fi)

        def over_blocks(eng, one, last):
            one(0)
            with eng.Fori(1, blocks) as b:
                one(b)
            last()

        first = lambda b: isinstance(b, int) and b == 0

        @block.sync
        def _(sp):
            def one(b):
                wait(sp, g_fill, UNITS * b)
                wait(sp, u_fill, UNITS * b)
                for v in range(2):
                    for r, part in enumerate((0, 1, 0)):
                        for at, start in ((0, 0), (ER, ER)):
                            sp.dma_start(a6[r * 2 * ER + at:r * 2 * ER + at + ER, v],
                                         w["a_rows"][v, part, start:start + ERS, bass.ds(b * NB, NB)].rearrange("(e r) n -> r e n", r=ER)
                                         ).then_inc(a_here, 16)
                if not first(b):
                    store(b - 1)

            def store(b):
                sp.wait_ge(y_read, 2 * b + 2)
                sp.dma_start(io["out"].rearrange("(t p) n -> p t n", p=P)[:, bass.ds(b * TB, TB), :], sb_x[:, bass.ds(b * TB, TB), :]
                             ).then_inc(stored, 16)

            def last():
                store(blocks - 1)
                sp.wait_ge(stored, 16 * blocks)
            over_blocks(sp, one, last)

        @block.gpsimd
        def _(pool):
            def final(b):
                pool.wait_ge(d_hi, b + 1)
                pool.tensor_tensor(d_hl[:, 1], d_f[:], d_hl[:, 0], ALU.subtract).then_inc(d_lo, 1)
            with pool.Fori(0, blocks) as b:
                final(b)

        @block.scalar
        def _(act):
            def final(b):
                act.wait_ge(d_scaled, b + 1)
                wait(act, y_fill, b)
                act.activation(d_hl[:, 0], d_f[:], ACT.Copy).then_inc(d_hi, 1)

            def one(b):
                for p in range(PAIRS):
                    for k in range(-1, NE):
                        for fi in range(2):
                            n, m = unit(b, p, k, fi), rows_of(2 * p + fi)
                            slot = ((p * (NE + 1) + k + 1) * 2 + fi)
                            act.wait_ge(g_fill, n)
                            if not first(b) or slot >= 3:
                                act.wait_ge(u_read, n - 3)
                            act.activation(sg[slot % 3][0:m], gate[fi][0:m], ACT.Silu, scale=1 / WS).then_inc(g_read, 1)
                        if p == 0 and k == 0 and not first(b):
                            final(b - 1)
            over_blocks(act, one, lambda: final(blocks - 1))

        @block.vector
        def _(dve):
            def scale(b):
                dve.wait_ge(d_done, DOWNS * (b + 1))
                wait(dve, d_lo, b)
                for g in range(GROUPS):
                    ins = dve.tensor_tensor(d_f[:, g], down[g][:], w["weT"][:, g, bass.ds(b * NB, NB)], ALU.mult)
                ins.then_inc(d_scaled, 1)

            def final(b):
                dve.wait_ge(y_fill, b + 1)
                for n in range(2):
                    x_t = sb_x[:, bass.ds(TB * b + 2 * n, 2), :]
                    dve.scalar_tensor_tensor(out=x_t, in0=y[n][:].rearrange("p (t n) -> p t n", t=2), scalar=1 / WS, in1=x_t,
                                             op0=ALU.mult, op1=ALU.add).then_inc(y_read, 1)

            def one(b):
                for p in range(PAIRS):
                    for k in range(-1, NE):
                        for fi in range(2):
                            n, m = unit(b, p, k, fi), rows_of(2 * p + fi)
                            slot = ((p * (NE + 1) + k + 1) * 2 + fi)
                            if k < 0:
                                out = h_base[fi]
                                if not first(b) or p > 0:
                                    dve.wait_ge(d_done, downed(b, p - 1, -1, fi) if p > 0 else downed(b - 1, PAIRS - 1, -1, fi))
                            else:
                                out = h_e[fi][(NE * p + k) % RING]
                                if not first(b) or NE * p + k >= RING:
                                    dve.wait_ge(d_done, free_at(b, p, k, fi))
                            dve.wait_ge(g_read, n)
                            dve.wait_ge(u_fill, n)
                            dve.scalar_tensor_tensor(out=out[0:m], in0=up[fi][0:m], scalar=1 / WS, in1=sg[slot % 3][0:m],
                                                     op0=ALU.mult, op1=ALU.mult).then_inc(u_read, 1)
                        if p == 0 and not first(b):
                            if k == -1:
                                scale(b - 1)
                            if k == 1:
                                final(b - 1)

            def last():
                scale(blocks - 1)
                final(blocks - 1)
            over_blocks(dve, one, last)

        @block.tensor
        def _(pe):
            def sums(b, p, k):
                for v, bank, fill, read in ((0, gate, g_fill, g_read), (1, up, u_fill, u_read)):
                    if k < 0 and not (first(b) and p == 0):
                        pe.wait_ge(read, unit(b, p, k, 1) - 2)
                    for fi in range(2):
                        f, m = 2 * p + fi, rows_of(2 * p + fi)
                        if k >= 0:
                            pe.wait_ge(read, unit(b, p, k, fi) - 2)
                        out = bank[fi][0:m]
                        if k < 0:
                            terms = [(d, x, y_) for d in range(DK) for x, y_ in ((0, 0), (1, 0), (0, 1))]
                            for n, (d, x, y_) in enumerate(terms):
                                ins = pe.matmul(out, w["Wgu"][:, y_, d, v, f * P:f * P + m], w["nT"][:, x, d, bass.ds(b * NB, NB)],
                                                start=(n == 0), stop=(n == len(terms) - 1), skip_group_check=True)
                        else:
                            if p == 0 and k == 0:
                                pe.wait_ge(a_here, 16 * ADMAS * (b + 1))
                            ins = pe.matmul(out, w["B"][:, v, k, f * P:f * P + m], a6[:, v, k, :], start=False, stop=True, skip_group_check=True)
                        ins.then_inc(fill, 1)

            def base_down(b, p):
                for fi in range(2):
                    f, m = 2 * p + fi, rows_of(2 * p + fi)
                    pe.wait_ge(u_read, unit(b, p, -1, fi))
                    for t in range(TB):
                        ins = pe.matmul(y[t // 2][:, (t % 2) * HID:(t % 2 + 1) * HID], h_base[fi][0:m, t * P:(t + 1) * P], w["WdT"][0:m, f, :],
                                        start=(f == 0 and t % 2 == 0), stop=True, skip_group_check=True)
                    ins.then_inc(d_done, 1)

            def expert_down(b, p, g):
                pe.wait_ge(u_read, unit(b, p, EPB * (g + 1) - 1, 1))
                for fi in range(2):
                    f, m = 2 * p + fi, rows_of(2 * p + fi)
                    for q in range(EPB):
                        k = EPB * g + q
                        ins = pe.matmul(down[g][LR * q:LR * (q + 1)], w["AdT"][0:m, f, k, :], h_e[fi][(NE * p + k) % RING][0:m],
                                        start=(f == 0), stop=(f == FC - 1), skip_group_check=True)
                    ins.then_inc(d_done, 1)

            def final(b):
                pe.wait_ge(d_lo, b + 1)
                for t in range(TB):
                    for g in range(GROUPS):
                        for x, y_ in ((0, 0), (1, 0), (0, 1)):
                            ins = pe.matmul(y[t // 2][:, (t % 2) * HID:(t % 2 + 1) * HID], d_hl[:, x, g, t * P:(t + 1) * P], w["BdT"][:, y_, g, :],
                                            start=False, stop=True, skip_group_check=True)
                ins.then_inc(y_fill, 1)

            def one(b):
                for p in range(PAIRS):
                    for k in range(-1, NE):
                        sums(b, p, k)
                        if k == -1 and p > 0:
                            expert_down(b, p - 1, 1)
                        if k == 1:
                            if p == 0 and not first(b):
                                final(b - 1)
                                pe.wait_ge(y_read, 2 * b)
                            if p == 0 and not first(b):
                                pe.wait_ge(d_scaled, b)
                            base_down(b, p)
                        if k == 4:
                            expert_down(b, p, 0)
                expert_down(b, PAIRS - 1, 1)
            over_blocks(pe, one, lambda: final(blocks - 1))


def shared_tiles(nc, ctx):
    return {"ident": ctx.enter_context(nc.sbuf_tensor("ident", [P, P], F16)),
            "minus_half": ctx.enter_context(nc.sbuf_tensor("minus_half", [P, XH], F32))}


def build(nc, io, tiles):
    with nc.sbuf_tensor("x_all", [P, tiles, HID], F32) as sb_x, ExitStack() as shared:
        common = shared_tiles(nc, shared)
        with ExitStack() as ctx:
            w = {**common, **cross_weights(nc, ctx)}
            prepare_cross(nc, io, sb_x, w, tiles)
            cross_attention(nc, io, sb_x, w, tiles)
        with ExitStack() as ctx:
            w = {**common, **self_weights(nc, ctx)}
            prepare_self(nc, io, w)
            self_attention(nc, io, sb_x, w, tiles)
        with ExitStack() as ctx:
            w = {**common, **ffn_weights(nc, ctx, tiles)}
            prepare_ffn(nc, io, w, tiles)
            route(nc, io, sb_x, w, tiles)
            feed_forward(nc, io, sb_x, w, tiles)


ROWS = 128
NAMES = {
    "x": "x", "ctx": "ctx_2048", "mask": "mask_1xSxS2_ff0",
    "Wq": "L0_xattn_Wq", "bq": "L0_xattn_bq", "Wk": "L0_xattn_Wk", "bk": "L0_xattn_bk", "Wv": "L0_xattn_Wv",
    "bv": "L0_xattn_bv", "Wo": "L0_xattn_Wo", "qn": "L0_xattn_qn_w", "kn": "L0_xattn_kn_w",
    "a_Wq": "L0_attn_Wq", "a_bq": "L0_attn_bq", "a_Wk": "L0_attn_Wk", "a_bk": "L0_attn_bk", "a_Wv": "L0_attn_Wv",
    "a_bv": "L0_attn_bv", "a_Wo": "L0_attn_Wo", "a_bo": "L0_attn_bo", "a_kw": "L0_attn_key_weights",
    "f_Wg": "L0_ffn_Wg", "f_Wu": "L0_ffn_Wu", "f_Wd": "L0_ffn_Wd", "f_Wr": "L0_ffn_Wr", "f_Ag": "L0_ffn_Ag",
    "f_Bg": "L0_ffn_Bg", "f_Au": "L0_ffn_Au", "f_Bu": "L0_ffn_Bu", "f_Ad": "L0_ffn_Ad", "f_Bd": "L0_ffn_Bd",
}


def kernel(**inputs):
    import numpy as _np
    import concourse.bacc as _bacc
    from concourse import mybir as _mybir
    from concourse.bass_utils import run_bass_kernel_spmd as _run

    nc = _bacc.Bacc("TRN2", target_bir_lowering=False, num_devices=1)
    arrays, io = {}, {}
    for short, name in NAMES.items():
        a = _np.ascontiguousarray(inputs[name])
        arrays[f"in_{name}"] = a
        io[short] = nc.dram_tensor(f"in_{name}", a.shape, _mybir.dt.from_np(a.dtype), kind="ExternalInput").ap()
    freq = _np.float32(1.0) / _np.power(_np.float32(10000.0), _np.arange(0, AD, 2, dtype=_np.float32) / _np.float32(AD))
    angle = _np.arange(S, dtype=_np.float32)[:, None] * freq[None, :]
    rope = _np.stack([_np.cos(angle), _np.sin(angle)]).astype(_np.float32)
    arrays["rope_table"] = rope
    io["rope"] = nc.dram_tensor("rope_table", rope.shape, F32, kind="ExternalInput").ap()
    shape = inputs["x"].shape
    out = nc.dram_tensor("out_0", shape, F32, kind="ExternalOutput").ap()
    io["x"] = io["x"].rearrange("b s n -> (b s) n")
    io["out"] = out.rearrange("b s n -> (b s) n")
    build(nc, io, ROWS // BT)
    return _run(nc, [arrays], core_ids=[0]).results[0]["out_0"]
```

```python
from contextlib import ExitStack

import concourse.bass as bass
from concourse import mybir

F32 = mybir.dt.float32
F16 = mybir.dt.float16
ALU = mybir.AluOpType
ACT = mybir.ActivationFunctionType
AX = mybir.AxisListType

P = 128
HID = 256
DK = HID // P
S = 32
BT = P // S
WS = 64.0
PS = 4096.0

XH, XKV, XD = 16, 4, 128
XG = XH // XKV
SE = 257
KT = 2
LAST = SE - 1
XR = 3


class BankCount:

    def __init__(self, order, tiles, steps, banks, first=1, emptier=lambda name: 0):
        self.first, self.last, self.found, slot, fills, held, emptied = first, tiles - 1, {}, 0, 0, {}, {}
        for t in range(-2, tiles + 1):
            for i in range(steps):
                for name in order(t, i):
                    if name is not None:
                        who, fills = emptier(name), fills + 1
                        emptied[who] = emptied.get(who, 0) + 1
                        before, n_before = held.get(slot % banks, (0, 0))
                        self.found[t, i, name] = (slot % banks, who, before), (fills, emptied[who], n_before)
                        held[slot % banks] = who, emptied[who]
                    slot += 1
        for t, i, name in self.found:
            if first <= t < self.last:
                assert self.at(t, i, name) == self.linear(t, i, name), (t, i, name)

    def linear(self, t, i, name):
        (place, n), (_, n2) = self.found[self.first, i, name], self.found[self.first + 1, i, name]
        return place, tuple(a + (b - a) * (t - self.first) for a, b in zip(n, n2))

    def at(self, t, i, name):
        return self.found[t, i, name] if isinstance(t, int) else self.linear(t, i, name)

    def bank(self, t, i, name):
        return self.at(t, i, name)[0][0]

    def filled(self, t, i, name):
        return self.at(t, i, name)[1][0]

    def emptied(self, t, i, name):
        return self.at(t, i, name)[1][1]

    def held_before(self, t, i, name):
        (_, _, who), (_, _, n) = self.at(t, i, name)
        return who, n


def wait(eng, sem, value):
    if not isinstance(value, int) or value > 0:
        eng.wait_ge(sem, value)


def wait_apart(eng, sem, value, passed):
    wait(eng, sem, value)
    if not isinstance(value, int):
        eng.sem_inc(passed, 1)


def spread(ap, n=P):
    return ap.partition_broadcast(n)


def prepare_cross(nc, io, sb_x, w, tiles):
    with ExitStack() as ctx:
        sb = lambda name, shape, dt=F32: ctx.enter_context(nc.sbuf_tensor(name, shape, dt))
        sem = lambda name: ctx.enter_context(nc.semaphore(name))
        pst = ctx.enter_context(nc.psum_tensor("p0_t", [P, 1024], F16))
        psk = ctx.enter_context(nc.psum_tensor("p0_k", [P, 2, 512], F32))
        psc = ctx.enter_context(nc.psum_tensor("p0_c", [P, HID], F32))
        raw_q = sb("raw_q", [P, DK, XH * XD])
        raw_kv = sb("raw_kv", [P, DK, 2, XKV * XD])
        raw_o = sb("raw_o", [P, XH, HID])
        bvt = sb("bvt", [P, XKV])
        kn = sb("kn", [P, XD])
        ct_in = sb("ct_in", [P, HID])
        ct_hl = sb("ct_hl", [P, 2, HID], F16)
        ctT = sb("ctT", [P, 2, DK, P], F16)
        kb = sb("kb0", [P, XKV * XD])
        ksq = sb("ksq0", [P, XKV * XD])
        ssq = sb("ssq0", [P, XKV])
        rk = sb("rk0", [P, XKV])
        mean = sb("mean0", [P, XKV])
        kh = sb("kh0", [P, 2, XKV * XD], F16)
        vpad = sb("vpad", [P, XKV, XR, XKV * XD], F16)

        w_in, x_in, small_in, mask_in, scratch_out = (sem(n) for n in ("w_in", "x_in", "small_in", "mask_in", "scratch_out"))
        hi_done, lo_done, pool_done, pe_done = (sem(n) for n in ("hi_done", "lo_done", "pool_done", "pe_done"))
        k_step = sem("k_step")
        block = ctx.enter_context(nc.Block())

        @block.sync
        def _(sp):
            sp.dma_start(raw_q[:], io["Wq"].rearrange("(c p) n -> p c n", p=P)).then_inc(w_in, 16)
            sp.dma_start(raw_kv[:, :, 0, :], io["Wk"].rearrange("(c p) n -> p c n", p=P)).then_inc(w_in, 16)
            sp.dma_start(raw_kv[:, :, 1, :], io["Wv"].rearrange("(c p) n -> p c n", p=P)).then_inc(w_in, 16)
            sp.dma_start(raw_o[:], io["Wo"].rearrange("(h p) n -> p h n", p=P)).then_inc(w_in, 16)
            sp.dma_start(ct_in[:], io["ctx"][:, LAST, :]).then_inc(small_in, 16)
            sp.dma_start(w["bq"][:], spread(io["bq"])).then_inc(small_in, 16)
            sp.dma_start(w["bk"][:], spread(io["bk"])).then_inc(small_in, 16)
            sp.dma_start(w["wqk"][:], spread(io["qn"])).then_inc(small_in, 16)
            sp.dma_start(kn[:], spread(io["kn"])).then_inc(small_in, 16)
            with nc.allow_non_contiguous_dma(reason="512 elements, once"):
                sp.dma_start(bvt[:], io["bv"].rearrange("(k p) -> p k", p=P)).then_inc(small_in, 16)
            for g in range(XG):
                sp.dma_start(w["mask"][g * S:(g + 1) * S, :], io["mask"][0]).then_inc(mask_in, 16)
            sp.dma_start(sb_x[:, 0:tiles, :], io["x"].rearrange("(t p) n -> p t n", p=P)[:, 0:tiles, :]).then_inc(x_in, 16)
            sp.wait_ge(lo_done, 14)
            sp.wait_ge(pool_done, 2)
            for k in range(XKV):
                sp.dma_start(w["v_last"][XR * k:XR * (k + 1)].rearrange("r b n -> b r n"), vpad[:, k, :, :]).then_inc(scratch_out, 16)
            sp.wait_ge(scratch_out, 16 * XKV)
            sp.wait_ge(x_in, 16)

        @block.gpsimd
        def _(pool):
            pool.memset(w["ident"][:], 0.0).then_inc(pool_done, 1)
            pool.wait_ge(pool_done, 1)
            pool.affine_select(out=w["ident"][:], in_=w["ident"][:], compare_op=ALU.not_equal, fill=1.0, base=0,
                               pattern=[[-1, P]], channel_multiplier=1).then_inc(pool_done, 1)
            pool.memset(w["minus_half"][:], -0.5).then_inc(pool_done, 1)
            pool.wait_ge(pool_done, 3)
            pool.wait_ge(lo_done, 9)
            pool.tensor_tensor(rk[:], mean[:], w["minus_half"][:, 0:XKV], ALU.pow).then_inc(pool_done, 1)

        @block.scalar
        def _(act):
            act.wait_ge(w_in, 64)
            act.wait_ge(small_in, 96)
            act.activation(w["Wq"][:, 0], raw_q[:], ACT.Copy, scale=WS).then_inc(hi_done, 1)
            act.activation(w["Wkv"][:, 0], raw_kv[:], ACT.Copy, scale=WS).then_inc(hi_done, 1)
            act.activation(w["Wo"][:, 0], raw_o[:], ACT.Copy, scale=WS).then_inc(hi_done, 1)
            act.activation(ct_hl[:, 0], ct_in[:], ACT.Copy).then_inc(hi_done, 1)
            act.wait_ge(pe_done, 3)
            act.wait_ge(lo_done, 6)
            for k in range(XKV):
                act.activation(vpad[:, k, 0, k * XD:(k + 1) * XD], psk[:, 1, k * XD:(k + 1) * XD], ACT.Copy, scale=1 / WS).then_inc(hi_done, 1)
                act.activation(vpad[:, k, 1, k * XD:(k + 1) * XD], psk[:, 1, k * XD:(k + 1) * XD], ACT.Copy, scale=1 / WS).then_inc(hi_done, 1)

        @block.vector
        def _(dve):
            dve.memset(vpad[:], 0.0)
            dve.wait_ge(small_in, 96)
            dve.wait_ge(mask_in, 16 * XG)
            dve.tensor_scalar(w["mask"][:], w["mask"][:], float(XD) ** 0.5, None, ALU.mult)
            dve.tensor_tensor(w["wqk"][:], w["wqk"][:], kn[:], ALU.mult)
            for n, (name, raw) in enumerate((("Wq", raw_q), ("Wkv", raw_kv), ("Wo", raw_o))):
                dve.wait_ge(hi_done, n + 1)
                if name == "Wkv":
                    dst, src = (w[name][:, h].rearrange("p c v n -> p (c v n)") for h in (1, 0)), raw[:].rearrange("p c v n -> p (c v n)")
                    lo, hi = dst
                else:
                    lo, hi = (w[name][:, h].rearrange("p c n -> p (c n)") for h in (1, 0))
                    src = raw[:].rearrange("p c n -> p (c n)")
                dve.scalar_tensor_tensor(out=lo, in0=src, scalar=WS, in1=hi, op0=ALU.mult, op1=ALU.subtract).then_inc(lo_done, 1)
            dve.wait_ge(hi_done, 4)
            dve.tensor_tensor(ct_hl[:, 1], ct_in[:], ct_hl[:, 0], ALU.subtract).then_inc(lo_done, 1)
            dve.wait_ge(pe_done, 1)
            dve.tensor_copy(ctT[:].rearrange("p l c n -> p (l c n)"), pst[:, 0:2 * DK * P]).then_inc(lo_done, 1)
            dve.wait_ge(pe_done, 2)
            dve.tensor_scalar(w["cvec"][:], psc[:], 1.0, None, ALU.mult).then_inc(lo_done, 1)
            dve.wait_ge(pe_done, 3)
            dve.scalar_tensor_tensor(out=kb[:], in0=psk[:, 0], scalar=1 / WS, in1=w["bk"][:], op0=ALU.mult, op1=ALU.add).then_inc(lo_done, 1)
            dve.wait_ge(lo_done, 7)
            dve.tensor_tensor(ksq[:], kb[:], kb[:], ALU.mult).then_inc(lo_done, 1)
            dve.wait_ge(lo_done, 8)
            dve.tensor_reduce(ssq[:], ksq[:].rearrange("p (k d) -> p k d", k=XKV), AX.X, ALU.add).then_inc(k_step, 1)
            dve.wait_ge(k_step, 1)
            dve.tensor_scalar(mean[:], ssq[:], 1.0 / XD, 1e-6, ALU.mult, ALU.add).then_inc(lo_done, 1)
            dve.wait_ge(pool_done, 4)
            for k in range(XKV):
                dve.tensor_scalar(kh[:, 0, k * XD:(k + 1) * XD], kb[:, k * XD:(k + 1) * XD], rk[:, k:k + 1], None, ALU.mult).then_inc(k_step, 1)
            dve.wait_ge(k_step, 1 + XKV)
            for k in range(XKV):
                ins = dve.scalar_tensor_tensor(out=kh[:, 1, k * XD:(k + 1) * XD], in0=kb[:, k * XD:(k + 1) * XD], scalar=rk[:, k:k + 1],
                                               in1=kh[:, 0, k * XD:(k + 1) * XD], op0=ALU.mult, op1=ALU.subtract)
            ins.then_inc(lo_done, 1)
            dve.wait_ge(hi_done, 4 + 2 * XKV)
            for k in range(XKV):
                dve.scalar_tensor_tensor(out=vpad[:, k, 2, k * XD:(k + 1) * XD], in0=psk[:, 1, k * XD:(k + 1) * XD], scalar=1 / WS,
                                         in1=vpad[:, k, 0, k * XD:(k + 1) * XD], op0=ALU.mult, op1=ALU.subtract).then_inc(lo_done, 1)
            dve.wait_ge(pe_done, 4)
            dve.tensor_copy(w["kT_last"][:].rearrange("p l k b -> p (l k b)"), pst[:]).then_inc(lo_done, 1)

        @block.tensor
        def _(pe):
            pe.wait_ge(pool_done, 2)
            pe.wait_ge(lo_done, 4)
            for l in range(2):
                for c in range(DK):
                    ins = pe.transpose(pst[:, (l * DK + c) * P:(l * DK + c + 1) * P], ct_hl[:, l, c * P:(c + 1) * P], w["ident"][:])
            ins.then_inc(pe_done, 1)
            for h in range(XH):
                ins = pe.matmul(psc[:], bvt[:, h // XG:h // XG + 1].broadcast_to([P, P]), raw_o[:, h, :], start=(h == 0), stop=(h == XH - 1))
            ins.then_inc(pe_done, 1)
            pe.wait_ge(lo_done, 5)
            for v in range(2):
                n = 0
                for c in range(DK):
                    for a, b in ((0, 0), (1, 0), (0, 1)):
                        ins = pe.matmul(psk[:, v], ctT[:, a, c, :], w["Wkv"][:, b, c, v, :], start=(n == 0), stop=(n == 3 * DK - 1))
                        n += 1
            ins.then_inc(pe_done, 1)
            pe.wait_ge(lo_done, 10)
            for l in range(2):
                for k in range(XKV):
                    ins = pe.transpose(pst[:, (l * XKV + k) * P:(l * XKV + k + 1) * P], kh[:, l, k * XD:(k + 1) * XD], w["ident"][:])
            ins.then_inc(pe_done, 1)


def cross_attention(nc, io, sb_x, w, tiles):
    rows = tiles * BT
    with ExitStack() as ctx:
        sb = lambda name, shape, dt=F32: ctx.enter_context(nc.sbuf_tensor(name, shape, dt))
        sem = lambda name: ctx.enter_context(nc.semaphore(name))
        bank_t = [ctx.enter_context(nc.psum_tensor(f"turn{n}", [P, 1024], F16)) for n in range(3)]
        bank_m = [ctx.enter_context(nc.psum_tensor(f"proj{n}", [P, 512], F32)) for n in range(2)]
        bank_s = [ctx.enter_context(nc.psum_tensor(f"score{n}", [P, SE], F32)) for n in range(2)]
        bank_o = ctx.enter_context(nc.psum_tensor("sum", [P, XKV, XG * S], F32))

        c_in = [sb(f"c_in{n}", [P, KT, HID]) for n in range(2)]
        c_hl = [sb(f"c_hl{n}", [P, 2, KT, HID], F16) for n in range(2)]
        cT = [sb(f"cT{n}", [P, 2, DK, KT, P], F16) for n in range(2)]
        k_b = sb("k_b", [P, KT, XKV * XD])
        k_sq = sb("k_sq", [P, KT, XKV * XD])
        k_ss = sb("k_ss", [P, KT * XKV])
        k_ms = sb("k_ms", [P, KT * XKV])
        k_r = sb("k_r", [P, KT * XKV])
        k_n = sb("k_n", [P, KT, XKV * XD])
        k_hl = sb("k_hl", [P, 2, KT, XKV * XD], F16)
        kT = [sb(f"kT{n}", [P, 2, XKV, SE], F16) for n in range(2)]
        v_hl = [sb(f"v_hl{n}", [P, 2, KT, XKV * XD], F16) for n in range(BT)]
        v_end = [sb(f"v_end{n}", [XKV * XR, XKV * XD], F16) for n in range(BT)]
        s_n = sb("s_n", [P, XKV, SE])
        s_min = sb("s_min", [P, XKV])
        p_f = sb("p_f", [P, XKV, SE])
        p_sum = sb("p_sum", [P, XKV])
        p_inv = sb("p_inv", [P, XKV])
        p_scl = sb("p_scl", [P, XKV])
        p_hl = sb("p_hl", [P, 2, XKV, SE], F16)
        p_end = sb("p_end", [P, XKV, XR], F16)
        pT = sb("pT", [P, XKV, 2, KT, P], F16)
        pT_end = sb("pT_end", [XKV * XR, P], F16)
        oT = sb("oT", [P, 2, XH, P], F16)
        n_st = sb("n_st", [P, 6])
        n_ag = sb("n_ag", [P, 2])
        n_r = sb("n_r", [P, 2])
        n_x = sb("n_x", [P, HID])
        n_hl = sb("n_hl", [P, 2, HID], F16)
        nT = sb("nT", [P, 2, DK, P], F16)
        q_b = sb("q_b", [P, XH * XD])
        q_w = sb("q_w", [P, XH * XD])
        q_ms = sb("q_ms", [P, XH])
        q_ss = sb("q_ss", [P, XH])
        q_r = sb("q_r", [P, XH])
        q_hl = sb("q_hl", [P, 2, XH * XD], F16)
        q_sq = q_hl[:].rearrange("p l n -> p (l n)").bitcast(F32)
        qT = sb("qT", [P, 2, XKV, BT, XG, S], F16)

        ctx_loaded = [sem(f"ctx_loaded{n}") for n in range(2)]
        end_loaded = [sem(f"end_loaded{n}") for n in range(BT)]
        t_fill, t_read, m_fill, m_read, s_fill, s_read, o_fill, o_read = (
            sem(n) for n in ("t_fill", "t_read", "m_fill", "m_read", "s_fill", "s_read", "o_fill", "o_read"))
        c_hi, v_hi, k_sqd, k_hi, exp_done, o_hi, n_hi, q_sqd, q_hi = (
            sem(n) for n in ("c_hi", "v_hi", "k_sqd", "k_hi", "exp_done", "o_hi", "n_hi", "q_sqd", "q_hi"))
        c_lo, k_rs, k_lo, k_end, p_hi, p_ends, n_rs, n_lo, q_rs, q_wd, q_lo = (
            sem(n) for n in ("c_lo", "k_rs", "k_lo", "k_end", "p_hi", "p_ends", "n_rs", "n_lo", "q_rs", "q_wd", "q_lo"))
        k_msd, k_nd, p_scd, p_lo, n_msd, n_xd, q_msd, q_nd = (
            sem(n) for n in ("k_msd", "k_nd", "p_scd", "p_lo", "n_msd", "n_xd", "q_msd", "q_nd"))

        row = lambda t, i: BT * t + i
        has = lambda j: not isinstance(j, int) or 0 <= j < rows
        has_tile = lambda t: not isinstance(t, int) or 0 <= t < tiles
        step_before = lambda t, i: (t, i - 1) if i else (t - 1, BT - 1)

        def order_t(t, i):
            j = row(t, i)
            out = []
            out += ["K0", "K1"] if has(j - 1) else [None] * 2
            out += ["P0", "P1", "Pe"] if has(j - 2) else [None] * 3
            out += ["C"] if has(j + 1) else [None]
            if i == 0:
                out += ["Q0", "Q1", "Q2", "Q3"] if has_tile(t) else [None] * 4
            if i == 0:
                out += ["X"] if has_tile(t + 1) else [None]
            return out + ([None] if i == 3 else [])

        def order_m(t, i):
            out = []
            out += ["K0"] if has(row(t, i)) else []
            out += ["K1"] if has(row(t, i)) else []
            out += ["V0"] if has(row(t, i)) else []
            out += ["V1"] if has(row(t, i)) else []
            out += ["W", None] if i == 2 and has_tile(t - 1) else []
            out += ["Q0", "Q1", "Q2", "Q3"] if i == 1 and has_tile(t + 1) else []
            return out

        passed_dve, passed_pool = sem("passed_dve"), sem("passed_pool")
        t_read_act = sem("t_read_act")
        T_READ = {"act": t_read_act, "dve": t_read}
        turns = BankCount(order_t, tiles, BT, 3, emptier=lambda name: "act" if name in ("P0", "P1") else "dve")
        projs = BankCount(order_m, tiles, BT, 2)
        block = ctx.enter_context(nc.Block())

        def over_tiles(eng, tile):
            tile(-1)
            tile(0)
            with eng.Fori(1, tiles - 1) as t:
                tile(t)
            tile(tiles - 1)
            tile(tiles)

        @block.sync
        def _(sp):
            def tile(t):
                for i in range(BT):
                    j = row(t, i)
                    if has(j + 2):
                        wait(sp, c_lo, j + 1)
                        sp.dma_start(c_in[i % 2][:], io["ctx"][bass.ds(j + 2, 1), 0:LAST, :].rearrange("o (c p) n -> p (o c) n", p=P)
                                     ).then_inc(ctx_loaded[i % 2], 16)
                    if has(j):
                        wait(sp, o_fill, j - 3)
                        sp.dma_start(v_end[i][:], w["v_last"][:, bass.ds(j, 1), :].rearrange("r o n -> r (o n)")).then_inc(end_loaded[i], 16)
            over_tiles(sp, tile)

        @block.gpsimd
        def _(pool):
            by_head = lambda ap, half: ap[:, half * XH // 2 * XD:(half + 1) * XH // 2 * XD].rearrange("p (h d) -> p h d", h=XH // 2)

            def weigh_q(t, half):
                pool.wait_ge(m_read, projs.emptied(t, 1, f"Q{2 * half + 1}"))
                wait(pool, q_nd, 2 * (t + 1))
                pool.tensor_tensor(by_head(q_w, half), by_head(q_b, half), w["wqk"][:].unsqueeze(1).broadcast_to([P, XH // 2, XD]),
                                   ALU.mult).then_inc(q_wd, 1)

            def norm_q(t, half):
                pool.wait_ge(q_rs, t + 2)
                pool.tensor_tensor(by_head(q_w, half), by_head(q_w, half),
                                   q_r[:, half * XH // 2:(half + 1) * XH // 2].unsqueeze(2).broadcast_to([P, XH // 2, XD]), ALU.mult).then_inc(q_nd, 1)

            def low_q(t, half):
                at = slice(half * XH // 2 * XD, (half + 1) * XH // 2 * XD)
                pool.wait_ge(q_hi, 2 * t + half + 1)
                pool.tensor_tensor(q_hl[:, 1, at], q_w[:, at], q_hl[:, 0, at], ALU.subtract).then_inc(q_lo, 1)

            def tile(t):
                for i in range(BT):
                    j = row(t, i)
                    if has(j - 1):
                        wait_apart(pool, s_fill, XKV * (j - 2), passed_pool)
                        pool.tensor_copy(kT[(i - 1) % 2][:, :, :, LAST:SE],
                                         w["kT_last"][:, :, :, bass.ds(j - 1, 1)]).then_inc(k_end, 1)
                    if has(j + 2):
                        pool.wait_ge(c_hi, j + 3)
                        pool.tensor_tensor(c_hl[i % 2][:, 1], c_in[i % 2][:], c_hl[i % 2][:, 0], ALU.subtract).then_inc(c_lo, 1)
                    if i == 2 and has_tile(t + 1):
                        weigh_q(t, 0)
                    if i == 0 and has_tile(t + 1):
                        pool.wait_ge(n_msd, t + 2)
                        wait(pool, n_xd, t + 1)
                        pool.tensor_tensor(n_r[:, 0:1], n_r[:, 1:2], w["minus_half"][:, 0:1], ALU.pow).then_inc(n_rs, 1)
                    if i == 0 and has_tile(t):
                        low_q(t, 0)
                    if i == 3 and has_tile(t + 1):
                        pool.wait_ge(q_msd, t + 2)
                        pool.tensor_tensor(q_r[:], q_ms[:], w["minus_half"][:, 0:XH], ALU.pow).then_inc(q_rs, 1)
                    if has(j):
                        wait_apart(pool, k_sqd, KT * XKV * (j + 1), passed_pool)
                        wait_apart(pool, k_nd, j, passed_pool)
                        pool.tensor_scalar(k_ms[:], k_ss[:], 1.0 / XD, 1e-6, ALU.mult, ALU.add).then_inc(k_msd, 1)
                        pool.wait_ge(k_msd, j + 1)
                        pool.tensor_tensor(k_r[:], k_ms[:], w["minus_half"][:, 0:KT * XKV], ALU.pow).then_inc(k_rs, 1)
                    if i == 2 and has_tile(t + 1):
                        weigh_q(t, 1)
                    if i == 3 and has_tile(t + 1):
                        norm_q(t, 0)
                    if i == 3 and has_tile(t + 1):
                        norm_q(t, 1)
                    if i == 0 and has_tile(t):
                        low_q(t, 1)
                    if has(j):
                        pool.wait_ge(k_hi, j + 1)
                        pool.tensor_tensor(k_hl[:, 1], k_n[:], k_hl[:, 0], ALU.subtract).then_inc(k_lo, 1)
                    if i == 0 and has_tile(t + 1):
                        pool.wait_ge(n_hi, t + 2)
                        pool.tensor_tensor(n_hl[:, 1], n_x[:], n_hl[:, 0], ALU.subtract).then_inc(n_lo, 1)
                    if has(j - 1):
                        wait_apart(pool, p_lo, j, passed_pool)
                        for r, part in enumerate((0, 1, 0)):
                            ins = pool.tensor_copy(p_end[:, :, r], p_hl[:, part, :, LAST])
                        ins.then_inc(p_ends, 1)
            over_tiles(pool, tile)

        @block.scalar
        def _(act):
            def high_q(t, half):
                at = slice(half * XH // 2 * XD, (half + 1) * XH // 2 * XD)
                act.wait_ge(q_nd, 2 * t + half + 1)
                act.activation(q_hl[:, 0, at], q_w[:, at], ACT.Copy).then_inc(q_hi, 1)

            def square_q(t, half):
                at = slice(half * XH // 2 * XD, (half + 1) * XH // 2 * XD)
                act.wait_ge(m_read, projs.emptied(t, 1, f"Q{2 * half + 1}"))
                if has_tile(t):
                    act.wait_ge(t_fill, turns.filled(t, 0, "Q3"))
                act.activation(q_sq[:, at], q_b[:, at], ACT.Square).then_inc(q_sqd, 1)

            def square_k(t, i, c):
                act.wait_ge(m_read, projs.emptied(t, i, f"K{c}"))
                for k in range(XKV):
                    act.activation(k_sq[:, c, k * XD:(k + 1) * XD], k_b[:, c, k * XD:(k + 1) * XD], ACT.Square,
                                   accum_out=k_ss[:, c * XKV + k:c * XKV + k + 1]).then_inc(k_sqd, 1)

            def high_v(t, i, c):
                act.wait_ge(m_fill, projs.filled(t, i, f"V{c}"))
                act.activation(v_hl[i][:, 0, c, :], bank_m[projs.bank(t, i, f"V{c}")][:], ACT.Copy, scale=1 / WS).then_inc(v_hi, 1)

            def tile(t):
                for i in range(BT):
                    j = row(t, i)
                    if has(j + 2):
                        act.wait_ge(ctx_loaded[i % 2], 16 * (2 * t + i // 2 + 2))
                        if has(j):
                            wait(act, t_fill, turns.filled(*step_before(t, i), "C"))
                        act.activation(c_hl[i % 2][:, 0], c_in[i % 2][:], ACT.Copy).then_inc(c_hi, 1)
                    if i == 0 and has_tile(t):
                        high_q(t, 0)
                    if i == 0 and has_tile(t):
                        high_q(t, 1)
                    if has(j):
                        wait(act, k_msd, j)
                        square_k(t, i, 0)
                    if has(j):
                        square_k(t, i, 1)
                    if has(j):
                        wait(act, o_fill, j - 3)
                        high_v(t, i, 0)
                    if has(j - 1):
                        wait(act, p_lo, j - 1)
                        for k in range(XKV):
                            act.wait_ge(s_read, XKV * (j - 1) + k + 1)
                            ins = act.activation(p_f[:, k, :], s_n[:, k, :], ACT.Exp, bias=s_min[:, k:k + 1], scale=-1.0,
                                                 accum_out=p_sum[:, k:k + 1])
                        ins.then_inc(exp_done, 1)
                    if has(j - 2):
                        wait(act, o_fill, j - 2)
                        for half in range(2):
                            act.wait_ge(t_fill, turns.filled(t, i, f"P{half}"))
                            act.activation(pT[:, 2 * half:2 * half + 2].rearrange("p k l c n -> p (k l c n)"),
                                           bank_t[turns.bank(t, i, f"P{half}")][:], ACT.Copy).then_inc(t_read_act, 1)
                    if has(j):
                        high_v(t, i, 1)
                    if has(j - 1):
                        wait(act, t_fill, turns.filled(t, i, "Pe") if has(j - 2) else 0)
                        for k in range(XKV):
                            if k == 0:
                                act.wait_ge(p_scd, j)
                            ins = act.activation(p_hl[:, 0, k, :], p_f[:, k, :], ACT.Copy, scale=p_scl[:, k:k + 1])
                        ins.then_inc(p_hi, 1)
                    if has(j):
                        act.wait_ge(k_nd, j + 1)
                        act.activation(k_hl[:, 0], k_n[:], ACT.Copy).then_inc(k_hi, 1)
                    if i == 2 and has_tile(t + 1):
                        square_q(t, 0)
                    if has(j - 2):
                        act.wait_ge(o_fill, j - 1)
                        tt = t if i >= 2 else t - 1
                        if has_tile(tt - 1):
                            act.wait_ge(m_fill, projs.filled(tt, 2, "W"))
                        b = (i - 2) % BT
                        act.activation(oT[:, 0, :, b * S:(b + 1) * S], bank_o[:].rearrange("p k (g s) -> p (k g) s", g=XG), ACT.Copy,
                                       scale=1 / PS).then_inc(o_hi, 1)
                    if i == 2 and has_tile(t + 1):
                        square_q(t, 1)
                    if i == 0 and has_tile(t + 1):
                        act.wait_ge(n_xd, t + 2)
                        act.activation(n_hl[:, 0], n_x[:], ACT.Copy).then_inc(n_hi, 1)
            over_tiles(act, tile)

        @block.vector
        def _(dve):
            link_a, link_p, link_q = (sem(n) for n in ("link_a", "link_p", "link_q"))

            def sum_q(t, half):
                at = slice(half * XH // 2 * XD, (half + 1) * XH // 2 * XD)
                dve.wait_ge(q_sqd, 2 * (t + 1) + half + 1)
                dve.tensor_reduce(q_ss[:, half * XH // 2:(half + 1) * XH // 2], q_sq[:, at].rearrange("p (h d) -> p h d", h=XH // 2),
                                  AX.X, ALU.add).then_inc(link_q, 1)

            def low_v(t, i, j, c):
                dve.wait_ge(v_hi, KT * j + c + 1)
                dve.scalar_tensor_tensor(out=v_hl[i][:, 1, c, :], in0=bank_m[projs.bank(t, i, f"V{c}")][:], scalar=1 / WS,
                                         in1=v_hl[i][:, 0, c, :], op0=ALU.mult, op1=ALU.subtract).then_inc(m_read, 1)

            def read_turned(t, i, name, out, columns=1024, rows_=P):
                dve.wait_ge(t_fill, turns.filled(t, i, name))
                dve.tensor_copy(out, bank_t[turns.bank(t, i, name)][0:rows_, 0:columns]).then_inc(t_read, 1)

            def tile(t):
                for i in range(BT):
                    j = row(t, i)
                    if has(j):
                        wait(dve, k_nd, j)
                        wait(dve, k_sqd, KT * XKV * j)
                        for c in range(KT):
                            dve.wait_ge(m_fill, projs.filled(t, i, f"K{c}"))
                            dve.scalar_tensor_tensor(out=k_b[:, c, :], in0=bank_m[projs.bank(t, i, f"K{c}")][:], scalar=1 / WS, in1=w["bk"][:],
                                                     op0=ALU.mult, op1=ALU.add).then_inc(m_read, 1)
                    if i == 0 and has_tile(t + 1):
                        dve.bn_stats(n_st[:], sb_x[:, bass.ds(t + 1, 1), :].rearrange("p o n -> p (o n)")).then_inc(link_a, 1)
                        wait_apart(dve, link_a, 2 * (t + 1) + 1, passed_dve)
                        dve.bn_aggr(n_ag[:], n_st[:]).then_inc(link_a, 1)
                        dve.wait_ge(link_a, 2 * (t + 1) + 2)
                        wait(dve, n_rs, t + 1)
                        dve.tensor_scalar(n_r[:, 1:2], n_ag[:, 1:2], 1e-5, None, ALU.add).then_inc(n_msd, 1)
                    if has(j - 1):
                        wait(dve, s_fill, XKV * (j - 2))
                        for c in range(KT):
                            dve.wait_ge(t_fill, turns.filled(t, i, f"K{c}"))
                            dve.tensor_copy(kT[(i - 1) % 2][:, :, :, c * P:(c + 1) * P],
                                            bank_t[turns.bank(t, i, f"K{c}")][:].rearrange("p (l k n) -> p l k n", l=2, k=XKV)).then_inc(t_read, 1)
                    if has(j - 1):
                        wait(dve, exp_done, j - 1)
                        for k in range(XKV):
                            wait_apart(dve, s_fill, XKV * (j - 1) + k + 1, passed_dve)
                            dve.tensor_tensor_reduce(out=s_n[:, k, :], in0=bank_s[k % 2][:], in1=w["mask"][:], scale=-(XD ** -0.5),
                                                     scalar=3e38, op0=ALU.add, op1=ALU.min,
                                                     accum_out=s_min[:, k:k + 1]).then_inc(s_read, 1)
                    if has(j):
                        dve.wait_ge(k_rs, j + 1)
                        wait(dve, k_lo, j)
                        dve.tensor_tensor(k_n[:].rearrange("p c (k d) -> p (c k) d", k=XKV), k_b[:].rearrange("p c (k d) -> p (c k) d", k=XKV),
                                          k_r[:].unsqueeze(2).broadcast_to([P, KT * XKV, XD]), ALU.mult).then_inc(k_nd, 1)
                    if has(j - 2):
                        wait(dve, o_fill, j - 2)
                        read_turned(t, i, "Pe", pT_end[:], P, XKV * XR)
                    if has(j - 1):
                        dve.wait_ge(exp_done, j)
                        wait(dve, p_hi, j - 1)
                        wait(dve, p_lo, j - 1)
                        dve.reciprocal(p_inv[:], p_sum[:]).then_inc(link_p, 1)
                        dve.wait_ge(link_p, j)
                        dve.tensor_scalar(p_scl[:], p_inv[:], PS, None, ALU.mult).then_inc(p_scd, 1)
                    if has(j):
                        low_v(t, i, j, 0)
                    if has(j):
                        low_v(t, i, j, 1)
                    if has(j + 1):
                        read_turned(t, i, "C", cT[(i + 1) % 2][:].rearrange("p l d c n -> p (l d c n)"))
                    if i == 0 and has_tile(t + 1):
                        dve.wait_ge(n_rs, t + 2)
                        wait(dve, n_lo, t + 1)
                        dve.tensor_scalar(n_x[:], sb_x[:, bass.ds(t + 1, 1), :].rearrange("p o n -> p (o n)"), n_ag[:, 0:1], n_r[:, 0:1],
                                          ALU.subtract, ALU.mult).then_inc(n_xd, 1)
                    if i == 2 and has_tile(t - 1):
                        n = projs.filled(t, i, "W")
                        dve.wait_ge(m_fill, n)
                        x_t = sb_x[:, bass.ds(t - 1, 1), :].rearrange("p o n -> p (o n)")
                        dve.scalar_tensor_tensor(out=x_t, in0=bank_m[projs.bank(t, i, "W")][:, 0:HID], scalar=1 / WS, in1=x_t,
                                                 op0=ALU.mult, op1=ALU.add).then_inc(m_read, 1)
                        dve.wait_ge(m_read, n)
                        dve.tensor_tensor(x_t, x_t, w["cvec"][:], ALU.add)
                    if has(j - 1):
                        dve.wait_ge(p_hi, j)
                        for k in range(XKV):
                            ins = dve.scalar_tensor_tensor(out=p_hl[:, 1, k, :], in0=p_f[:, k, :], scalar=p_scl[:, k:k + 1],
                                                           in1=p_hl[:, 0, k, :], op0=ALU.mult, op1=ALU.subtract)
                        ins.then_inc(p_lo, 1)
                    if i == 0 and has_tile(t):
                        wait(dve, s_fill, XKV * BT * t)
                        for k in range(XKV):
                            dve.wait_ge(t_fill, turns.filled(t, i, f"Q{k}"))
                            src = bank_t[turns.bank(t, i, f"Q{k}")][:].rearrange("p (l g b s) -> p l b g s", l=2, g=XG, b=BT)
                            dve.tensor_copy(qT[:, 0, k], src[:, 0])
                            dve.tensor_copy(qT[:, 1, k], src[:, 1]).then_inc(t_read, 1)
                    if i == 2 and has_tile(t + 1):
                        sum_q(t, 0)
                    if i == 2 and has_tile(t + 1):
                        sum_q(t, 1)
                        dve.wait_ge(link_q, 2 * (t + 2))
                        wait(dve, q_rs, t + 1)
                        dve.tensor_scalar(q_ms[:], q_ss[:], 1.0 / XD, 1e-6, ALU.mult, ALU.add).then_inc(q_msd, 1)
                    if i == 0 and has_tile(t + 1):
                        read_turned(t, i, "X", nT[:].rearrange("p l d n -> p (l d n)"), 2 * DK * P)
                    if has(j - 2):
                        dve.wait_ge(o_hi, j - 1)
                        b = (i - 2) % BT
                        dve.scalar_tensor_tensor(out=oT[:, 1, :, b * S:(b + 1) * S], in0=bank_o[:].rearrange("p k (g s) -> p (k g) s", g=XG),
                                                 scalar=1 / PS, in1=oT[:, 0, :, b * S:(b + 1) * S],
                                                 op0=ALU.mult, op1=ALU.subtract).then_inc(o_read, 1)
                    if i == 1 and has_tile(t + 1):
                        wait(dve, q_wd, 2 * (t + 1))
                        wait(dve, q_sqd, 2 * (t + 1))
                        for c in range(XKV):
                            dve.wait_ge(m_fill, projs.filled(t, i, f"Q{c}"))
                            dve.scalar_tensor_tensor(out=q_b[:, 512 * c:512 * (c + 1)], in0=bank_m[projs.bank(t, i, f"Q{c}")][:], scalar=1 / WS,
                                                     in1=w["bq"][:, 512 * c:512 * (c + 1)], op0=ALU.mult, op1=ALU.add).then_inc(m_read, 1)
            over_tiles(dve, tile)

        @block.tensor
        def _(pe):
            ident = w["ident"]

            def turn(t, i, name, parts):
                who, n = turns.held_before(t, i, name)
                if who:
                    wait(pe, T_READ[who], n)
                out = bank_t[turns.bank(t, i, name)]
                for n, part in enumerate(parts):
                    ins = pe.transpose(out[0:part.shape[-1], n * P:(n + 1) * P], part, ident[:])
                ins.then_inc(t_fill, 1)

            def project(t, i, name, terms):
                wait(pe, m_read, projs.held_before(t, i, name)[1])
                out = bank_m[projs.bank(t, i, name)]
                for n, (a, b) in enumerate(terms):
                    ins = pe.matmul(out[:, 0:b.shape[-1]], a, b, start=(n == 0), stop=(n == len(terms) - 1))
                ins.then_inc(m_fill, 1)

            def project_kv(t, i, name, c):
                project(t, i, f"{name}{c}", [(cT[i % 2][:, a, d, c, :], w["Wkv"][:, b, d, "KV".index(name), :])
                                             for d in range(DK) for a, b in ((0, 0), (1, 0), (0, 1))])

            def tile(t):
                for i in range(BT):
                    j = row(t, i)
                    if has(j):
                        pe.wait_ge(t_read, turns.emptied(*step_before(t, i), "C"))
                        project_kv(t, i, "K", 0)
                    if has(j):
                        project_kv(t, i, "K", 1)
                    if has(j - 1):
                        pe.wait_ge(k_lo, j)
                        for c in range(KT):
                            turn(t, i, f"K{c}", [k_hl[:, l, c, k * XD:(k + 1) * XD] for l in range(2) for k in range(XKV)])
                    if has(j):
                        project_kv(t, i, "V", 0)
                    if has(j - 1):
                        pe.wait_ge(t_read, turns.emptied(t, i, "K1"))
                        pe.wait_ge(k_end, j)
                        b = (i - 1) % BT
                        for k in range(XKV):
                            wait(pe, s_read, XKV * (j - 1) + k - 1)
                            for n, (x, y) in enumerate(((0, 0), (1, 0), (0, 1))):
                                ins = pe.matmul(bank_s[k % 2][:], qT[:, x, k, b].rearrange("p g s -> p (g s)"), kT[(i - 1) % 2][:, y, k, :],
                                                start=(n == 0), stop=(n == 2))
                            ins.then_inc(s_fill, 1)
                    if has(j - 2):
                        pe.wait_ge(p_lo, j - 1)
                        for half in range(2):
                            turn(t, i, f"P{half}", [p_hl[:, l, k, c * P:(c + 1) * P] for k in (2 * half, 2 * half + 1) for l in range(2) for c in range(KT)])
                        pe.wait_ge(p_ends, j - 1)
                        turn(t, i, "Pe", [p_end[:].rearrange("p k r -> p (k r)")])
                    if has(j):
                        project_kv(t, i, "V", 1)
                    if has(j + 1):
                        pe.wait_ge(c_lo, j + 2)
                        turn(t, i, "C", [c_hl[(i + 1) % 2][:, l, c, d * P:(d + 1) * P] for l in range(2) for d in range(DK) for c in range(KT)])
                    if i == 2 and has_tile(t - 1):
                        pe.wait_ge(o_read, BT * t)
                        project(t, i, "W", [(oT[:, a, h, :], w["Wo"][:, b, h, :]) for h in range(XH) for a, b in ((0, 0), (1, 0), (0, 1))])
                    if has(j - 2):
                        pe.wait_ge(t_read_act, turns.emptied(t, i, "P1"))
                        pe.wait_ge(t_read, turns.emptied(t, i, "Pe"))
                        wait(pe, o_read, j - 2)
                        b = (i - 2) % BT
                        pe.wait_ge(end_loaded[b], 16 * (t + 1 if i >= 2 else t))
                        for k in range(XKV):
                            for c in range(KT):
                                for n, (x, y) in enumerate(((0, 0), (1, 0), (0, 1))):
                                    pe.matmul(bank_o[:, k, :], v_hl[b][:, x, c, k * XD:(k + 1) * XD], pT[:, k, y, c, :],
                                              start=(c == 0 and n == 0), stop=False)
                            ins = pe.matmul(bank_o[:, k, :], v_end[b][:, k * XD:(k + 1) * XD], pT_end[:], start=False, stop=True)
                        ins.then_inc(o_fill, 1)
                    if i == 1 and has_tile(t + 1):
                        pe.wait_ge(t_read, turns.emptied(t, 0, "X"))
                        for c in range(XKV):
                            project(t, i, f"Q{c}", [(nT[:, a, d, :], w["Wq"][:, b, d, 512 * c:512 * (c + 1)])
                                                    for d in range(DK) for a, b in ((0, 0), (1, 0), (0, 1))])
                    if i == 0 and has_tile(t):
                        pe.wait_ge(q_lo, 2 * (t + 1))
                        for k in range(XKV):
                            turn(t, i, f"Q{k}", [q_hl[:, l, h * XD:(h + 1) * XD] for l in range(2) for h in range(k * XG, (k + 1) * XG)])
                    if i == 0 and has_tile(t + 1):
                        pe.wait_ge(n_lo, t + 2)
                        turn(t, i, "X", [n_hl[:, l, d * P:(d + 1) * P] for l in range(2) for d in range(DK)])
            over_tiles(pe, tile)


def cross_weights(nc, ctx):
    sb = lambda name, shape, dt=F32: ctx.enter_context(nc.sbuf_tensor(name, shape, dt))
    return {
        "Wq": sb("wq_hl", [P, 2, DK, XH * XD], F16), "Wkv": sb("wkv_hl", [P, 2, DK, 2, XKV * XD], F16),
        "Wo": sb("wo_hl", [P, 2, XH, HID], F16), "bq": sb("bq_all", [P, XH * XD]), "bk": sb("bk_all", [P, XKV * XD]),
        "wqk": sb("wqk", [P, XD]), "mask": sb("mask_all", [P, SE]), "cvec": sb("cvec", [P, HID]),
        "kT_last": sb("kT_last", [P, 2, XKV, P], F16),
        "v_last": nc.dram_tensor("v_last", [XKV * XR, P, XKV * XD], F16, kind="Internal").ap(),
    }


AH, AKV, AD = 32, 8, 64
AG = AH // AKV
AQ, AK = AH * AD, AKV * AD
AQKV = AQ + 2 * AK
AP2 = AKV // 2
ROT = AD // 2
PARTS = 4


def prepare_self(nc, io, w):
    with ExitStack() as ctx:
        sb = lambda name, shape, dt=F32: ctx.enter_context(nc.sbuf_tensor(name, shape, dt))
        sem = lambda name: ctx.enter_context(nc.semaphore(name))
        pst = [ctx.enter_context(nc.psum_tensor(f"p1_t{n}", [P, 2 * DK * P], F16)) for n in range(2)]
        NQ, NKV = AQ // P, AK // P
        NR = NQ + 2 * NKV
        raw = sb("raw_qkv", [P, NR, HID])
        hl = sb("hl_qkv", [P, 2, NR, HID], F16)
        raw_o = sb("raw_wo", [P, DK, AQ])
        kw = sb("kw", [P, AH])
        w_in, small_in, hi_done, lo_done, pe_done, read = (sem(n) for n in ("a_w_in", "a_small_in", "a_hi", "a_lo", "a_pe", "a_read"))
        o_in = sem("a_o_in")
        link = sem("a_link")
        block = ctx.enter_context(nc.Block())
        NO = AP2 * AG

        @block.sync
        def _(sp):
            for name, at, n in (("Wq", 0, NQ), ("Wk", NQ, NKV), ("Wv", NQ + NKV, NKV)):
                sp.dma_start(raw[:, at:at + n, :], io["a_" + name].rearrange("(c p) n -> p c n", p=P)).then_inc(w_in, 16)
            for name, at, n in (("bq", 0, AQ), ("bk", AQ, AK), ("bv", AQ + AK, AK)):
                sp.dma_start(w["b"][:, at:at + n], spread(io["a_" + name])).then_inc(small_in, 16)
            sp.dma_start(w["bo"][:], spread(io["a_bo"])).then_inc(small_in, 16)
            sp.dma_start(kw[:], spread(io["a_kw"])).then_inc(small_in, 16)
            for b in range(BT):
                for n in range(2):
                    for half in range(2):
                        sp.dma_start(w["rot"][b * S:(b + 1) * S, n, half, :], io["rope"][n]).then_inc(small_in, 16)
            sp.dma_start(raw_o[:], io["a_Wo"].rearrange("(c p) n -> p c n", p=P)).then_inc(o_in, 16)

        def of_wo(ap, c, k):
            return ap[:, c, k * 2 * AG * AD:(k + 1) * 2 * AG * AD].rearrange("p (e g d) -> p g e d", e=2, g=AG)

        def to_wo(l, c, k):
            return (hl[:, l, 0:NQ, :].rearrange("p c n -> p (c n)").rearrange("p (c n) -> p c n", c=DK)
                    [:, c, k * 2 * AG * AD:(k + 1) * 2 * AG * AD].rearrange("p (g e d) -> p g e d", g=AG, e=2))

        @block.scalar
        def _(act):
            act.wait_ge(w_in, 48)
            act.activation(hl[:, 0], raw[:], ACT.Copy, scale=WS).then_inc(hi_done, 1)
            act.wait_ge(o_in, 16)
            act.wait_ge(pe_done, NR)
            for c in range(DK):
                for k in range(AP2):
                    ins = act.activation(to_wo(0, c, k), of_wo(raw_o, c, k), ACT.Copy, scale=WS)
            ins.then_inc(hi_done, 1)

        @block.gpsimd
        def _(pool):
            pool.memset(w["causal"][:], 0.0).then_inc(link, 1)
            for n in range(BT * AG // AG):
                pool.wait_ge(link, n + 1)
                part = w["causal"][n * S:(n + 1) * S, :]
                pool.affine_select(out=part, in_=part, compare_op=ALU.is_ge, fill=-1e30, base=0, pattern=[[-1, S]],
                                   channel_multiplier=1).then_inc(link, 1)

        @block.vector
        def _(dve):
            dve.wait_ge(hi_done, 1)
            dve.scalar_tensor_tensor(out=hl[:, 1], in0=raw[:], scalar=WS, in1=hl[:, 0], op0=ALU.mult, op1=ALU.subtract).then_inc(lo_done, 1)
            dve.wait_ge(small_in, 16 * (5 + BT * 4))
            dve.tensor_scalar(w["rot"][:, 1, 0, :], w["rot"][:, 1, 0, :], -1.0, None, ALU.mult).then_inc(lo_done, 1)
            dve.wait_ge(lo_done, 2)
            for n in range(2):
                dve.tensor_tensor(w["rot_q"][:, n], w["rot"][:, n].rearrange("p a f -> p (a f)").unsqueeze(1).broadcast_to([P, AH, AD]),
                                  kw[:].unsqueeze(2).broadcast_to([P, AH, AD]), ALU.mult)
            for r in range(NR):
                dve.wait_ge(pe_done, r + 1)
                dve.tensor_copy(w["Wqkv"][:, :, :, r * P:(r + 1) * P], pst[r % 2][:].rearrange("p (l c n) -> p l c n", l=2, c=DK)).then_inc(read, 1)
            dve.wait_ge(hi_done, 2)
            for c in range(DK):
                for k in range(AP2):
                    for e in range(2):
                        ins = dve.scalar_tensor_tensor(out=to_wo(1, c, k)[:, :, e], in0=of_wo(raw_o, c, k)[:, :, e], scalar=WS,
                                                       in1=to_wo(0, c, k)[:, :, e], op0=ALU.mult, op1=ALU.subtract)
            ins.then_inc(lo_done, 1)
            for r in range(NO):
                dve.wait_ge(pe_done, NR + r + 1)
                dve.tensor_copy(w["Wo"][:, :, r, :].rearrange("p l (c n) -> p l c n", c=DK),
                                pst[(NR + r) % 2][:].rearrange("p (l c n) -> p l c n", l=2, c=DK)).then_inc(read, 1)

        @block.tensor
        def _(pe):
            pe.wait_ge(lo_done, 1)
            for r in range(NR):
                wait(pe, read, r - 1)
                for l in range(2):
                    for c in range(DK):
                        ins = pe.transpose(pst[r % 2][:, (l * DK + c) * P:(l * DK + c + 1) * P], hl[:, l, r, c * P:(c + 1) * P], w["ident"][:])
                ins.then_inc(pe_done, 1)
            pe.wait_ge(lo_done, 3)
            wo = hl[:, :, 0:NQ, :].rearrange("p l c n -> p l (c n)").rearrange("p l (c r m) -> p l c r m", c=DK, r=NO)
            for r in range(NO):
                wait(pe, read, NR + r - 1)
                for l in range(2):
                    for c in range(DK):
                        ins = pe.transpose(pst[(NR + r) % 2][:, (l * DK + c) * P:(l * DK + c + 1) * P], wo[:, l, c, r, :], w["ident"][:])
                ins.then_inc(pe_done, 1)


def self_weights(nc, ctx):
    sb = lambda name, shape, dt=F32: ctx.enter_context(nc.sbuf_tensor(name, shape, dt))
    return {
        "Wqkv": sb("a_wqkv", [P, 2, DK, AQKV], F16), "Wo": sb("a_wo", [P, 2, AP2 * AG, HID], F16), "b": sb("a_b", [P, AQKV]),
        "bo": sb("a_bo", [P, HID]), "rot": sb("a_rot", [P, 2, 2, ROT]), "rot_q": sb("a_rot_q", [P, 2, AH, AD]),
        "causal": sb("a_causal", [P, S]), 
        "v_rows": nc.dram_tensor("v_rows", [2, BT, S, AK], F16, kind="Internal").ap(),
    }


def self_attention(nc, io, sb_x, w, tiles):
    with ExitStack() as ctx:
        sb = lambda name, shape, dt=F32: ctx.enter_context(nc.sbuf_tensor(name, shape, dt))
        sem = lambda name: ctx.enter_context(nc.semaphore(name))
        bank_t = [ctx.enter_context(nc.psum_tensor(f"a_turn{n}", [P, 1024], F16)) for n in range(2)]
        bank_m = [ctx.enter_context(nc.psum_tensor(f"a_proj{n}", [P, 512], F32)) for n in range(2)]
        bank_s = ctx.enter_context(nc.psum_tensor("a_score", [P, AKV, BT, S], F32))
        bank_o = [ctx.enter_context(nc.psum_tensor(f"a_sum{n}", [P, BT, AG * S], F32)) for n in range(2)]
        n_st, n_ag, n_r = sb("a_st", [P, 6]), sb("a_ag", [P, 2]), sb("a_r", [P, 2])
        n_x, n_hl = sb("a_n", [P, HID]), sb("a_nhl", [P, 2, HID], F16)
        nT = sb("a_nT", [P, 2, DK, P], F16)
        qk = sb("a_qk", [P, AH + AKV, 2, ROT])
        qk_c = sb("a_qkc", [P, AH + AKV, 2, ROT])
        qk_s = sb("a_qks", [P, AH + AKV, 2, ROT])
        q_hl = sb("a_qhl", [P, AH, 2, AD], F16)
        k_hl = sb("a_khl", [P, AKV, 2, 2, AD], F16)
        v_f = sb("a_vf", [P, AK])
        v_hl = sb("a_vhl", [P, 2, AK], F16)
        v4 = sb("a_v4", [P, BT, AK], F16)
        qT = sb("a_qT", [P, AKV, BT, AG, S], F16)
        kT = sb("a_kT", [P, 2, AKV, P], F16)
        s_f = sb("a_s", [P, AKV * BT, S])
        s_max, p_sum, p_inv, p_scl = (sb(n, [P, AKV * BT]) for n in ("a_smax", "a_psum", "a_pinv", "a_pscl"))
        p4 = sb("a_p4", [P, AKV * BT, PARTS, S], F16)
        pT = sb("a_pT", [P, AKV, BT, AG * S], F16)
        oT = sb("a_oT", [P, 2, AP2, AG, BT, S], F16)

        t_fill, t_read, m_fill, m_read, s_fill, s_read, o_fill, o_read = (
            sem("a_" + n) for n in ("t_fill", "t_read", "m_fill", "m_read", "s_fill", "s_read", "o_fill", "o_read"))
        v_saved, v_here = sem("a_v_saved"), sem("a_v_here")
        n_hi, q_hi, v_hi, exp_done, p_hi, o_hi = (sem("a_" + n) for n in ("n_hi", "q_hi", "v_hi", "exp_done", "p_hi", "o_hi"))
        n_rs, n_lo, q_lo, c_done, p_nd, p_lo, p_lo2 = (sem("a_" + n) for n in ("n_rs", "n_lo", "q_lo", "c_done", "p_nd", "p_lo", "p_lo2"))
        q_lo1 = sem("a_q_lo1")
        n_msd, n_xd, v_lo, rot_done, s_maxd, s_sub, p_invd = (
            sem("a_" + n) for n in ("n_msd", "n_xd", "v_lo", "rot_done", "s_maxd", "s_sub", "p_invd"))
        link_n, link_r, link_p, link_i = (sem("a_" + n) for n in ("link_n", "link_r", "link_p", "link_i"))
        has = lambda t: not isinstance(t, int) or 0 <= t < tiles

        def order_t(t, i):
            out = []
            out += ["K0", "K1"] if has(t) else [None] * 2
            out += ["Q0", "Q1", "Q2", "Q3"] if has(t) else [None] * 4
            out += ["P0", "P1", "P2", "P3"] if has(t - 1) else [None] * 4
            out += ["X"] if has(t + 2) else [None]
            return out + [None]

        def order_m(t, i):
            out = []
            out += [f"M{n}" for n in range(6)] if has(t + 1) else [None] * 6
            out += ["W"] if has(t - 1) else [None]
            return out + [None]

        passed_dve, passed_pool, passed_sp = (sem(n) for n in ("a_passed_dve", "a_passed_pool", "a_passed_sp"))
        t_read_act = sem("a_t_read_act")
        T_READ = {"act": t_read_act, "dve": t_read}
        turns = BankCount(order_t, tiles, 1, 2, 2, emptier=lambda name: "act" if name[0] in "KP" else "dve")
        projs = BankCount(order_m, tiles, 1, 2, 2)
        block = ctx.enter_context(nc.Block())

        def over_tiles(eng, tile):
            for t in (-2, -1, 0, 1):
                tile(t)
            with eng.Fori(2, tiles - 2) as t:
                tile(t)
            for t in (tiles - 2, tiles - 1, tiles):
                tile(t)

        @block.sync
        def _(sp):
            def tile(t):
                if has(t + 1):
                    sp.wait_ge(v_lo, t + 2)
                    wait(sp, v_here, 16 * PARTS * (t + 1))
                    sp.dma_start(w["v_rows"].rearrange("l b s n -> (b s) l n"), v_hl[:]).then_inc(v_saved, 16)
                    wait_apart(sp, v_saved, 16 * (t + 2), passed_sp)
                    wait(sp, o_fill, AP2 * (t + 1))
                    for r, part in enumerate((0, 0, 1, 1)):
                        sp.dma_start(v4[r * S:(r + 1) * S], w["v_rows"][part].rearrange("b s n -> s b n")).then_inc(v_here, 16)
            over_tiles(sp, tile)

        @block.gpsimd
        def _(pool):
            def tile(t):
                if has(t + 2):
                    pool.wait_ge(n_msd, t + 3)
                    wait(pool, n_xd, t + 2)
                    pool.tensor_tensor(n_r[:, 0:1], n_r[:, 1:2], w["minus_half"][:, 0:1], ALU.pow).then_inc(n_rs, 1)
                if has(t + 1):
                    pool.wait_ge(m_read, projs.filled(t, 0, "M3"))
                    wait(pool, q_lo1, t + 1)
                    pool.tensor_tensor(qk_c[:, 0:AH].rearrange("p h a f -> p h (a f)"), qk[:, 0:AH].rearrange("p h a f -> p h (a f)"),
                                       w["rot_q"][:, 0], ALU.mult).then_inc(c_done, 1)
                if has(t + 1):
                    pool.wait_ge(m_read, projs.filled(t, 0, "M3"))
                    for half in range(2):
                        pool.tensor_tensor(qk_s[:, 0:AH, half, :], qk[:, 0:AH, 1 - half, :], w["rot_q"][:, 1, :, half * ROT:(half + 1) * ROT],
                                           ALU.mult).then_inc(c_done, 1)
                if has(t):
                    pool.wait_ge(p_invd, t + 1)
                    pool.tensor_tensor(s_f[:], s_f[:], p_scl[:].unsqueeze(2).broadcast_to([P, AKV * BT, S]), ALU.mult).then_inc(p_nd, 1)
                if has(t):
                    pool.wait_ge(p_hi, 2 * t + 1)
                    pool.tensor_tensor(p4[:, :, 1, :], s_f[:], p4[:, :, 0, :], ALU.subtract).then_inc(p_lo, 1)
                if has(t + 2):
                    pool.wait_ge(n_hi, t + 3)
                    wait(pool, t_fill, turns.filled(t - 1, 0, "X") if has(t + 1) else 0)
                    pool.tensor_tensor(n_hl[:, 1], n_x[:], n_hl[:, 0], ALU.subtract).then_inc(n_lo, 1)
            over_tiles(pool, tile)

        @block.scalar
        def _(act):
            def read_turned(t, name, out):
                act.wait_ge(t_fill, turns.filled(t, 0, name))
                act.activation(out, bank_t[turns.bank(t, 0, name)][:], ACT.Copy).then_inc(t_read_act, 1)

            def tile(t):
                if has(t):
                    for n in range(2):
                        read_turned(t, f"K{n}", kT[:, n].rearrange("p k n -> p (k n)"))
                if has(t + 2):
                    act.wait_ge(n_xd, t + 3)
                    wait(act, t_fill, turns.filled(t - 1, 0, "X") if has(t + 1) else 0)
                    act.activation(n_hl[:, 0], n_x[:], ACT.Copy).then_inc(n_hi, 1)
                if has(t):
                    act.wait_ge(s_sub, t + 1)
                    act.activation(s_f[:], s_f[:], ACT.Exp).then_inc(exp_done, 1)
                if has(t - 1):
                    for n in (0, 1):
                        read_turned(t, f"P{n}", pT[:, 2 * n:2 * n + 2].rearrange("p k b n -> p (k b n)"))
                if has(t - 1):
                    for n in (2, 3):
                        read_turned(t, f"P{n}", pT[:, 2 * n:2 * n + 2].rearrange("p k b n -> p (k b n)"))
                if has(t + 1):
                    act.wait_ge(m_read, projs.filled(t, 0, "M5"))
                    wait(act, v_saved, 16 * (t + 1))
                    act.activation(v_hl[:, 0], v_f[:], ACT.Copy).then_inc(v_hi, 1)
                if has(t - 1):
                    for n in (0, 1):
                        act.wait_ge(o_fill, AP2 * (t - 1) + n + 1)
                        if has(t - 2):
                            act.wait_ge(m_fill, projs.filled(t - 1, 0, "W"))
                        act.activation(oT[:, 0, n], bank_o[n % 2][:].rearrange("p b (g s) -> p g b s", g=AG), ACT.Copy, scale=1 / PS
                                       ).then_inc(o_hi, 1)
                if has(t):
                    act.wait_ge(p_nd, t + 1)
                    wait(act, t_fill, turns.filled(t, 0, "P3") if has(t - 1) else 0)
                    for part in (0, 2):
                        act.activation(p4[:, :, part, :], s_f[:], ACT.Copy).then_inc(p_hi, 1)
                if has(t - 1):
                    for n in (2, 3):
                        act.wait_ge(o_fill, AP2 * (t - 1) + n + 1)
                        if has(t - 2):
                            act.wait_ge(m_fill, projs.filled(t - 1, 0, "W"))
                        act.activation(oT[:, 0, n], bank_o[n % 2][:].rearrange("p b (g s) -> p g b s", g=AG), ACT.Copy, scale=1 / PS
                                       ).then_inc(o_hi, 1)
                if has(t + 1):
                    act.wait_ge(rot_done, t + 2)
                    for n in range(2):
                        act.activation(k_hl[:, :, 0, n, :], qk_c[:, AH:].rearrange("p h a f -> p h (a f)"), ACT.Copy).then_inc(q_hi, 1)
                if has(t + 1):
                    act.wait_ge(rot_done, t + 2)
                    act.activation(q_hl[:, :, 0, :], qk_c[:, 0:AH].rearrange("p h a f -> p h (a f)"), ACT.Copy).then_inc(q_hi, 1)
                if has(t):
                    act.wait_ge(p_lo, t + 1)
                    act.activation(p4[:, :, 3, :], p4[:, :, 1, :], ACT.Copy).then_inc(p_lo2, 1)
            over_tiles(act, tile)

        @block.vector
        def _(dve):
            def read_turned(t, name, out):
                bank, n = turns.bank(t, 0, name), turns.filled(t, 0, name)
                dve.wait_ge(t_fill, n)
                dve.tensor_copy(out, bank_t[bank][:, 0:out.shape[1]]).then_inc(t_read, 1)

            def tile_of_x(t):
                return sb_x[:, bass.ds(t, 1), :].rearrange("p o n -> p (o n)")

            def tile(t):
                if has(t + 2):
                    x_t = tile_of_x(t + 2)
                    dve.bn_stats(n_st[:], x_t).then_inc(link_n, 1)
                    wait_apart(dve, link_n, 2 * (t + 2) + 1, passed_dve)
                    dve.bn_aggr(n_ag[:], n_st[:]).then_inc(link_n, 1)
                    dve.wait_ge(link_n, 2 * (t + 2) + 2)
                    wait(dve, n_rs, t + 2)
                    dve.tensor_scalar(n_r[:, 1:2], n_ag[:, 1:2], 1e-5, None, ALU.add).then_inc(n_msd, 1)
                if has(t + 1):
                    wait(dve, rot_done, t + 1)
                    wait(dve, c_done, 3 * (t + 1))
                    for c in range(6):
                        bank, n = projs.bank(t, 0, f"M{c}"), projs.filled(t, 0, f"M{c}")
                        dve.wait_ge(m_fill, n)
                        if c == 5:
                            wait(dve, v_lo, t + 1)
                            wait(dve, v_hi, t + 1)
                        out = qk[:].rearrange("p h a f -> p (h a f)")[:, 512 * c:512 * (c + 1)] if c < 5 else v_f[:]
                        dve.scalar_tensor_tensor(out=out, in0=bank_m[bank][:], scalar=1 / WS, in1=w["b"][:, 512 * c:512 * (c + 1)],
                                                 op0=ALU.mult, op1=ALU.add).then_inc(m_read, 1)
                if has(t):
                    for k in range(4):
                        bank, n = turns.bank(t, 0, f"Q{k}"), turns.filled(t, 0, f"Q{k}")
                        dve.wait_ge(t_fill, n)
                        src = bank_t[bank][:].rearrange("p (k g b s) -> p k b g s", k=2, g=AG, b=BT)
                        dve.tensor_copy(qT[:, 2 * k], src[:, 0])
                        dve.tensor_copy(qT[:, 2 * k + 1], src[:, 1]).then_inc(t_read, 1)
                if has(t + 2):
                    dve.wait_ge(n_rs, t + 3)
                    wait(dve, n_lo, t + 2)
                    dve.tensor_scalar(n_x[:], tile_of_x(t + 2), n_ag[:, 0:1], n_r[:, 0:1], ALU.subtract, ALU.mult).then_inc(n_xd, 1)
                if has(t):
                    wait(dve, p_lo, t)
                    dve.wait_ge(s_fill, t + 1)
                    dve.scalar_tensor_tensor(out=s_f[:], in0=bank_s[:].rearrange("p k b s -> p (k b) s"), scalar=AD ** -0.5,
                                             in1=w["causal"][:].unsqueeze(1).broadcast_to([P, AKV * BT, S]),
                                             op0=ALU.mult, op1=ALU.add).then_inc(s_read, 1)
                if has(t):
                    dve.wait_ge(s_read, t + 1)
                    dve.tensor_reduce(s_max[:], s_f[:], AX.X, ALU.max).then_inc(s_maxd, 1)
                if has(t):
                    dve.wait_ge(s_maxd, t + 1)
                    dve.tensor_tensor(s_f[:], s_f[:], s_max[:].unsqueeze(2).broadcast_to([P, AKV * BT, S]), ALU.subtract).then_inc(s_sub, 1)
                if has(t):
                    dve.wait_ge(exp_done, t + 1)
                    dve.tensor_reduce(p_sum[:], s_f[:], AX.X, ALU.add).then_inc(link_p, 1)
                    dve.wait_ge(link_p, t + 1)
                    dve.reciprocal(p_inv[:], p_sum[:]).then_inc(link_r, 1)
                    dve.wait_ge(link_r, t + 1)
                    wait(dve, p_nd, t)
                    dve.tensor_scalar(p_scl[:], p_inv[:], PS, None, ALU.mult).then_inc(p_invd, 1)
                if has(t + 1):
                    dve.wait_ge(m_read, projs.filled(t, 0, "M4"))
                    for half in range(2):
                        dve.tensor_tensor(qk_s[:, AH:, half, :], qk[:, AH:, 1 - half, :],
                                          w["rot"][:, 1, half, :].unsqueeze(1).broadcast_to([P, AKV, ROT]), ALU.mult)
                    dve.tensor_tensor(qk_c[:, AH:].rearrange("p h a f -> p h (a f)"), qk[:, AH:].rearrange("p h a f -> p h (a f)"),
                                      w["rot"][:, 0].rearrange("p a f -> p (a f)").unsqueeze(1).broadcast_to([P, AKV, AD]), ALU.mult).then_inc(link_i, 1)
                if has(t - 1):
                    for n in (0, 1):
                        dve.wait_ge(o_hi, AP2 * (t - 1) + n + 1)
                        for g in range(AG):
                            ins = dve.scalar_tensor_tensor(out=oT[:, 1, n, g], in0=bank_o[n % 2][:, :, g * S:(g + 1) * S], scalar=1 / PS,
                                                           in1=oT[:, 0, n, g], op0=ALU.mult, op1=ALU.subtract)
                        ins.then_inc(o_read, 1)
                if has(t + 1):
                    dve.wait_ge(link_i, t + 2)
                    dve.wait_ge(c_done, 3 * (t + 2))
                    dve.tensor_tensor(qk_c[:].rearrange("p h a f -> p (h a f)"), qk_c[:].rearrange("p h a f -> p (h a f)"),
                                      qk_s[:].rearrange("p h a f -> p (h a f)"), ALU.add).then_inc(rot_done, 1)
                if has(t - 1):
                    for n in (2, 3):
                        dve.wait_ge(o_hi, AP2 * (t - 1) + n + 1)
                        for g in range(AG):
                            ins = dve.scalar_tensor_tensor(out=oT[:, 1, n, g], in0=bank_o[n % 2][:, :, g * S:(g + 1) * S], scalar=1 / PS,
                                                           in1=oT[:, 0, n, g], op0=ALU.mult, op1=ALU.subtract)
                        ins.then_inc(o_read, 1)
                if has(t + 2):
                    read_turned(t, "X", nT[:].rearrange("p l d n -> p (l d n)"))
                if has(t + 1):
                    dve.wait_ge(v_hi, t + 2)
                    wait(dve, v_saved, 16 * (t + 1))
                    dve.tensor_tensor(v_hl[:, 1], v_f[:], v_hl[:, 0], ALU.subtract).then_inc(v_lo, 1)
                if has(t - 1):
                    bank, n = projs.bank(t, 0, "W"), projs.filled(t, 0, "W")
                    dve.wait_ge(m_fill, n)
                    x_t = sb_x[:, bass.ds(t - 1, 1), :].rearrange("p o n -> p (o n)")
                    dve.scalar_tensor_tensor(out=x_t, in0=bank_m[bank][:, 0:HID], scalar=1 / WS, in1=x_t,
                                             op0=ALU.mult, op1=ALU.add).then_inc(m_read, 1)
                    dve.wait_ge(m_read, n)
                    dve.tensor_tensor(x_t, x_t, w["bo"][:], ALU.add)
                if has(t + 1):
                    dve.wait_ge(q_hi, 3 * (t + 2))
                    q_r = qk_c[:].rearrange("p h a f -> p h (a f)")
                    dve.tensor_tensor(k_hl[:, :, 1, 0, :], q_r[:, AH:], k_hl[:, :, 0, 0, :], ALU.subtract)
                    dve.tensor_tensor(k_hl[:, :, 1, 1, :], q_r[:, AH:], k_hl[:, :, 0, 0, :], ALU.subtract).then_inc(q_lo, 1)
                if has(t + 1):
                    dve.wait_ge(q_hi, 3 * (t + 2))
                    q_r = qk_c[:].rearrange("p h a f -> p h (a f)")
                    dve.tensor_tensor(q_hl[:, :, 1, :], q_r[:, 0:AH], q_hl[:, :, 0, :], ALU.subtract).then_inc(q_lo1, 1)
            over_tiles(dve, tile)

        @block.tensor
        def _(pe):
            ident = w["ident"]

            def take(ring, t, name, read):
                who, n = ring.held_before(t, 0, name)
                if who in read:
                    wait(pe, read[who], n)
                return ring.bank(t, 0, name)

            def turn(t, name, parts):
                out = bank_t[take(turns, t, name, T_READ)]
                for n, part in enumerate(parts):
                    ins = pe.transpose(out[:, n * P:(n + 1) * P], part, ident[:])
                ins.then_inc(t_fill, 1)

            def project(t, name, terms):
                out = bank_m[take(projs, t, name, {0: m_read})]
                for n, (a, b) in enumerate(terms):
                    ins = pe.matmul(out[:, 0:b.shape[-1]], a, b, start=(n == 0), stop=(n == len(terms) - 1))
                ins.then_inc(m_fill, 1)

            def sum_v(t, n):
                pe.wait_ge(t_read_act, turns.emptied(t, 0, f"P{n}"))
                wait(pe, o_read, AP2 * (t - 1) + n - 1)
                for e in range(2):
                    k = 2 * n + e
                    for b in range(BT):
                        ins = pe.matmul(bank_o[n % 2][e * AD:(e + 1) * AD, b, :], v4[:, b, k * AD:(k + 1) * AD], pT[:, k, b, :],
                                        start=True, stop=True)
                ins.then_inc(o_fill, 1)

            def apply_wo(t, n):
                pe.wait_ge(o_read, AP2 * (t - 1) + n + 1)
                for g in range(AG):
                    for a, b in ((0, 0), (1, 0), (0, 1)):
                        ins = pe.matmul(bank_m[projs.bank(t, 0, "W")][:, 0:HID], oT[:, a, n, g].rearrange("p b s -> p (b s)"),
                                        w["Wo"][:, b, n * AG + g, :], start=(n == 0 and g == 0 and a + b == 0), stop=(n == AP2 - 1 and g == AG - 1 and b == 1))
                if n == AP2 - 1:
                    ins.then_inc(m_fill, 1)

            def tile(t):
                if has(t):
                    pe.wait_ge(q_lo, t + 1)
                    for n in range(2):
                        turn(t, f"K{n}", [k_hl[:, k, n].rearrange("p l d -> p (l d)") for k in range(AKV)])
                if has(t + 1):
                    pe.wait_ge(t_read, turns.emptied(t - 1, 0, "X"))
                    for c in range(6):
                        project(t, f"M{c}", [(nT[:, a, d, :], w["Wqkv"][:, b, d, 512 * c:512 * (c + 1)])
                                             for d in range(DK) for a, b in ((0, 0), (1, 0), (0, 1))])
                if has(t):
                    pe.wait_ge(q_lo1, t + 1)
                    for n in range(4):
                        turn(t, f"Q{n}", [q_hl[:, h].rearrange("p l d -> p (l d)") for h in range(8 * n, 8 * n + 8)])
                if has(t):
                    pe.wait_ge(t_read, turns.emptied(t, 0, "Q3"))
                    pe.wait_ge(t_read_act, turns.emptied(t, 0, "K1"))
                    wait(pe, s_read, t)
                    for k in range(AKV):
                        for b in range(BT):
                            for n in range(2):
                                ins = pe.matmul(bank_s[:, k, b, :], qT[:, k, b].rearrange("p g s -> p (g s)"), kT[:, n, k, b * S:(b + 1) * S],
                                                start=(n == 0), stop=(n == 1))
                    ins.then_inc(s_fill, 1)
                if has(t - 1):
                    pe.wait_ge(p_lo2, t)
                    for n in range(4):
                        turn(t, f"P{n}", [p4[:, k * BT + b].rearrange("p r s -> p (r s)") for k in (2 * n, 2 * n + 1) for b in range(BT)])
                if has(t - 1):
                    pe.wait_ge(v_here, 16 * PARTS * t)
                    wait(pe, m_read, projs.held_before(t, 0, "W")[1])
                    sum_v(t, 0)
                    sum_v(t, 1)
                if has(t - 1):
                    apply_wo(t, 0)
                    sum_v(t, 2)
                if has(t - 1):
                    apply_wo(t, 1)
                    sum_v(t, 3)
                if has(t - 1):
                    apply_wo(t, 2)
                    apply_wo(t, 3)
                if has(t + 2):
                    pe.wait_ge(n_lo, t + 3)
                    turn(t, "X", [n_hl[:, l, d * P:(d + 1) * P] for l in range(2) for d in range(DK)])
            over_tiles(pe, tile)


FF, NE, ER = 704, 8, 16
FC = -(-FF // P)
ERS = NE * ER
SCALING = 2.0
TOP = 2
EPB = 4
LR = 32
STACK = 3 * 2 * ER
TB = 4
NB = TB * P


def rows_of(f):
    return min(P, FF - f * P)


def ffn_weights(nc, ctx, tiles):
    sb = lambda name, shape, dt=F32: ctx.enter_context(nc.sbuf_tensor(name, shape, dt))
    dram = lambda name, shape, dt: nc.dram_tensor(name, shape, dt, kind="Internal").ap()
    return {
        "Wgu": sb("f_wgu", [P, 2, DK, 2, FF], F16), "B": sb("f_B", [STACK, 2, NE, FF], F16), "WdT": sb("f_WdT", [P, FC, HID]),
        "AdT": sb("f_AdT", [P, FC, NE, LR]), "BdT": sb("f_BdT", [P, 2, 2, HID], F16),
        "nT": sb("f_nT", [P, 2, DK, tiles * P], F16), "weT": sb("f_weT", [P, 2, tiles * P]),
        "b_rows": dram("b_rows", [2, 2, 2, ER + ERS, FF], F16), "a_rows": dram("a_rows", [2, 2, ER + ERS, tiles * P], F16),
    }


def prepare_ffn(nc, io, w, tiles):
    with ExitStack() as ctx:
        sb = lambda name, shape, dt=F32: ctx.enter_context(nc.sbuf_tensor(name, shape, dt))
        sem = lambda name: ctx.enter_context(nc.semaphore(name))
        bank = [ctx.enter_context(nc.psum_tensor(f"p2_t{n}", [P, 1024], F16)) for n in range(2)]
        bank_f = [ctx.enter_context(nc.psum_tensor(f"p2_f{n}", [P, 512], F32)) for n in range(2)]
        raw = sb("raw_gu", [P, 2, FC, HID])
        hl = sb("hl_gu", [P, 2, 2, FC, HID], F16)
        raw_b = sb("raw_b", [P, 2, FC, NE, ER])
        hl_b = sb("hl_b", [P, 2, 2, FC, ERS], F16)
        bT = sb("bT", [P, 2, 2, 2, FF], F16)
        raw_bd = sb("raw_bd", [P, DK, NE, LR])
        hl_bd = sb("hl_bd", [P, 2, DK, NE * LR], F16)
        raw_d = sb("raw_d", [P, DK, FF])
        raw_ad = sb("raw_ad", [ERS, FF])
        ident32 = sb("ident32", [P, P])
        zero = w["nT"][0:ER, 0, 0, :]
        loads, loads_gu, hi, lo, fill, read, fill_f, read_f, saved, stacked, setup = (
            sem("f0_" + n) for n in ("loads", "loads_gu", "hi", "lo", "fill", "read", "fill_f", "read_f", "saved", "stacked", "setup"))
        block = ctx.enter_context(nc.Block())

        @block.sync
        def _(sp):
            sp.wait_ge(setup, 2)

            def load(dst, src, done=loads):
                sp.dma_start(dst, src).then_inc(done, 16)

            full = FF // P
            for v, name in enumerate(("f_Wg", "f_Wu")):
                load(raw[:, v, 0:full, :], io[name][0:full * P].rearrange("(c p) n -> p c n", p=P), loads_gu)
                load(raw[0:FF - full * P, v, full, :], io[name][full * P:FF], loads_gu)
            for v, name in enumerate(("f_Bg", "f_Bu")):
                for c in range(FC):
                    m = rows_of(c)
                    load(raw_b[0:m, v, c, :, :], io[name][:, c * P:c * P + m].rearrange("e p r -> p e r"))
            for c in range(DK):
                load(raw_bd[:, c, :, 0:ER], io["f_Bd"][:, c * P:(c + 1) * P].rearrange("e p r -> p e r"))
            load(raw_d[:], io["f_Wd"].rearrange("(c p) n -> p c n", p=P))
            load(raw_ad[:], io["f_Ad"].rearrange("e r n -> (e r) n"))
            for v in range(2):
                for a in range(2):
                    sp.dma_start(w["a_rows"][v, a, 0:ER, :], zero[:, 0:tiles * P]).then_inc(saved, 16)
                    for b in range(2):
                        sp.dma_start(w["b_rows"][v, a, b, 0:ER, :], zero[:, 0:FF]).then_inc(saved, 16)
            sp.wait_ge(read, 4 * FC)
            for v in range(2):
                for a in range(2):
                    sp.dma_start(w["b_rows"][v, a, :, ER:].rearrange("l r n -> r l n"), bT[:, v, a]).then_inc(saved, 16)
            sp.wait_ge(saved, 16 * 16)
            for v in range(2):
                for r, part in enumerate((0, 0, 1)):
                    for a, first in ((1, 0), (0, ER)):
                        at = r * 2 * ER + (0 if a else ER)
                        sp.dma_start(w["B"][at:at + ER, v], w["b_rows"][v, a, part, first:first + ERS].rearrange("(e r) n -> r e n", r=ER)
                                     ).then_inc(stacked, 16)
            sp.wait_ge(stacked, 16 * 12)

        total = 16 * (2 * FC + DK + 2)

        @block.gpsimd
        def _(pool):
            pool.memset(raw_bd[:], 0.0).then_inc(setup, 1)
            pool.memset(zero, 0.0).then_inc(setup, 1)
            pool.memset(ident32[:], 0.0).then_inc(setup, 1)
            pool.wait_ge(setup, 3)
            pool.affine_select(out=ident32[:], in_=ident32[:], compare_op=ALU.not_equal, fill=1.0, base=0,
                               pattern=[[-1, P]], channel_multiplier=1).then_inc(setup, 1)
            pool.memset(w["AdT"][:], 0.0).then_inc(setup, 1)

        full, rest = FF // P, FF - FF // P * P

        @block.scalar
        def _(act):
            act.wait_ge(loads_gu, 16 * 4)
            act.activation(hl[:, 0, :, 0:full], raw[:, :, 0:full], ACT.Copy, scale=WS)
            act.activation(hl[0:rest, 0, :, full], raw[0:rest, :, full], ACT.Copy, scale=WS).then_inc(hi, 1)
            act.wait_ge(loads, total)
            act.activation(hl_b[:, 0, :, 0:full], raw_b[:, :, 0:full].rearrange("p v c e r -> p v c (e r)"), ACT.Copy, scale=WS * SCALING)
            act.activation(hl_b[0:rest, 0, :, full], raw_b[0:rest, :, full].rearrange("p v e r -> p v (e r)"), ACT.Copy, scale=WS * SCALING).then_inc(hi, 1)
            act.activation(hl_bd[:, 0].rearrange("p c n -> p (c n)"), raw_bd[:].rearrange("p c e r -> p (c e r)"), ACT.Copy, scale=SCALING).then_inc(hi, 1)

        @block.vector
        def _(dve):
            dve.wait_ge(hi, 1)
            for v in range(2):
                for p, a, b in ((P, 0, full), (rest, full, FC)):
                    ins = dve.scalar_tensor_tensor(out=hl[0:p, 1, v, a:b], in0=raw[0:p, v, a:b], scalar=WS, in1=hl[0:p, 0, v, a:b],
                                                   op0=ALU.mult, op1=ALU.subtract)
            ins.then_inc(lo, 1)
            n = 0
            for v in range(2):
                for f in range(FC):
                    m = rows_of(f)
                    dve.wait_ge(fill, n + 1)
                    src = bank[n % 2][:, 0:2 * DK * m].rearrange("p (l c n) -> p l c n", l=2, c=DK)
                    dve.tensor_copy(w["Wgu"][:, :, :, v, f * P:f * P + m], src).then_inc(read, 1)
                    n += 1
            dve.wait_ge(hi, 3)
            for v in range(2):
                for p, a, b in ((P, 0, full), (rest, full, FC)):
                    dve.scalar_tensor_tensor(out=hl_b[0:p, 1, v, a:b], in0=raw_b[0:p, v, a:b].rearrange("p c e r -> p c (e r)"),
                                             scalar=WS * SCALING, in1=hl_b[0:p, 0, v, a:b], op0=ALU.mult, op1=ALU.subtract)
            dve.scalar_tensor_tensor(out=hl_bd[:, 1].rearrange("p c n -> p (c n)"), in0=raw_bd[:].rearrange("p c e r -> p (c e r)"),
                                     scalar=SCALING, in1=hl_bd[:, 0].rearrange("p c n -> p (c n)"), op0=ALU.mult, op1=ALU.subtract).then_inc(lo, 1)
            for v in range(2):
                for f in range(FC):
                    m = rows_of(f)
                    dve.wait_ge(fill, n + 1)
                    src = bank[n % 2][:, 0:2 * m].rearrange("p (l n) -> p l n", l=2)
                    dve.tensor_copy(bT[:, v, 0, :, f * P:f * P + m], src)
                    ins = dve.tensor_scalar(bT[:, v, 1, :, f * P:f * P + m], src, -1.0, None, ALU.mult)
                    ins.then_inc(read, 1)
                    n += 1
            dve.wait_ge(fill, n + 1)
            dve.tensor_copy(w["BdT"][:].rearrange("p l b n -> p (l b n)"), bank[n % 2][:]).then_inc(read, 1)
            dve.wait_ge(setup, 5)
            for f in range(FC):
                m = rows_of(f)
                dve.wait_ge(fill_f, f + 1)
                b = bank_f[f % 2]
                dve.tensor_scalar(w["WdT"][0:m, f, :], b[0:m, 0:HID], WS, None, ALU.mult)
                dve.tensor_scalar(w["AdT"][0:m, f, :, 0:ER], b[0:m, HID:HID + ERS].rearrange("p (e r) -> p e r", e=NE), WS, None,
                                  ALU.mult).then_inc(read_f, 1)
        @block.tensor
        def _(pe):
            ident = w["ident"]
            pe.wait_ge(lo, 1)
            pe.wait_ge(setup, 4)
            n = 0
            for v in range(2):
                for f in range(FC):
                    m = rows_of(f)
                    wait(pe, read, n - 1)
                    for l in range(2):
                        for c in range(DK):
                            ins = pe.transpose(bank[n % 2][:, (l * DK + c) * m:(l * DK + c + 1) * m], hl[0:m, l, v, f, c * P:(c + 1) * P], ident[0:m, 0:m])
                    ins.then_inc(fill, 1)
                    n += 1
            pe.wait_ge(lo, 2)
            for v in range(2):
                for f in range(FC):
                    m = rows_of(f)
                    wait(pe, read, n - 1)
                    for l in range(2):
                        ins = pe.transpose(bank[n % 2][:, l * m:(l + 1) * m], hl_b[0:m, l, v, f, :], ident[0:m, 0:m])
                    ins.then_inc(fill, 1)
                    n += 1
            wait(pe, read, n - 1)
            for l in range(2):
                for b in range(2):
                    for c in range(DK):
                        at = (l * 2 + b) * HID + c * P
                        ins = pe.transpose(bank[n % 2][:, at:at + P], hl_bd[:, l, c, b * P:(b + 1) * P], ident[:])
            ins.then_inc(fill, 1)
            pe.wait_ge(loads, total)
            for f in range(FC):
                m = rows_of(f)
                wait(pe, read_f, f - 1)
                b = bank_f[f % 2]
                for c in range(DK):
                    pe.transpose(b[0:m, c * P:(c + 1) * P], raw_d[:, c, f * P:f * P + m], ident32[:])
                pe.transpose(b[0:m, HID:HID + ERS], raw_ad[:, f * P:f * P + m], ident32[:]).then_inc(fill_f, 1)


def route(nc, io, sb_x, w, tiles):
    with ExitStack() as ctx:
        sb = lambda name, shape, dt=F32: ctx.enter_context(nc.sbuf_tensor(name, shape, dt))
        sem = lambda name: ctx.enter_context(nc.semaphore("r_" + name))
        bank_w = ctx.enter_context(nc.psum_tensor("r_w", [P, 1024], F16))
        bank_t = [ctx.enter_context(nc.psum_tensor(f"r_t{n}", [P, 2 * DK * P], F16)) for n in range(2)]
        bank_l = ctx.enter_context(nc.psum_tensor("r_l", [P, TB, NE], F32))
        bank_a = [ctx.enter_context(nc.psum_tensor(f"r_a{n}", [P, NB], F32)) for n in range(2)]
        bank_e = [ctx.enter_context(nc.psum_tensor(f"r_e{n}", [P, 2, P], F32)) for n in range(2)]
        raw_a = sb("r_raw", [P, 2, HID])
        hl_a = sb("r_hl", [P, 2, 2, HID], F16)
        aT = sb("r_aT", [P, 2, 2, DK, P], F16)
        wr = sb("r_wr", [P, DK, NE])
        wr_hl = sb("r_wrhl", [P, 2, DK, NE], F16)
        st, ag, rs = sb("r_st", [P, TB, 6]), sb("r_ag", [P, TB, 2]), sb("r_rs", [P, 2, TB])
        n_x, n_hl = sb("r_nx", [P, TB, HID]), sb("r_nhl", [P, 2, TB, HID], F16)
        a_f = sb("r_af", [P, 2, NB])
        a_hl = sb("r_ahl", [P, 2, 2, NB], F16)
        logit = sb("r_logit", [P, tiles, NE])
        top = sb("r_top", [P, tiles])
        total = sb("r_total", [P, tiles])
        inv = sb("r_inv", [P, tiles])
        rank = sb("r_rank", [P, tiles, NE])
        earlier = sb("r_earlier", [P, NE, NE])
        more = sb("r_more", [P, tiles, NE, NE])
        same = sb("r_same", [P, tiles, NE, NE])
        wide = [sb(f"r_wide{n}", [P, NE, LR]) for n in range(2)]
        ident32 = sb("r_ident32", [P, P])
        loads, setup, w_hi, w_lo, w_fill, w_read = (sem(n) for n in ("loads", "setup", "w_hi", "w_lo", "w_fill", "w_read"))
        stats, agg, msd, rsd, xd, n_hi, n_lo, t_fill, t_read = (sem(n) for n in ("stats", "agg", "msd", "rsd", "xd", "n_hi", "n_lo", "t_fill", "t_read"))
        l_fill, l_read, a_fill, a_hi, a_lo, saved = (sem(n) for n in ("l_fill", "l_read", "a_fill", "a_hi", "a_lo", "saved"))
        step, exp_d, e_fill, e_read, wide_d = (sem(n) for n in ("step", "exp_d", "e_fill", "e_read", "wide_d"))
        block = ctx.enter_context(nc.Block())
        blocks = tiles // TB
        passed_dve, passed_pe = sem("passed_dve"), sem("passed_pe")

        def over(eng, count, one):
            one(0)
            with eng.Fori(1, count - 1) as n:
                one(n)
            one(count - 1)

        has = lambda b: not isinstance(b, int) or b < blocks

        @block.sync
        def _(sp):
            for v, name in enumerate(("f_Ag", "f_Au")):
                sp.dma_start(raw_a[:, v, :], io[name].rearrange("e r n -> (e r) n")).then_inc(loads, 16)
            with nc.allow_non_contiguous_dma(reason="2048 elements, once"):
                for c in range(DK):
                    sp.dma_start(wr[:, c, :], io["f_Wr"][:, c * P:(c + 1) * P].rearrange("e p -> p e")).then_inc(loads, 16)

            def one(b):
                sp.wait_ge(a_lo, 2 * b + 2)
                for v in range(2):
                    sp.dma_start(w["a_rows"][v, :, ER:, bass.ds(b * NB, NB)].rearrange("l r n -> r l n"), a_hl[:, :, v, :]).then_inc(saved, 16)
            over(sp, blocks, one)
            sp.wait_ge(saved, 32 * blocks)

        @block.gpsimd
        def _(pool):
            pool.memset(ident32[:], 0.0).then_inc(setup, 1)
            pool.memset(earlier[:], 1.0).then_inc(setup, 1)
            pool.wait_ge(setup, 2)
            pool.affine_select(out=ident32[:], in_=ident32[:], compare_op=ALU.not_equal, fill=1.0, base=0,
                               pattern=[[-1, P]], channel_multiplier=1).then_inc(setup, 1)
            pool.affine_select(out=earlier[:], in_=earlier[:], compare_op=ALU.is_gt, fill=0.0, base=0,
                               pattern=[[1, NE], [-1, NE]], channel_multiplier=0).then_inc(setup, 1)

            def norm(b):
                pool.wait_ge(msd, b + 1)
                pool.tensor_tensor(rs[:, 0], rs[:, 1], w["minus_half"][:, 0:1].broadcast_to([P, TB]), ALU.pow).then_inc(rsd, 1)
                pool.wait_ge(n_hi, b + 1)
                pool.tensor_tensor(n_hl[:, 1], n_x[:], n_hl[:, 0], ALU.subtract).then_inc(n_lo, 1)
            norm(0)
            over(pool, blocks, lambda b: norm(b + 1) if has(b + 1) else None)

        @block.scalar
        def _(act):
            act.wait_ge(loads, 16 * (2 + DK))
            act.activation(hl_a[:, 0], raw_a[:], ACT.Copy, scale=WS).then_inc(w_hi, 1)
            act.activation(wr_hl[:, 0], wr[:], ACT.Copy, scale=WS).then_inc(w_hi, 1)
            def norm(b):
                act.wait_ge(xd, b + 1)
                wait(act, t_fill, TB * b)
                act.activation(n_hl[:, 0], n_x[:], ACT.Copy).then_inc(n_hi, 1)

            def one(b):
                if has(b + 1):
                    norm(b + 1)
                wait(act, saved, 32 * b)
                for v in range(2):
                    act.wait_ge(a_fill, 2 * b + v + 1)
                    act.activation(a_hl[:, 0, v, :], bank_a[v][:], ACT.Copy, scale=1 / WS).then_inc(a_hi, 1)
            norm(0)
            over(act, blocks, one)
            act.wait_ge(step, 2)
            act.activation(logit[:], logit[:], ACT.Exp).then_inc(exp_d, 1)

        @block.vector
        def _(dve):
            dve.wait_ge(w_hi, 2)
            dve.scalar_tensor_tensor(out=hl_a[:, 1], in0=raw_a[:], scalar=WS, in1=hl_a[:, 0], op0=ALU.mult, op1=ALU.subtract)
            dve.scalar_tensor_tensor(out=wr_hl[:, 1], in0=wr[:], scalar=WS, in1=wr_hl[:, 0], op0=ALU.mult, op1=ALU.subtract).then_inc(w_lo, 1)
            dve.wait_ge(w_fill, 1)
            dve.tensor_copy(aT[:].rearrange("p l v c n -> p (l v c n)"), bank_w[:]).then_inc(w_read, 1)
            def stats_of(b):
                for n in range(TB):
                    dve.bn_stats(st[:, n, :], sb_x[:, bass.ds(TB * b + n, 1), :].rearrange("p o n -> p (o n)")).then_inc(stats, 1)
                for n in range(TB):
                    wait_apart(dve, stats, TB * b + n + 1, passed_dve)
                    dve.bn_aggr(ag[:, n, :], st[:, n, :]).then_inc(agg, 1)
                dve.wait_ge(agg, TB * b + TB)
                wait(dve, rsd, b)
                dve.tensor_scalar(rs[:, 1], ag[:, :, 1], 1e-5, None, ALU.add).then_inc(msd, 1)

            def norm(b):
                dve.wait_ge(rsd, b + 1)
                wait(dve, n_lo, b)
                for n in range(TB):
                    ins = dve.tensor_scalar(n_x[:, n, :], sb_x[:, bass.ds(TB * b + n, 1), :].rearrange("p o n -> p (o n)"), ag[:, n, 0:1],
                                            rs[:, 0, n:n + 1], ALU.subtract, ALU.mult)
                ins.then_inc(xd, 1)

            def one(b):
                if has(b + 1):
                    dve.wait_ge(xd, b + 1)
                    stats_of(b + 1)
                    norm(b + 1)
                for n in range(TB):
                    dve.wait_ge(t_fill, TB * b + n + 1)
                    dve.tensor_copy(w["nT"][:, :, :, bass.ds(b * NB + n * P, P)], bank_t[n % 2][:].rearrange("p (l c n) -> p l c n", l=2, c=DK)
                                    ).then_inc(t_read, 1)
                dve.wait_ge(l_fill, b + 1)
                dve.tensor_scalar(logit[:, bass.ds(TB * b, TB), :], bank_l[:], 1 / WS, None, ALU.mult).then_inc(l_read, 1)
                for v in range(2):
                    dve.wait_ge(a_hi, 2 * b + v + 1)
                    dve.scalar_tensor_tensor(out=a_hl[:, 1, v, :], in0=bank_a[v][:], scalar=1 / WS, in1=a_hl[:, 0, v, :],
                                             op0=ALU.mult, op1=ALU.subtract).then_inc(a_lo, 1)
            stats_of(0)
            norm(0)
            over(dve, blocks, one)
            dve.wait_ge(l_read, blocks)
            dve.tensor_reduce(top[:], logit[:], AX.X, ALU.max).then_inc(step, 1)
            dve.wait_ge(step, 1)
            dve.tensor_tensor(logit[:], logit[:], top[:].unsqueeze(2).broadcast_to([P, tiles, NE]), ALU.subtract).then_inc(step, 1)
            dve.wait_ge(exp_d, 1)
            dve.tensor_reduce(total[:], logit[:], AX.X, ALU.add).then_inc(step, 1)
            dve.wait_ge(step, 3)
            dve.reciprocal(inv[:], total[:]).then_inc(step, 1)
            dve.wait_ge(step, 4)
            dve.tensor_tensor(logit[:], logit[:], inv[:].unsqueeze(2).broadcast_to([P, tiles, NE]), ALU.mult).then_inc(step, 1)
            dve.wait_ge(step, 5)
            dve.wait_ge(setup, 4)
            own = logit[:].unsqueeze(3).broadcast_to([P, tiles, NE, NE])
            other = logit[:].unsqueeze(2).broadcast_to([P, tiles, NE, NE])
            dve.tensor_tensor(more[:], other, own, ALU.is_gt)
            dve.tensor_tensor(same[:], other, own, ALU.is_equal).then_inc(step, 1)
            dve.wait_ge(step, 6)
            flat = lambda a: a[:].rearrange("p t e j -> p t (e j)")
            dve.tensor_tensor(flat(same), flat(same), earlier[:].rearrange("p e j -> p (e j)").unsqueeze(1).broadcast_to([P, tiles, NE * NE]),
                              ALU.mult).then_inc(step, 1)
            dve.wait_ge(step, 7)
            dve.tensor_tensor(flat(more), flat(more), flat(same), ALU.add).then_inc(step, 1)
            dve.wait_ge(step, 8)
            dve.tensor_reduce(rank[:], more[:], AX.X, ALU.add).then_inc(step, 1)
            dve.wait_ge(step, 9)
            dve.scalar_tensor_tensor(out=rank[:], in0=rank[:], scalar=TOP - 0.5, in1=logit[:], op0=ALU.is_lt, op1=ALU.mult).then_inc(step, 1)
            dve.wait_ge(step, 10)
            def widen(t, n):
                dve.tensor_copy(wide[n][:], rank[:, bass.ds(2 * t + n, 1), :].rearrange("p o e -> p (o e)").unsqueeze(2)
                                .broadcast_to([P, NE, LR])).then_inc(wide_d, 1)

            def spread_pair(t):
                for n in range(2):
                    wait(dve, e_fill, 2 * t + n - 1)
                    widen(t, n)
                for n in range(2):
                    dve.wait_ge(e_fill, 2 * t + n + 1)
                    dve.tensor_copy(w["weT"][:, :, bass.ds((2 * t + n) * P, P)], bank_e[n][:]).then_inc(e_read, 1)
            over(dve, tiles // 2, spread_pair)

        @block.tensor
        def _(pe):
            ident = w["ident"]
            pe.wait_ge(w_lo, 1)
            pe.wait_ge(setup, 3)
            for l in range(2):
                for v in range(2):
                    for c in range(DK):
                        at = ((l * 2 + v) * DK + c) * P
                        ins = pe.transpose(bank_w[:, at:at + P], hl_a[:, l, v, c * P:(c + 1) * P], ident[:])
            ins.then_inc(w_fill, 1)
            pe.wait_ge(w_read, 1)
            terms = [(d, a, b) for d in range(DK) for a, b in ((0, 0), (1, 0), (0, 1))]
            def one(b):
                pe.wait_ge(n_lo, b + 1)
                for n in range(TB):
                    if n >= 2:
                        wait(pe, t_read, TB * b + n - 1)
                    for l in range(2):
                        for c in range(DK):
                            ins = pe.transpose(bank_t[n % 2][:, (l * DK + c) * P:(l * DK + c + 1) * P], n_hl[:, l, n, c * P:(c + 1) * P], ident[:])
                    ins.then_inc(t_fill, 1)
                wait(pe, l_read, b)
                wait_apart(pe, t_read, TB * (b + 1), passed_pe)
                for n in range(TB):
                    for m, (d, x, y) in enumerate(terms):
                        ins = pe.matmul(bank_l[:, n, :], w["nT"][:, x, d, bass.ds(b * NB + n * P, P)], wr_hl[:, y, d, :], start=(m == 0), stop=(m == len(terms) - 1))
                ins.then_inc(l_fill, 1)
                wait(pe, a_lo, 2 * b)
                for v in range(2):
                    for m, (d, x, y) in enumerate(terms):
                        ins = pe.matmul(bank_a[v][:], aT[:, y, v, d, :], w["nT"][:, x, d, bass.ds(b * NB, NB)], start=(m == 0), stop=(m == len(terms) - 1))
                    ins.then_inc(a_fill, 1)
            over(pe, blocks, one)
            def spread_pair(t):
                for n in range(2):
                    pe.wait_ge(wide_d, 2 * t + n + 1)
                    wait(pe, e_read, 2 * t + n - 1)
                    for m in range(2):
                        ins = pe.transpose(bank_e[n][:, m, :], wide[n][:, EPB * m:EPB * (m + 1), :].rearrange("p e r -> p (e r)"), ident32[:])
                    ins.then_inc(e_fill, 1)
            over(pe, tiles // 2, spread_pair)


def feed_forward(nc, io, sb_x, w, tiles):
    with ExitStack() as ctx:
        sb = lambda name, shape, dt=F32: ctx.enter_context(nc.sbuf_tensor(name, shape, dt))
        sem = lambda name: ctx.enter_context(nc.semaphore("m_" + name))
        ps = lambda name, n=2: [ctx.enter_context(nc.psum_tensor(f"{name}{i}", [P, NB], F32)) for i in range(n)]
        gate, up, down, y = ps("m_gate"), ps("m_up"), ps("m_down"), ps("m_y")
        RING = 6
        a6 = sb("m_a6", [STACK, 2, NE, NB], F16)
        sg = [sb(f"m_sg{n}", [P, NB]) for n in range(3)]
        h_base = [sb(f"m_hb{n}", [P, NB]) for n in range(2)]
        h_e = [[sb(f"m_he{f}_{n}", [P, NB]) for n in range(RING)] for f in range(2)]
        d_f, d_hl = sb("m_df", [P, 2, NB]), sb("m_dhl", [P, 2, 2, NB], F16)
        a_here, g_fill, g_read, u_fill, u_read, d_done, d_scaled, d_hi, d_lo, y_fill, y_read, stored = (
            sem(n) for n in ("a_here", "g_fill", "g_read", "u_fill", "u_read", "d_done", "d_scaled", "d_hi", "d_lo", "y_fill", "y_read", "stored"))
        block = ctx.enter_context(nc.Block())
        blocks = tiles // TB
        PAIRS = FC // 2
        UNITS = PAIRS * 2 * (NE + 1)
        GROUPS = NE // EPB
        DOWNS = PAIRS * 2 * (1 + GROUPS)
        ADMAS = 12

        def unit(b, p, k, fi):
            return UNITS * b + (p * (NE + 1) + k + 1) * 2 + fi + 1

        def downed(b, p, group, fi):
            return DOWNS * b + (p * (GROUPS + 1) + group + 1) * 2 + fi + 1

        def free_at(b, p, k, fi):
            m = NE * p + k - RING
            if m >= 0:
                return downed(b, m // NE, m % NE // EPB, fi)
            m += NE * PAIRS
            return downed(b - 1, m // NE, m % NE // EPB, fi)

        def over_blocks(eng, one, last):
            one(0)
            with eng.Fori(1, blocks) as b:
                one(b)
            last()

        first = lambda b: isinstance(b, int) and b == 0

        @block.sync
        def _(sp):
            def one(b):
                wait(sp, g_fill, UNITS * b)
                wait(sp, u_fill, UNITS * b)
                for v in range(2):
                    for r, part in enumerate((0, 1, 0)):
                        for at, start in ((0, 0), (ER, ER)):
                            sp.dma_start(a6[r * 2 * ER + at:r * 2 * ER + at + ER, v],
                                         w["a_rows"][v, part, start:start + ERS, bass.ds(b * NB, NB)].rearrange("(e r) n -> r e n", r=ER)
                                         ).then_inc(a_here, 16)
                if not first(b):
                    store(b - 1)

            def store(b):
                sp.wait_ge(y_read, 2 * b + 2)
                sp.dma_start(io["out"].rearrange("(t p) n -> p t n", p=P)[:, bass.ds(b * TB, TB), :], sb_x[:, bass.ds(b * TB, TB), :]
                             ).then_inc(stored, 16)

            def last():
                store(blocks - 1)
                sp.wait_ge(stored, 16 * blocks)
            over_blocks(sp, one, last)

        @block.gpsimd
        def _(pool):
            def final(b):
                pool.wait_ge(d_hi, b + 1)
                pool.tensor_tensor(d_hl[:, 1], d_f[:], d_hl[:, 0], ALU.subtract).then_inc(d_lo, 1)
            with pool.Fori(0, blocks) as b:
                final(b)

        @block.scalar
        def _(act):
            def final(b):
                act.wait_ge(d_scaled, b + 1)
                wait(act, y_fill, b)
                act.activation(d_hl[:, 0], d_f[:], ACT.Copy).then_inc(d_hi, 1)

            def one(b):
                for p in range(PAIRS):
                    for k in range(-1, NE):
                        for fi in range(2):
                            n, m = unit(b, p, k, fi), rows_of(2 * p + fi)
                            slot = ((p * (NE + 1) + k + 1) * 2 + fi)
                            act.wait_ge(g_fill, n)
                            if not first(b) or slot >= 3:
                                act.wait_ge(u_read, n - 3)
                            act.activation(sg[slot % 3][0:m], gate[fi][0:m], ACT.Silu, scale=1 / WS).then_inc(g_read, 1)
                        if p == 0 and k == 0 and not first(b):
                            final(b - 1)
            over_blocks(act, one, lambda: final(blocks - 1))

        @block.vector
        def _(dve):
            def scale(b):
                dve.wait_ge(d_done, DOWNS * (b + 1))
                wait(dve, d_lo, b)
                for g in range(GROUPS):
                    ins = dve.tensor_tensor(d_f[:, g], down[g][:], w["weT"][:, g, bass.ds(b * NB, NB)], ALU.mult)
                ins.then_inc(d_scaled, 1)

            def final(b):
                dve.wait_ge(y_fill, b + 1)
                for n in range(2):
                    x_t = sb_x[:, bass.ds(TB * b + 2 * n, 2), :]
                    dve.scalar_tensor_tensor(out=x_t, in0=y[n][:].rearrange("p (t n) -> p t n", t=2), scalar=1 / WS, in1=x_t,
                                             op0=ALU.mult, op1=ALU.add).then_inc(y_read, 1)

            def one(b):
                for p in range(PAIRS):
                    for k in range(-1, NE):
                        for fi in range(2):
                            n, m = unit(b, p, k, fi), rows_of(2 * p + fi)
                            slot = ((p * (NE + 1) + k + 1) * 2 + fi)
                            if k < 0:
                                out = h_base[fi]
                                if not first(b) or p > 0:
                                    dve.wait_ge(d_done, downed(b, p - 1, -1, fi) if p > 0 else downed(b - 1, PAIRS - 1, -1, fi))
                            else:
                                out = h_e[fi][(NE * p + k) % RING]
                                if not first(b) or NE * p + k >= RING:
                                    dve.wait_ge(d_done, free_at(b, p, k, fi))
                            dve.wait_ge(g_read, n)
                            dve.wait_ge(u_fill, n)
                            dve.scalar_tensor_tensor(out=out[0:m], in0=up[fi][0:m], scalar=1 / WS, in1=sg[slot % 3][0:m],
                                                     op0=ALU.mult, op1=ALU.mult).then_inc(u_read, 1)
                        if p == 0 and not first(b):
                            if k == -1:
                                scale(b - 1)
                            if k == 2:
                                final(b - 1)

            def last():
                scale(blocks - 1)
                final(blocks - 1)
            over_blocks(dve, one, last)

        @block.tensor
        def _(pe):
            def sums(b, p, k, between):
                for v, bank, fill, read in ((0, gate, g_fill, g_read), (1, up, u_fill, u_read)):
                    half_last = rows_of(2 * p + 1) < P
                    if k < 0 and half_last:
                        pe.wait_ge(read, unit(b, p, k, 1) - 2)
                    for fi in range(2):
                        f, m = 2 * p + fi, rows_of(2 * p + fi)
                        if not (k < 0 and (half_last or (first(b) and p == 0))):
                            pe.wait_ge(read, unit(b, p, k, fi) - 2)
                        out = bank[fi][0:m]
                        if k < 0:
                            terms = [(d, x, y_) for d in range(DK) for x, y_ in ((0, 0), (1, 0), (0, 1))]
                            for n, (d, x, y_) in enumerate(terms):
                                ins = pe.matmul(out, w["Wgu"][:, y_, d, v, f * P:f * P + m], w["nT"][:, x, d, bass.ds(b * NB, NB)],
                                                start=(n == 0), stop=(n == len(terms) - 1), skip_group_check=True)
                        else:
                            if p == 0 and k == 0:
                                pe.wait_ge(a_here, 16 * ADMAS * (b + 1))
                            ins = pe.matmul(out, w["B"][:, v, k, f * P:f * P + m], a6[:, v, k, :], start=False, stop=True, skip_group_check=True)
                        ins.then_inc(fill, 1)
                    if v == 0:
                        between()

            def base_down(b, p, fi, half):
                f, m = 2 * p + fi, rows_of(2 * p + fi)
                if half == 0:
                    pe.wait_ge(u_read, unit(b, p, -1, fi))
                for t in (0, 1):
                    at = (2 * half + t) * P
                    ins = pe.matmul(y[half][:, t * HID:(t + 1) * HID], h_base[fi][0:m, at:at + P], w["WdT"][0:m, f, :],
                                    start=(f == 0 and t == 0), stop=True, skip_group_check=True)
                if half == 1:
                    ins.then_inc(d_done, 1)

            def expert_down(b, p, g, fi):
                if fi == 0:
                    pe.wait_ge(u_read, unit(b, p, EPB * (g + 1) - 1, 1))
                f, m = 2 * p + fi, rows_of(2 * p + fi)
                for q in range(EPB):
                    k = EPB * g + q
                    ins = pe.matmul(down[g][LR * q:LR * (q + 1)], w["AdT"][0:m, f, k, :], h_e[fi][(NE * p + k) % RING][0:m],
                                    start=(f == 0), stop=(f == FC - 1), skip_group_check=True)
                ins.then_inc(d_done, 1)

            def final(b):
                pe.wait_ge(d_lo, b + 1)
                for t in range(TB):
                    for g in range(GROUPS):
                        for x, y_ in ((0, 0), (1, 0), (0, 1)):
                            ins = pe.matmul(y[t // 2][:, (t % 2) * HID:(t % 2 + 1) * HID], d_hl[:, x, g, t * P:(t + 1) * P], w["BdT"][:, y_, g, :],
                                            start=False, stop=True, skip_group_check=True)
                ins.then_inc(y_fill, 1)

            def one(b):
                for p in range(PAIRS):
                    def between(k):
                        if k == -1 and p > 0:
                            expert_down(b, p - 1, 1, 0)
                            expert_down(b, p - 1, 1, 1)
                        if k == 2 and p == 0 and not first(b):
                            final(b - 1)
                        if k == 4 and p == 0 and not first(b):
                            pe.wait_ge(y_read, 2 * b)
                            pe.wait_ge(d_scaled, b)
                        for fi, half, at in ((0, 0, 4), (0, 1, 4), (1, 0, 5), (1, 1, 5)) if p == 0 else ((0, 0, 1), (0, 1, 2), (1, 0, 3), (1, 1, 4)):
                            if k == at:
                                base_down(b, p, fi, half)
                        if k in (6, 7):
                            expert_down(b, p, 0, k - 6)
                    for k in range(-1, NE):
                        sums(b, p, k, lambda: between(k))
                expert_down(b, PAIRS - 1, 1, 0)
                expert_down(b, PAIRS - 1, 1, 1)
            over_blocks(pe, one, lambda: final(blocks - 1))


def shared_tiles(nc, ctx):
    return {"ident": ctx.enter_context(nc.sbuf_tensor("ident", [P, P], F16)),
            "minus_half": ctx.enter_context(nc.sbuf_tensor("minus_half", [P, XH], F32))}


def build(nc, io, tiles):
    with nc.sbuf_tensor("x_all", [P, tiles, HID], F32) as sb_x, ExitStack() as shared:
        common = shared_tiles(nc, shared)
        with ExitStack() as ctx:
            w = {**common, **cross_weights(nc, ctx)}
            prepare_cross(nc, io, sb_x, w, tiles)
            cross_attention(nc, io, sb_x, w, tiles)
        with ExitStack() as ctx:
            w = {**common, **self_weights(nc, ctx)}
            prepare_self(nc, io, w)
            self_attention(nc, io, sb_x, w, tiles)
        with ExitStack() as ctx:
            w = {**common, **ffn_weights(nc, ctx, tiles)}
            prepare_ffn(nc, io, w, tiles)
            route(nc, io, sb_x, w, tiles)
            feed_forward(nc, io, sb_x, w, tiles)


ROWS = 128
NAMES = {
    "x": "x", "ctx": "ctx_2048", "mask": "mask_1xSxS2_ff0",
    "Wq": "L0_xattn_Wq", "bq": "L0_xattn_bq", "Wk": "L0_xattn_Wk", "bk": "L0_xattn_bk", "Wv": "L0_xattn_Wv",
    "bv": "L0_xattn_bv", "Wo": "L0_xattn_Wo", "qn": "L0_xattn_qn_w", "kn": "L0_xattn_kn_w",
    "a_Wq": "L0_attn_Wq", "a_bq": "L0_attn_bq", "a_Wk": "L0_attn_Wk", "a_bk": "L0_attn_bk", "a_Wv": "L0_attn_Wv",
    "a_bv": "L0_attn_bv", "a_Wo": "L0_attn_Wo", "a_bo": "L0_attn_bo", "a_kw": "L0_attn_key_weights",
    "f_Wg": "L0_ffn_Wg", "f_Wu": "L0_ffn_Wu", "f_Wd": "L0_ffn_Wd", "f_Wr": "L0_ffn_Wr", "f_Ag": "L0_ffn_Ag",
    "f_Bg": "L0_ffn_Bg", "f_Au": "L0_ffn_Au", "f_Bu": "L0_ffn_Bu", "f_Ad": "L0_ffn_Ad", "f_Bd": "L0_ffn_Bd",
}


def kernel(**inputs):
    import numpy as _np
    import concourse.bacc as _bacc
    from concourse import mybir as _mybir
    from concourse.bass_utils import run_bass_kernel_spmd as _run

    nc = _bacc.Bacc("TRN2", target_bir_lowering=False, num_devices=1)
    arrays, io = {}, {}
    for short, name in NAMES.items():
        a = _np.ascontiguousarray(inputs[name])
        arrays[f"in_{name}"] = a
        io[short] = nc.dram_tensor(f"in_{name}", a.shape, _mybir.dt.from_np(a.dtype), kind="ExternalInput").ap()
    freq = _np.float32(1.0) / _np.power(_np.float32(10000.0), _np.arange(0, AD, 2, dtype=_np.float32) / _np.float32(AD))
    angle = _np.arange(S, dtype=_np.float32)[:, None] * freq[None, :]
    rope = _np.stack([_np.cos(angle), _np.sin(angle)]).astype(_np.float32)
    arrays["rope_table"] = rope
    io["rope"] = nc.dram_tensor("rope_table", rope.shape, F32, kind="ExternalInput").ap()
    shape = inputs["x"].shape
    out = nc.dram_tensor("out_0", shape, F32, kind="ExternalOutput").ap()
    io["x"] = io["x"].rearrange("b s n -> (b s) n")
    io["out"] = out.rearrange("b s n -> (b s) n")
    build(nc, io, ROWS // BT)
    return _run(nc, [arrays], core_ids=[0]).results[0]["out_0"]
```
